# Optimizing a Trainium2 kernel written in Bass

```python
import numpy as np
import jax
import jax.numpy as jnp

def _softmax(x, axis=-1):
    return jax.nn.softmax(x, axis=axis)

def _gelu(x):
    return jax.nn.gelu(x, approximate=True)

def _silu(x):
    return jax.nn.silu(x)

def _sigmoid(x):
    return jax.nn.sigmoid(x)

def _layernorm(x, axis=-1, eps=1e-05):
    m = jnp.mean(x, axis=axis, keepdims=True)
    v = jnp.var(x, axis=axis, keepdims=True)
    return (x - m) / jnp.sqrt(v + eps)

def _scatter_add(tgt, idx, src, axis=0):
    return tgt.at[idx].add(src)

def _segment_sum(src, seg, n):
    return jax.ops.segment_sum(src, seg, n)
kernel_name = 'mk_decoder_preln_d1_seqx_r4_8d06a8'

def setup_inputs(seed: int=0):
    np.random.seed(seed)
    _w = jnp.asarray

    def _rec_inputs():
        import jax
        import jax.numpy as jnp
        _rk = jax.random.key(seed)
        x = 7.22e-05 + 1 * jax.random.normal(jax.random.fold_in(_rk, 1), (16, 256, 512), jnp.float32)
        _lenS = 256 - jax.random.randint(jax.random.fold_in(_rk, 7), (16,), 0, max(1, 256 // 4) + 1, jnp.int32)
        _lenS2 = 256 - jax.random.randint(jax.random.fold_in(_rk, 8), (16,), 0, max(1, 256 // 4) + 1, jnp.int32)
        _ctx_2048P = jax.random.normal(jax.random.fold_in(_rk, 11), (16, 16, 512), jnp.float32)
        _ctx_2048c = jax.random.dirichlet(jax.random.fold_in(_rk, 511), 0.3 * jnp.ones((16,), jnp.float32), (16, 256))
        _ctx_2048t = jnp.einsum('bsk,bkd->bsd', _ctx_2048c, _ctx_2048P)
        _ctx_2048t = _ctx_2048t * jax.lax.rsqrt(jnp.mean(jnp.square(_ctx_2048t)) + 1e-12) * 0.953939
        ctx_2048 = 4.13588e-05 + 0.999923 * (_ctx_2048t + 0.3 * jax.random.normal(jax.random.fold_in(_rk, 611), (16, 256, 512), jnp.float32))
        return (x, ctx_2048)
    x, ctx_2048 = _rec_inputs()

    def _L0_attn_setup():
        import jax, jax.numpy as jnp
        import numpy as np
        E = 512
        H = 32
        KVH = 8
        D = E // H
        G = H // KVH
        key = jax.random.key(seed)
        ks = jax.random.split(key, 9)
        s = 0.02
        return {'datas': jax.random.normal(ks[0], (2, 512, E), dtype=jnp.float32), 'Wq': jax.random.normal(ks[1], (E, E), dtype=jnp.float32) * s, 'bq': jnp.zeros((E,), dtype=jnp.float32), 'Wk': jax.random.normal(ks[2], (E, KVH * D), dtype=jnp.float32) * s, 'bk': jnp.zeros((KVH * D,), dtype=jnp.float32), 'Wv': jax.random.normal(ks[3], (E, KVH * D), dtype=jnp.float32) * s, 'bv': jnp.zeros((KVH * D,), dtype=jnp.float32), 'Wo': jax.random.normal(ks[4], (E, E), dtype=jnp.float32) * s, 'bo': jnp.zeros((E,), dtype=jnp.float32)}
    _L0_attn_all = _L0_attn_setup()
    _L0_attn_in = {k: v for k, v in _L0_attn_all.items() if k in ('Wq', 'bq', 'Wk', 'bk', 'Wv', 'bv', 'Wo', 'bo')}
    del _L0_attn_all

    def _L0_xattn_setup():
        import jax, jax.numpy as jnp
        import numpy as np
        N_HEAD = 8
        key = jax.random.key(seed)
        k1, k2, k3 = jax.random.split(key, 3)
        B, D, L = (4, 256, 512)
        q = jax.random.normal(k1, (B, D, L), dtype=jnp.float32)
        k = jax.random.normal(k2, (B, D, L), dtype=jnp.float32)
        v = jax.random.normal(k3, (B, D, L), dtype=jnp.float32)
        gamma = jnp.ones((), dtype=jnp.float32)
        return {'q': q, 'k': k, 'v': v, 'gamma': gamma}
    _L0_xattn_all = _L0_xattn_setup()
    _L0_xattn_in = {k: v for k, v in _L0_xattn_all.items() if k in ('gamma',)}
    del _L0_xattn_all

    def _L0_ffn_setup():
        import jax, jax.numpy as jnp
        import numpy as np
        _FP8_MAX = 448.0
        _BLOCK = 32
        _EPS = 1e-30

        def _mx_dequant(t):
            rows, feat = t.shape
            blocks = t.reshape(rows, feat // _BLOCK, _BLOCK)
            max_abs = jnp.max(jnp.abs(blocks), axis=-1)
            scales = jnp.maximum(max_abs / _FP8_MAX, _EPS)
            q = (blocks / scales[..., None]).astype(jnp.float8_e4m3fn).astype(jnp.float32)
            return (q * scales[..., None]).reshape(rows, feat)

        def _mx_linear(x2d, w):
            return _mx_dequant(x2d) @ _mx_dequant(w).T
        key = jax.random.key(seed)
        k1, k2, k3, k4 = jax.random.split(key, 4)
        B, S, H, I = (2, 256, 512, 2048)
        return {'x': jax.random.normal(k1, (B, S, H), dtype=jnp.float32), 'gate_w': jax.random.normal(k2, (I, H), dtype=jnp.float32) * 0.02, 'up_w': jax.random.normal(k3, (I, H), dtype=jnp.float32) * 0.02, 'down_w': jax.random.normal(k4, (H, I), dtype=jnp.float32) * 0.02}
    _L0_ffn_all = _L0_ffn_setup()
    _L0_ffn_in = {k: v for k, v in _L0_ffn_all.items() if k in ('gate_w', 'up_w', 'down_w')}
    del _L0_ffn_all
    return {'x': x, 'ctx_2048': ctx_2048, 'L0_attn_Wq': _L0_attn_in['Wq'], 'L0_attn_bq': _L0_attn_in['bq'], 'L0_attn_Wk': _L0_attn_in['Wk'], 'L0_attn_bk': _L0_attn_in['bk'], 'L0_attn_Wv': _L0_attn_in['Wv'], 'L0_attn_bv': _L0_attn_in['bv'], 'L0_attn_Wo': _L0_attn_in['Wo'], 'L0_attn_bo': _L0_attn_in['bo'], 'L0_xattn_gamma': _L0_xattn_in['gamma'], 'L0_ffn_gate_w': _L0_ffn_in['gate_w'], 'L0_ffn_up_w': _L0_ffn_in['up_w'], 'L0_ffn_down_w': _L0_ffn_in['down_w']}

def reference(x, ctx_2048, L0_attn_Wq, L0_attn_bq, L0_attn_Wk, L0_attn_bk, L0_attn_Wv, L0_attn_bv, L0_attn_Wo, L0_attn_bo, L0_xattn_gamma, L0_ffn_gate_w, L0_ffn_up_w, L0_ffn_down_w):
    import jax
    import jax.numpy as jnp

    def _L0_attn_ref(datas, Wq, bq, Wk, bk, Wv, bv, Wo, bo):
        import jax, jax.numpy as jnp
        import numpy as np
        E = 512
        H = 32
        KVH = 8
        D = E // H
        G = H // KVH
        B, S, _ = datas.shape
        q = (datas @ Wq + bq).reshape(B, S, H, D).transpose(0, 2, 1, 3)
        k = (datas @ Wk + bk).reshape(B, S, KVH, D).transpose(0, 2, 1, 3)
        v = (datas @ Wv + bv).reshape(B, S, KVH, D).transpose(0, 2, 1, 3)
        k = jnp.repeat(k, G, axis=1)
        v = jnp.repeat(v, G, axis=1)
        scores = jnp.einsum('bhqd,bhkd->bhqk', q, k) / jnp.sqrt(jnp.asarray(D, q.dtype))
        attn = jax.nn.softmax(scores, axis=-1)
        out = jnp.einsum('bhqk,bhkd->bhqd', attn, v)
        out = out.transpose(0, 2, 1, 3).reshape(B, S, E)
        return out @ Wo + bo

    def _L0_xattn_ref(q, k, v, gamma):
        import jax, jax.numpy as jnp
        import numpy as np
        N_HEAD = 8
        B, Dq, Lq = q.shape
        Dv, Lk = (v.shape[-2], v.shape[-1])
        h = N_HEAD
        dq = Dq // h
        dv = Dv // h
        qh = q.reshape(B, h, dq, Lq)
        kh = k.reshape(B, h, dq, Lk)
        vh = v.reshape(B, h, dv, Lk)
        scale = 1.0 / jnp.sqrt(jnp.asarray(dq, dtype=q.dtype))
        qk = jnp.einsum('bhdq,bhdl->bhql', qh, kh) * scale
        sm = jax.nn.softmax(qk, axis=-1)
        ret = jnp.einsum('bhql,bhdl->bhdq', sm, vh)
        ret = ret.reshape(B, Dv, Lq)
        return gamma * ret

    def _L0_ffn_ref(x, gate_w, up_w, down_w):
        import jax, jax.numpy as jnp
        import numpy as np
        _FP8_MAX = 448.0
        _BLOCK = 32
        _EPS = 1e-30

        def _mx_dequant(t):
            rows, feat = t.shape
            blocks = t.reshape(rows, feat // _BLOCK, _BLOCK)
            max_abs = jnp.max(jnp.abs(blocks), axis=-1)
            scales = jnp.maximum(max_abs / _FP8_MAX, _EPS)
            q = (blocks / scales[..., None]).astype(jnp.float8_e4m3fn).astype(jnp.float32)
            return (q * scales[..., None]).reshape(rows, feat)

        def _mx_linear(x2d, w):
            return _mx_dequant(x2d) @ _mx_dequant(w).T
        B, S, H = x.shape
        x2d = x.reshape(B * S, H)
        gate = _mx_linear(x2d, gate_w)
        up = _mx_linear(x2d, up_w)
        h = jax.nn.silu(gate) * up
        out = _mx_linear(h, down_w)
        return out.reshape(B, S, H)
    x = x + _L0_attn_ref(_layernorm(x, axis=-1), L0_attn_Wq, L0_attn_bq, L0_attn_Wk, L0_attn_bk, L0_attn_Wv, L0_attn_bv, L0_attn_Wo, L0_attn_bo)
    x = x + _L0_xattn_ref(_layernorm(x, axis=-1), ctx_2048, ctx_2048, L0_xattn_gamma)
    x = x + _L0_ffn_ref(_layernorm(x, axis=-1), L0_ffn_gate_w, L0_ffn_up_w, L0_ffn_down_w)
    return x

_drawn_inputs = setup_inputs


def setup_inputs(seed=0):
    import zlib

    import numpy as np

    out = dict(_drawn_inputs(seed))
    spreads = {'L0_attn_bq': (0.0, 0.8),
     'L0_attn_bk': (0.0, 0.8),
     'L0_attn_bv': (0.0, 0.1),
     'L0_attn_bo': (0.0, 0.1)}
    factors = {'L0_attn_Wq': 8.0, 'L0_attn_Wk': 8.0}
    for name, (base, spread) in spreads.items():
        noise = np.random.default_rng([zlib.crc32(name.encode()), seed]).standard_normal(out[name].shape)
        drawn = base * np.exp(spread * noise) if base else spread * noise
        out[name] = jnp.asarray(drawn.astype(out[name].dtype))
    for name, factor in factors.items():
        out[name] = (out[name] * factor).astype(out[name].dtype)
    return out
```

```python
from contextlib import ExitStack

import concourse.bass as bass
from concourse import mybir

F32 = mybir.dt.float32
F16 = mybir.dt.float16
U32 = mybir.dt.uint32
I32 = mybir.dt.int32
ALU = mybir.AluOpType
ACT = mybir.ActivationFunctionType
AX = mybir.AxisListType

P = 128
BATCH, SEQ, E = 16, 256, 512
KC = E // P
TT = SEQ // P
HEADS, KV_HEADS, D = 32, 8, 16
GROUP = HEADS // KV_HEADS
X_HEADS, X_D = 8, 32
FF = 2048
LN_EPS = 1e-5
W_SCALE = 64.0
MX_BLOCK, MX_MAX, MX_EPS = 32, 448.0, 1e-30
FP8_MIN_EXP = 2.0 ** -6
EXP_MASK = 0x7F800000
HALF_BIT = 0x00400000
MX_SHIFT = 2.0 ** 20


class At:

    def __init__(self, k, off):
        self.k, self.off = k, off
        self.n = k * 2 + off
        self.par = off % 2
        self.half = k + off // 2

    def plus(self, m):
        return At(self.k, self.off + m)


class Chain:

    def __init__(self, eng, sem, per):
        self.eng, self.sem, self.per = eng, sem, per
        self.base, self.count = 0, 0

    def start(self, n):
        assert self.count in (0, self.per), (self.count, self.per)
        self.base, self.count = n * self.per, 0

    def link(self, ins):
        self.count += 1
        ins.then_inc(self.sem, 1)
        self.eng.wait_ge(self.sem, self.base + self.count)


def identity_matrix(gp, ones, ident, made, ready):
    gp.memset(ones[:, :], 1.0).then_inc(made, 1)
    gp.wait_ge(made, 1)
    gp.affine_select(ident[:, :], ones[:, :], pattern=[[-1, P]], compare_op=ALU.is_equal, fill=0.0,
                     base=0, channel_multiplier=1).then_inc(ready, 1)


MOMENT_CONSTANTS = (0.5, 1.0 / E, 0.25, LN_EPS, -0.5, 1.5)
MOMENT_LINKS = 10 + 5 * 2


def moment_constants(v, tile, done):
    for i, value in enumerate(MOMENT_CONSTANTS):
        v.memset(tile[:, i, :], value).then_inc(done, 1)


def moments(gp, link, stats, mean, rstd, const, t):
    half, inv_e, quarter, eps, neg_half, three_halves = (const[:, i, :] for i in range(6))
    op = gp.tensor_tensor
    link(op(mean, stats[:, :, 1], stats[:, :, 4], ALU.add))
    link(op(mean, mean, half, ALU.mult))
    link(op(t[:, 0], stats[:, :, 1], stats[:, :, 4], ALU.subtract))
    link(op(t[:, 0], t[:, 0], t[:, 0], ALU.mult))
    link(op(t[:, 0], t[:, 0], quarter, ALU.mult))
    link(op(t[:, 1], stats[:, :, 2], stats[:, :, 5], ALU.add))
    link(op(t[:, 1], t[:, 1], inv_e, ALU.mult))
    link(op(t[:, 0], t[:, 0], t[:, 1], ALU.add))
    link(op(t[:, 0], t[:, 0], eps, ALU.add))
    link(op(rstd, t[:, 0], neg_half, ALU.pow))
    for _ in range(2):
        link(op(t[:, 1], rstd, rstd, ALU.mult))
        link(op(t[:, 1], t[:, 1], t[:, 0], ALU.mult))
        link(op(t[:, 1], t[:, 1], half, ALU.mult))
        link(op(t[:, 1], three_halves, t[:, 1], ALU.subtract))
        link(op(rstd, rstd, t[:, 1], ALU.mult))


def blocks(ap):
    return ap.rearrange("p (a b) -> p a b", b=MX_BLOCK)


def spread(ap, n):
    return ap.rearrange("p (a o) -> p a o", o=1).to_broadcast([ap.shape[0], ap.shape[1], n])


def mx_round_links(v, link, src, scale, rscale, work, magic, eps, scale_out=None):
    link(v.tensor_reduce(scale, blocks(src), AX.X, ALU.max, apply_absolute_value=True))
    link(v.tensor_scalar(scale, scale, 1.0 / MX_MAX, eps, ALU.mult, ALU.max))
    if scale_out is not None:
        link(v.tensor_scalar(scale_out, scale, W_SCALE, None, ALU.mult))
    link(v.reciprocal(rscale, scale))
    link(v.tensor_tensor(blocks(work), blocks(src), spread(rscale, MX_BLOCK), ALU.mult))
    link(v.tensor_scalar(magic.bitcast(U32), work.bitcast(U32), EXP_MASK, HALF_BIT, ALU.bitwise_and,
                         ALU.bitwise_or))
    link(v.tensor_scalar(magic, magic, 1.5 * FP8_MIN_EXP, MX_SHIFT, ALU.max, ALU.mult))
    return v.tensor_tensor(work, work, magic, ALU.add)


MX_ROUND_LINKS = 6


def feed_forward(nc, x2, gate_w, up_w, down_w, out):
    TILES = x2.shape[0] // P
    NB = E // MX_BLOCK
    CH = FF // E
    WP = 2 * FF // P
    DP = (E // P) * CH
    STEPS = TILES * CH

    with ExitStack() as ctx:
        sb = lambda name, shape, dt=F32: ctx.enter_context(nc.sbuf_tensor("f_" + name, shape, dt))
        ps = lambda name: ctx.enter_context(nc.psum_tensor("f_" + name, [P, 512], F32))
        sem = lambda name: ctx.enter_context(nc.semaphore("f_" + name))

        ones, ident = sb("ones", [P, P]), sb("ident", [P, P])
        wgu = [sb(f"wgu{i}", [P, KC, 2 * FF], F16) for i in range(2)]
        wdn = [sb(f"wdn{i}", [P, FF // P, E], F16) for i in range(2)]
        w_in = [sb(f"w_in{i}", [P, E]) for i in range(2)]
        w_work = [sb(f"w_work{i}", [P, E]) for i in range(2)]
        w_magic = [sb(f"w_magic{i}", [P, E]) for i in range(2)]
        w_scales = [sb(f"w_scales{i}", [P, 3, NB]) for i in range(2)]
        x_in = [sb(f"x_in{i}", [P, E]) for i in range(2)]
        x_res = [sb(f"x_res{i}", [P, E]) for i in range(2)]
        x_norm, x_work, x_magic = sb("x_norm", [P, E]), sb("x_work", [P, E]), sb("x_magic", [P, E])
        x_stats, x_mean, x_rstd = sb("x_stats", [P, 1, 6]), sb("x_mean", [P, 1]), sb("x_rstd", [P, 1])
        m_const, m_tmp = sb("m_const", [P, len(MOMENT_CONSTANTS), 1]), sb("m_tmp", [P, 2, 1])
        x_scales = sb("x_scales", [P, 2, NB])
        xT = [[sb(f"xT{i}{h}", [P, KC, P], F16) for h in "hl"] for i in range(2)]
        sg = [sb(f"sg{i}", [P, E]) for i in range(2)]
        h = [sb(f"h{i}", [P, E]) for i in range(2)]
        h_work = [sb(f"h_work{i}", [P, E]) for i in range(2)]
        h_magic = [sb(f"h_magic{i}", [P, E]) for i in range(2)]
        h_scales = [sb(f"h_scales{i}", [P, 2, NB]) for i in range(2)]
        hT = [[sb(f"hT{i}{x}", [P, KC, P], F16) for x in "hl"] for i in range(2)]
        y = [sb(f"y{i}", [P, E]) for i in range(2)]

        g_ps, u_ps, d_ps = ([ps(f"{n}{i}") for i in range(2)] for n in ("g", "u", "d"))
        t_ps, xt_ps = ps("t"), ps("xt")

        ones_made, ident_ready, const_ready = sem("ones_made"), sem("ident_ready"), sem("const_ready")
        w_loaded = [sem(f"w_loaded{i}") for i in range(2)]
        w_chain, w_rounded, w_pool, w_ready = sem("w_chain"), sem("w_rounded"), sem("w_pool"), sem("w_ready")
        w_transposed, w_hi, w_lo = sem("w_transposed"), sem("w_hi"), sem("w_lo")

        with nc.Block() as block:
            def w_source(q, lot):
                if lot == 0:
                    return gate_w.rearrange("(q p) f -> q p f", p=P)[q]
                if lot == 1:
                    return up_w.rearrange("(q p) f -> q p f", p=P)[q]
                r, c = q // CH, q % CH
                return down_w[P * r:P * r + P, E * c:E * c + E]

            def w_target(dst, q, lot):
                if lot < 2:
                    return dst[:, :, bass.ds(lot * FF + q * P, P)]
                r, c = q // CH, q % CH
                return dst[:, CH * c:CH * c + CH, P * r:P * r + P]

            def each_piece(eng, body):
                for lot in (0, 1):
                    first = At(lot * 8, 0)
                    if lot == 0:
                        body(At(0, 0), 0, 0)
                        body(At(0, 1), 1, 0)
                    with eng.Fori(1 if lot == 0 else 0, 8) as k:
                        for j in (0, 1):
                            body(At(k + 8 * lot, j), k * 2 + j, lot)
                for q in range(DP):
                    body(At(16 + q // 2, q % 2), q, 2)

            @block.gpsimd
            def _(gp):
                identity_matrix(gp, ones, ident, ones_made, ident_ready)

                def body(a, q, lot):
                    gp.wait_ge(w_rounded, a.n + 1)
                    work, magic = w_work[a.par], w_magic[a.par]
                    nc.gpsimd.tensor_tensor(work[:, :], work[:, :], magic[:, :], ALU.subtract).then_inc(w_pool, 1)
                    gp.wait_ge(w_pool, a.n + 1)
                    nc.gpsimd.tensor_tensor(blocks(work[:, :]), blocks(work[:, :]),
                                            spread(w_scales[a.par][:, 2, :], MX_BLOCK), ALU.mult).then_inc(w_ready, 1)

                each_piece(gp, body)

            @block.sync
            def _(sp):
                def body(a, q, lot):
                    if not (isinstance(a.n, int) and a.n < 2):
                        sp.wait_ge(w_rounded, a.n - 1)
                    sp.dma_start(w_in[a.par][:, :], w_source(q, lot)).then_inc(w_loaded[a.par], 16)

                each_piece(sp, body)

            @block.vector
            def _(v):
                chain = Chain(v, w_chain, MX_ROUND_LINKS + 1)
                moment_constants(nc.vector, m_const, const_ready)

                def low(a, q, lot):
                    v.wait_ge(w_hi, a.n + 1)
                    dst = wgu if lot < 2 else wdn
                    src = t_ps if a.par == 0 else xt_ps
                    nc.vector.tensor_tensor(w_target(dst[1], q, lot), src[:, :].rearrange("p (a b) -> p a b", b=P),
                                            w_target(dst[0], q, lot), ALU.subtract).then_inc(w_lo, 1)

                def body(a, q, lot):
                    v.wait_ge(w_loaded[a.par], 16 * (a.half + 1))
                    if not (isinstance(a.n, int) and a.n < 2):
                        v.wait_ge(w_transposed, a.n - 1)
                    sc = w_scales[a.par]
                    chain.start(a.n)
                    mx_round_links(nc.vector, chain.link, w_in[a.par][:, :], sc[:, 0, :], sc[:, 1, :],
                                   w_work[a.par][:, :], w_magic[a.par][:, :], MX_EPS, sc[:, 2, :]).then_inc(w_rounded, 1)
                    low(a, q, lot)

                each_piece(v, body)

            @block.tensor
            def _(pe):
                pe.wait_ge(ident_ready, 1)

                def body(a, q, lot):
                    pe.wait_ge(w_ready, a.n + 1)
                    if not (isinstance(a.n, int) and a.n < 2):
                        pe.wait_ge(w_lo, a.n - 1)
                    dst = t_ps if a.par == 0 else xt_ps
                    for j in range(KC):
                        last = nc.tensor.transpose(dst[:, P * j:P * j + P], w_work[a.par][:, P * j:P * j + P], ident[:, :])
                    last.then_inc(w_transposed, 1)

                each_piece(pe, body)

            @block.scalar
            def _(act):
                def body(a, q, lot):
                    act.wait_ge(w_transposed, a.n + 1)
                    dst = wgu if lot < 2 else wdn
                    src = t_ps if a.par == 0 else xt_ps
                    nc.scalar.activation(w_target(dst[0], q, lot), src[:, :].rearrange("p (a b) -> p a b", b=P),
                                         ACT.Copy).then_inc(w_hi, 1)

                each_piece(act, body)

        x_loaded = [sem(f"x_loaded{i}") for i in range(2)]
        res_loaded = [sem(f"res_loaded{i}") for i in range(2)]
        stats_ready, x_pool = sem("stats_ready"), sem("x_pool")
        x_chain, x_rounded, xd_ready = sem("x_chain"), sem("x_rounded"), sem("xd_ready")
        xt_done, xt_hi, xt_lo = sem("xt_done"), sem("xt_hi"), sem("xt_lo")
        gate_done, up_done, silu_done = sem("gate_done"), sem("up_done"), sem("silu_done")
        h_chain, h_made, h_rounded, h_pool, hd_ready = (sem("h_chain"), sem("h_made"), sem("h_rounded"),
                                                        sem("h_pool"), sem("hd_ready"))
        ht_done, ht_hi, ht_lo = sem("ht_done"), sem("ht_hi"), sem("ht_lo")
        down_step, y_made = sem("down_step"), sem("y_made")
        stored = [sem(f"stored{i}") for i in range(2)]

        x2_t = x2.rearrange("(t p) e -> t p e", p=P)
        out_t = out.rearrange("(t p) e -> t p e", p=P)

        def tiles(eng, body):
            body(At(0, 0))
            body(At(0, 1))
            with eng.Fori(1, TILES // 2 - 1) as k:
                body(At(k, 0))
                body(At(k, 1))
            body(At(TILES // 2 - 1, 0))
            body(At(TILES // 2 - 1, 1))

        def early(t, n):
            return isinstance(t.n, int) and t.n < n

        def final(t):
            return isinstance(t.n, int) and t.n == TILES - 1

        with nc.Block() as block:
            @block.sync
            def _(sp):
                def load_x(t):
                    if not early(t, 2):
                        sp.wait_ge(x_rounded, t.n - 1)
                    sp.dma_start(x_in[t.par][:, :], x2_t[t.n]).then_inc(x_loaded[t.par], 16)

                def store(t):
                    sp.wait_ge(y_made, t.n + 1)
                    sp.dma_start(out_t[t.n], y[t.par][:, :]).then_inc(stored[t.par], 16)

                load_x(At(0, 0))

                def body(t):
                    if not final(t):
                        load_x(t.plus(1))
                    if not early(t, 2):
                        sp.wait_ge(y_made, t.n - 1)
                    sp.dma_start(x_res[t.par][:, :], x2_t[t.n]).then_inc(res_loaded[t.par], 16)
                    if not early(t, 1):
                        store(t.plus(-1))

                tiles(sp, body)
                store(At(TILES // 2 - 1, 1))
                for i in range(2):
                    sp.wait_ge(stored[i], 16 * (TILES // 2))

            @block.gpsimd
            def _(gp):
                chain = Chain(gp, x_pool, MOMENT_LINKS + 1)

                def rstd(t):
                    gp.wait_ge(stats_ready, t.n + 1)
                    chain.start(t.n)
                    moments(nc.gpsimd, chain.link, x_stats, x_mean[:, :], x_rstd[:, :], m_const, m_tmp)

                def x_dequant(t):
                    gp.wait_ge(x_rounded, t.n + 1)
                    chain.link(nc.gpsimd.tensor_tensor(x_work[:, :], x_work[:, :], x_magic[:, :], ALU.subtract))
                    nc.gpsimd.tensor_tensor(blocks(x_work[:, :]), blocks(x_work[:, :]),
                                            spread(x_scales[:, 0, :], MX_BLOCK), ALU.mult).then_inc(xd_ready, 1)

                def h_dequant(t, c):
                    s = t.n * CH + c
                    gp.wait_ge(h_rounded, s + 1)
                    w = h_work[c % 2]
                    nc.gpsimd.tensor_tensor(w[:, :], w[:, :], h_magic[c % 2][:, :], ALU.subtract).then_inc(h_pool, 1)
                    gp.wait_ge(h_pool, s + 1)
                    nc.gpsimd.tensor_tensor(blocks(w[:, :]), blocks(w[:, :]),
                                            spread(h_scales[c % 2][:, 0, :], MX_BLOCK), ALU.mult).then_inc(hd_ready, 1)

                rstd(At(0, 0))
                x_dequant(At(0, 0))

                def body(t):
                    for c in range(CH):
                        if c == 0 and not final(t):
                            rstd(t.plus(1))
                        h_dequant(t, c)
                        if c == 1 and not final(t):
                            x_dequant(t.plus(1))

                tiles(gp, body)

            @block.vector
            def _(v):
                x_links = Chain(v, x_chain, 1 + MX_ROUND_LINKS)
                h_links = Chain(v, h_chain, 1 + MX_ROUND_LINKS)

                def x_stats_of(t):
                    v.wait_ge(x_loaded[t.par], 16 * (t.half + 1))
                    nc.vector.bn_stats(x_stats[:, 0, :], x_in[t.par][:, :]).then_inc(stats_ready, 1)

                def x_round(t):
                    v.wait_ge(x_pool, (MOMENT_LINKS + 1) * t.n + MOMENT_LINKS)
                    x_links.start(t.n)
                    if not early(t, 1):
                        v.wait_ge(xt_done, t.n)
                    x_links.link(nc.vector.tensor_scalar(x_norm[:, :], x_in[t.par][:, :], x_mean[:, 0:1],
                                                         x_rstd[:, 0:1], ALU.subtract, ALU.mult))
                    mx_round_links(nc.vector, x_links.link, x_norm[:, :], x_scales[:, 0, :], x_scales[:, 1, :],
                                   x_work[:, :], x_magic[:, :], MX_EPS).then_inc(x_rounded, 1)

                def x_low(t):
                    v.wait_ge(xt_hi, t.n + 1)
                    nc.vector.tensor_tensor(xT[t.par][1][:, :, :], xt_ps[:, :].rearrange("p (a b) -> p a b", b=P),
                                            xT[t.par][0][:, :, :], ALU.subtract).then_inc(xt_lo, 1)

                def h_round(t, c):
                    s, i = t.n * CH + c, c % 2
                    v.wait_ge(up_done, s + 1)
                    v.wait_ge(silu_done, s + 1)
                    h_links.start(s)
                    link_h = nc.vector.tensor_tensor(h[i][:, :], u_ps[i][:, :], sg[i][:, :], ALU.mult)
                    h_links.link(link_h)
                    if not (early(t, 1) and c < 2):
                        v.wait_ge(ht_done, s - 1)
                    mx_round_links(nc.vector, h_links.link, h[i][:, :], h_scales[i][:, 0, :], h_scales[i][:, 1, :],
                                   h_work[i][:, :], h_magic[i][:, :], W_SCALE * MX_EPS).then_inc(h_rounded, 1)

                def h_low(t, c):
                    s, i = t.n * CH + c, c % 2
                    v.wait_ge(ht_hi, s + 1)
                    if not (early(t, 1) and c < 2):
                        v.wait_ge(down_step, s - 1)
                    nc.vector.tensor_tensor(hT[i][1][:, :, :], t_ps[:, :].rearrange("p (a b) -> p a b", b=P),
                                            hT[i][0][:, :, :], ALU.subtract).then_inc(ht_lo, 1)

                def y_of(t):
                    v.wait_ge(down_step, CH * t.n + CH)
                    v.wait_ge(res_loaded[t.par], 16 * (t.half + 1))
                    if not early(t, 2):
                        v.wait_ge(stored[t.par], 16 * t.half)
                    nc.vector.scalar_tensor_tensor(y[t.par][:, :], d_ps[t.par][:, :], W_SCALE ** -2, x_res[t.par][:, :],
                                                   ALU.mult, ALU.add).then_inc(y_made, 1)

                x_stats_of(At(0, 0))
                x_round(At(0, 0))
                x_low(At(0, 0))

                def body(t):
                    for c in range(CH):
                        if c == 0 and not final(t):
                            x_stats_of(t.plus(1))
                        if c == 1 and not final(t):
                            x_round(t.plus(1))
                        h_round(t, c)
                        if c >= 2:
                            h_low(t, c - 2)
                        elif not early(t, 1):
                            h_low(t.plus(-1), CH + c - 2)
                        if c == 2 and not early(t, 1):
                            y_of(t.plus(-1))
                        if c == 3 and not final(t):
                            x_low(t.plus(1))

                tiles(v, body)
                last = At(TILES // 2 - 1, 1)
                h_low(last, 2)
                h_low(last, 3)
                y_of(last)

            @block.scalar
            def _(act):
                def x_high(t):
                    act.wait_ge(xt_done, t.n + 1)
                    nc.scalar.activation(xT[t.par][0][:, :, :], xt_ps[:, :].rearrange("p (a b) -> p a b", b=P),
                                         ACT.Copy).then_inc(xt_hi, 1)

                def silu(t, c):
                    s, i = t.n * CH + c, c % 2
                    act.wait_ge(gate_done, s + 1)
                    if not (early(t, 1) and c < 2):
                        act.wait_ge(h_chain, (1 + MX_ROUND_LINKS) * (s - 2) + 1)
                    nc.scalar.activation(sg[i][:, :], g_ps[i][:, :], ACT.Silu, scale=1.0 / W_SCALE).then_inc(silu_done, 1)

                def h_high(t, c):
                    s, i = t.n * CH + c, c % 2
                    act.wait_ge(ht_done, s + 1)
                    if not (early(t, 1) and c < 2):
                        act.wait_ge(down_step, s - 1)
                    nc.scalar.activation(hT[i][0][:, :, :], t_ps[:, :].rearrange("p (a b) -> p a b", b=P),
                                         ACT.Copy).then_inc(ht_hi, 1)

                x_high(At(0, 0))

                def body(t):
                    for c in range(CH):
                        silu(t, c)
                        if c >= 2:
                            h_high(t, c - 2)
                        elif not early(t, 1):
                            h_high(t.plus(-1), CH + c - 2)
                        if c == 3 and not final(t):
                            x_high(t.plus(1))

                tiles(act, body)
                last = At(TILES // 2 - 1, 1)
                h_high(last, 2)
                h_high(last, 3)

            @block.tensor
            def _(pe):
                def x_transpose(t):
                    pe.wait_ge(xd_ready, t.n + 1)
                    if not early(t, 1):
                        pe.wait_ge(xt_lo, t.n)
                    for j in range(KC):
                        last = nc.tensor.transpose(xt_ps[:, P * j:P * j + P], x_work[:, P * j:P * j + P], ident[:, :])
                    last.then_inc(xt_done, 1)

                def three_products(dst, a_hi, a_lo, b_hi, b_lo, n, start=True, stop=True):
                    last = None
                    for j in range(n):
                        for i, (a, b) in enumerate(((a_hi, b_hi), (a_hi, b_lo), (a_lo, b_hi))):
                            last = nc.tensor.matmul(dst, a(j), b(j), start=start and j == 0 and i == 0,
                                                    stop=stop and j == n - 1 and i == 2)
                    return last

                def gate_up(t, c):
                    s, i = t.n * CH + c, c % 2
                    if c == 0:
                        pe.wait_ge(xt_lo, t.n + 1)
                    if not (early(t, 1) and c < 2):
                        pe.wait_ge(silu_done, s - 1)
                    x_hi, x_lo = (lambda j, z=z: xT[t.par][z][:, j, :] for z in range(2))
                    for base, dst, done in ((0, g_ps, gate_done), (FF, u_ps, up_done)):
                        if base and not (early(t, 1) and c < 2):
                            pe.wait_ge(h_chain, (1 + MX_ROUND_LINKS) * (s - 2) + 1)
                        lo = base + E * c
                        w_hi_, w_lo_ = (lambda j, z=z: wgu[z][:, j, lo:lo + E] for z in range(2))
                        three_products(dst[i][:, :], x_hi, x_lo, w_hi_, w_lo_, KC).then_inc(done, 1)

                def h_transpose(t, c):
                    s, i = t.n * CH + c, c % 2
                    pe.wait_ge(hd_ready, s + 1)
                    if not (early(t, 1) and c < 1):
                        pe.wait_ge(ht_lo, s)
                    for j in range(KC):
                        last = nc.tensor.transpose(t_ps[:, P * j:P * j + P], h_work[i][:, P * j:P * j + P], ident[:, :])
                    last.then_inc(ht_done, 1)

                def down(t, c):
                    s, i = t.n * CH + c, c % 2
                    pe.wait_ge(ht_lo, s + 1)
                    if c == 0 and not early(t, 2):
                        pe.wait_ge(y_made, t.n - 1)
                    h_hi, h_lo = (lambda j, z=z: hT[i][z][:, j, :] for z in range(2))
                    w_hi_, w_lo_ = (lambda j, z=z: wdn[z][:, KC * c + j, :] for z in range(2))
                    three_products(d_ps[t.par][:, :], h_hi, h_lo, w_hi_, w_lo_, KC, start=c == 0,
                                   stop=c == CH - 1).then_inc(down_step, 1)

                x_transpose(At(0, 0))

                def body(t):
                    for c in range(CH):
                        gate_up(t, c)
                        if c >= 2:
                            h_transpose(t, c - 2)
                        elif not early(t, 1):
                            h_transpose(t.plus(-1), CH + c - 2)
                        if c == 3:
                            down(t, 0)
                        elif not early(t, 1):
                            down(t.plus(-1), c + 1)
                        if c == 3 and not final(t):
                            x_transpose(t.plus(1))

                tiles(pe, body)
                last = At(TILES // 2 - 1, 1)
                down(last, 1)
                h_transpose(last, 2)
                down(last, 2)
                h_transpose(last, 3)
                down(last, 3)
def split_weights(nc, block, parts, loaded, hi_done, lo_done, fixed):
    @block.sync
    def _(sp):
        for loads, *_ in parts:
            for dst, src in loads:
                sp.dma_start(dst, src).then_inc(loaded, 16)

    @block.scalar
    def _(act):
        act.wait_ge(loaded, 16 * sum(len(p[0]) for p in parts))
        for _, src, hi, _ in parts:
            nc.scalar.activation(hi, src, ACT.Copy, scale=W_SCALE).then_inc(hi_done, 1)

    @block.vector
    def _(v):
        fixed()
        v.wait_ge(loaded, 16 * sum(len(p[0]) for p in parts))
        for n, (_, src, hi, lo) in enumerate(parts):
            v.wait_ge(hi_done, n + 1)
            nc.vector.scalar_tensor_tensor(lo, src, W_SCALE, hi, ALU.mult, ALU.subtract).then_inc(lo_done, 1)


def self_attention(nc, x, wq, bq, wk, bk, wv, bv, wo, bo, qk_scratch, x1):
    NQ = E // P
    NKV = KV_HEADS * D
    SLOTS = HEADS + KV_HEADS
    STACK = 96
    MAX_ROW = STACK
    S2 = W_SCALE ** 2
    PAIRS = KV_HEADS // 2
    MU = 2 * TT

    with ExitStack() as ctx:
        sb = lambda name, shape, dt=F32: ctx.enter_context(nc.sbuf_tensor("a_" + name, shape, dt))
        ps = lambda name, n=512: ctx.enter_context(nc.psum_tensor("a_" + name, [P, n], F32))
        sem = lambda name: ctx.enter_context(nc.semaphore("a_" + name))
        two = lambda f, name, *a: [f(f"{name}{i}", *a) for i in range(2)]

        ones, ident = sb("ones", [P, P]), sb("ident", [P, P])
        w_qkv = two(sb, "w_qkv", [P, KC, E + 2 * NKV], F16)
        w_o = two(sb, "w_o", [P, PAIRS, E], F16)
        bias_qk = sb("bias_qk", [P, NQ + 1])
        bias_v, bias_o = sb("bias_v", [P, NKV]), sb("bias_o", [P, E])
        x_in = two(sb, "x_in", [P, TT, E])
        x_norm = sb("x_norm", [P, TT, E])
        stats, mean, rstd = sb("stats", [P, TT, 6]), sb("mean", [P, TT]), sb("rstd", [P, TT])
        m_const, m_tmp = sb("m_const", [P, len(MOMENT_CONSTANTS), TT]), sb("m_tmp", [P, 2, TT])
        xT = two(sb, "xT", [P, KC, SEQ], F16)
        qk = two(sb, "qk", [P, NQ + 1, SEQ], F16)
        stack = two(sb, "stack", [P, SLOTS, SEQ], F16)
        v_ones = two(sb, "v_ones", [P, TT, KV_HEADS, 2 * D])
        row_max, max_row = sb("row_max", [P, P]), sb("max_row", [HEADS * TT, P], F16)
        prob = [two(sb, f"prob{g}", [P, GROUP * SEQ]) for g in range(2)]
        o_t, o_norm = sb("o_t", [P, 2, SEQ // 32, 32]), sb("o_norm", [P, SEQ // 32, 2, D])
        o_rec = sb("o_rec", [P, 2, SEQ // 32])
        att = sb("att", [P, PAIRS, SEQ])
        att16 = two(sb, "att16", [P, PAIRS, SEQ], F16)
        x_res = two(sb, "x_res", [P, TT, E])

        s_ps = two(ps, "s", 1024)
        m_ps = two(ps, "m")
        o_ps, c_ps = ps("o"), ps("c")

        ones_made, ident_ready = sem("ones_made"), sem("ident_ready")
        loaded, hi_done, lo_done, bias_loaded, bias_ready = (
            sem("w_loaded"), sem("w_hi"), sem("w_lo"), sem("bias_loaded"), sem("bias_ready"))
        fixed_ready = sem("fixed_ready")

        with ExitStack() as prep, nc.Block() as block:
            stage = prep.enter_context(nc.sbuf_tensor("a_stage", [P, KC, E + 2 * NKV], F32))
            stage_o = prep.enter_context(nc.sbuf_tensor("a_stage_o", [P, PAIRS, E], F32))
            rows = lambda w: w.rearrange("(c p) n -> p c n", p=P)
            wo_rows = wo.rearrange("(gp g2 j d) n -> j g2 d gp n", gp=PAIRS, g2=2, j=GROUP)
            wo_loads = [(stage_o[32 * j + D * g2:32 * j + D * g2 + D, :, :], wo_rows[j, g2])
                        for j in range(GROUP) for g2 in range(2)]
            def constants():
                moment_constants(nc.vector, m_const, fixed_ready)
                for st in stack:
                    nc.vector.memset(st[64:STACK, :, :].bitcast(U32), 0).then_inc(fixed_ready, 1)
                    nc.vector.memset(st[MAX_ROW:MAX_ROW + 1, HEADS:SLOTS, :], -S2).then_inc(fixed_ready, 1)
                nc.vector.memset(row_max[:, HEADS * TT:P], 0.0).then_inc(fixed_ready, 1)
                for t in v_ones:
                    nc.vector.memset(t[:, :, :, D:2 * D], 1.0).then_inc(fixed_ready, 1)

            split_weights(nc, block, [
                ([(stage[:, :, 0:E], rows(wq)), (stage[:, :, E:E + NKV], rows(wk)),
                  (stage[:, :, E + NKV:E + 2 * NKV], rows(wv))], stage[:, :, :], w_qkv[0][:, :, :], w_qkv[1][:, :, :]),
                (wo_loads, stage_o[:, :, :], w_o[0][:, :, :], w_o[1][:, :, :]),
            ], loaded, hi_done, lo_done, constants)

            @block.gpsimd
            def _(gp):
                gp.dma_start(bias_qk[:, 0:NQ], bq.rearrange("(c p) -> p c", p=P), allow_slow_non_contiguous=True).then_inc(bias_loaded, 16)
                gp.dma_start(bias_qk[:, NQ:NQ + 1], bk.rearrange("(c p) -> p c", p=P), allow_slow_non_contiguous=True).then_inc(bias_loaded, 16)
                gp.dma_start(bias_v[:, :], bv.rearrange("(o n) -> o n", o=1).to_broadcast([P, NKV])).then_inc(bias_loaded, 16)
                gp.dma_start(bias_o[:, :], bo.rearrange("(o n) -> o n", o=1).to_broadcast([P, E])).then_inc(bias_loaded, 16)
                identity_matrix(gp, ones, ident, ones_made, ident_ready)
                gp.wait_ge(bias_loaded, 64)
                nc.gpsimd.tensor_scalar(bias_qk[:, :], bias_qk[:, :], W_SCALE, None, ALU.mult).then_inc(bias_ready, 1)
                nc.gpsimd.tensor_scalar(bias_v[:, :], bias_v[:, :], W_SCALE, None, ALU.mult).then_inc(bias_ready, 1)

        x_loaded, res_loaded, stored = two(sem, "x_loaded"), two(sem, "res_loaded"), two(sem, "stored")
        stats_ready, m_chain, norm_ready = sem("stats_ready"), sem("m_chain"), sem("norm_ready")
        xt_done, xt_hi, xt_lo = sem("xt_done"), sem("xt_hi"), sem("xt_lo")
        qkv_done, qk_hi, qk_lo, v_ready = sem("qkv_done"), sem("qk_hi"), sem("qk_lo"), sem("v_ready")
        left, stacked = sem("left"), two(sem, "stacked")
        max_done, max_taken, max_t, max_cast, max_placed = (
            sem("max_done"), sem("max_taken"), sem("max_t"), sem("max_cast"), two(sem, "max_placed"))
        score_done, prob_ready, pv_done = sem("score_done"), sem("prob_ready"), sem("pv_done")
        o_chain, att_ready, att_hi, att_lo = sem("o_chain"), sem("att_ready"), sem("att_hi"), sem("att_lo")
        y_done, biased, y_added = sem("y_done"), sem("biased"), sem("y_added")
        O_LINKS = 3

        xb = x.rearrange("b (t p) e -> b p t e", p=P)
        x1b = x1.rearrange("b (t p) e -> b p t e", p=P)

        known = lambda b: isinstance(b.n, int)
        early = lambda b, n: known(b) and b.n < n
        within = lambda b: not known(b) or b.n < BATCH

        def batches(eng, body):
            body(At(0, 0))
            body(At(0, 1))
            with eng.Fori(1, BATCH // 2 - 2) as k:
                body(At(k, 0))
                body(At(k, 1))
            for k in (BATCH // 2 - 2, BATCH // 2 - 1):
                body(At(k, 0))
                body(At(k, 1))

        with nc.Block() as block:
            @block.sync
            def _(sp):
                def load_x(b):
                    if not early(b, 2):
                        sp.wait_ge(norm_ready, b.n - 1)
                    sp.dma_start(x_in[b.par][:, :, :], xb[b.n]).then_inc(x_loaded[b.par], 16)

                def bounce(b):
                    sp.wait_ge(qk_hi, (NQ + 1) * (b.n + 1))
                    sp.dma_start(qk_scratch[b.n, 0].rearrange("(c p) s -> p c s", p=P), qk[0][:, :, :]).then_inc(left, 16)
                    sp.wait_ge(qk_lo, (NQ + 1) * (b.n + 1))
                    sp.dma_start(qk_scratch[b.n, 1].rearrange("(c p) s -> p c s", p=P), qk[1][:, :, :]).then_inc(left, 16)
                    sp.wait_ge(left, 32 * (b.n + 1))
                    st = stack[b.par]
                    src = [qk_scratch[b.n, z].rearrange("(h d) s -> d h s", d=D) for z in range(2)]
                    for row, q_half, k_half in ((0, 0, 0), (1, 1, 0), (2, 0, 1), (3, 1, 1)):
                        dst = st[D * row:D * row + D, :, :]
                        sp.dma_start(dst[:, 0:HEADS, :], src[q_half][:, 0:HEADS, :]).then_inc(stacked[b.par], 16)
                        sp.dma_start(dst[:, HEADS:SLOTS, :], src[k_half][:, HEADS:SLOTS, :]).then_inc(stacked[b.par], 16)

                def place_max(b):
                    sp.wait_ge(max_cast, b.n + 1)
                    dst = stack[b.par][MAX_ROW:MAX_ROW + 1, 0:HEADS, :]
                    sp.dma_start(dst.rearrange("o h (q t) -> o (h q) t", t=P),
                                 max_row[:, :]).then_inc(max_placed[b.par], 16)

                def load_res(b):
                    if not early(b, 2):
                        sp.wait_ge(stored[b.par], 16 * b.half)
                    sp.dma_start(x_res[b.par][:, :, :], xb[b.n]).then_inc(res_loaded[b.par], 16)

                def store(b):
                    sp.wait_ge(y_added, TT * (b.n + 1))
                    sp.dma_start(x1b[b.n], x_res[b.par][:, :, :]).then_inc(stored[b.par], 16)

                for n in range(3):
                    load_x(At(n // 2, n % 2)) if n < 2 else None
                bounce(At(0, 0))
                load_x(At(1, 0))
                place_max(At(0, 0))
                bounce(At(0, 1))

                def body(b):
                    if within(b.plus(3)):
                        load_x(b.plus(3))
                    load_res(b)
                    if within(b.plus(1)):
                        place_max(b.plus(1))
                    store(b)
                    if within(b.plus(2)):
                        bounce(b.plus(2))

                batches(sp, body)
                for i in range(2):
                    sp.wait_ge(stored[i], 16 * (BATCH // 2))

            @block.gpsimd
            def _(gp):
                chain = Chain(gp, m_chain, MOMENT_LINKS)

                def row_moments(b):
                    gp.wait_ge(stats_ready, TT * (b.n + 1))
                    chain.start(b.n)
                    moments(nc.gpsimd, chain.link, stats, mean[:, :], rstd[:, :], m_const, m_tmp)

                def add_bias(b):
                    gp.wait_ge(res_loaded[b.par], 16 * (b.half + 1))
                    r = x_res[b.par]
                    for t in range(TT):
                        nc.gpsimd.tensor_tensor(r[:, t, :], r[:, t, :], bias_o[:, :], ALU.add).then_inc(biased, 1)

                def low_att(b, p):
                    if p == 0 and not early(b, 1):
                        gp.wait_ge(y_done, TT * b.n)
                    gp.wait_ge(att_hi, PAIRS * b.n + p + 1)
                    nc.gpsimd.tensor_tensor(att16[1][:, p, :], att[:, p, :], att16[0][:, p, :],
                                            ALU.subtract).then_inc(att_lo, 1)

                row_moments(At(0, 0))
                row_moments(At(0, 1))

                def body(b):
                    if within(b.plus(2)):
                        row_moments(b.plus(2))
                    add_bias(b)
                    for p in range(PAIRS):
                        low_att(b, p)

                batches(gp, body)

            @block.vector
            def _(v):
                o_links = Chain(v, o_chain, O_LINKS)

                def layernorm_stats(b):
                    v.wait_ge(x_loaded[b.par], 16 * (b.half + 1))
                    for t in range(TT):
                        nc.vector.bn_stats(stats[:, t, :], x_in[b.par][:, t, :]).then_inc(stats_ready, 1)

                def layernorm(b):
                    v.wait_ge(m_chain, MOMENT_LINKS * (b.n + 1))
                    if not early(b, 1):
                        v.wait_ge(xt_done, 2 * b.n)
                    for t in range(TT):
                        last = nc.vector.tensor_scalar(x_norm[:, t, :], x_in[b.par][:, t, :], mean[:, t:t + 1],
                                                       rstd[:, t:t + 1], ALU.subtract, ALU.mult)
                    last.then_inc(norm_ready, 1)

                def take_max(b, g):
                    for u in range(MU):
                        n = (b.n * KV_HEADS + g) * MU + u
                        qt, pair = u // 2, u % 2
                        first = (GROUP * g + 2 * pair) * TT + qt
                        v.wait_ge(max_done, n + 1)
                        if g == 0 and u == 0 and not early(b, 1):
                            v.wait_ge(max_t, b.n)
                        nc.vector.tensor_reduce(row_max[:, first:first + TT + 1:TT],
                                                m_ps[u % 2][:, :].rearrange("p (h k) -> p h k", h=2),
                                                AX.X, ALU.max).then_inc(max_taken, 1)

                def normalize(b, p):
                    v.wait_ge(pv_done, KV_HEADS * b.n + 2 * p + 2)
                    o_links.start(PAIRS * b.n + p)
                    o_links.link(nc.vector.transpose(o_t[:, :, :, :].rearrange("p a b c -> p (a b c)"), o_ps[:, :]))
                    o_links.link(nc.vector.reciprocal(o_rec[:, :, :], o_t[:, :, :, D]))
                    o_links.link(nc.vector.tensor_tensor(
                        o_norm[:, :, :, :].rearrange("p b a d -> p a b d"), o_t[:, :, :, 0:D],
                        o_rec[:, :, :].rearrange("p a (b o) -> p a b o", o=1).to_broadcast([P, 2, SEQ // 32, D]), ALU.mult))
                    if not early(b, 1):
                        v.wait_ge(att_lo, PAIRS * (b.n - 1) + p + 1)
                    nc.vector.transpose(att[:, p, :], o_norm[:, :, :, :].rearrange("p b a d -> p (b a d)")).then_inc(att_ready, 1)

                def residual(b):
                    v.wait_ge(biased, TT * (b.n + 1))
                    for t, bank in enumerate((c_ps, m_ps[0])):
                        v.wait_ge(y_done, TT * b.n + t + 1)
                        r = x_res[b.par][:, t, :]
                        nc.vector.scalar_tensor_tensor(r, bank[:, :], W_SCALE ** -2, r, ALU.mult, ALU.add).then_inc(y_added, 1)

                def split_projections(b):
                    for i in range(2):
                        v.wait_ge(xt_hi, 2 * b.n + i + 1)
                        nc.vector.tensor_tensor(xT[1][:, 2 * i:2 * i + 2, :], m_ps[i][:, :].rearrange("p (c s) -> p c s", s=SEQ),
                                                xT[0][:, 2 * i:2 * i + 2, :], ALU.subtract).then_inc(xt_lo, 1)
                    if not early(b, 1):
                        v.wait_ge(left, 32 * b.n)
                    for c, bank in enumerate((c_ps, c_ps, m_ps[0], m_ps[0], m_ps[1])):
                        v.wait_ge(qk_hi, (NQ + 1) * b.n + min(c // 2 * 2 + 2, NQ + 1))
                        nc.vector.scalar_tensor_tensor(qk[1][:, c, :], bank[:, SEQ * (c % 2):SEQ * (c % 2) + SEQ],
                                                       bias_qk[:, c:c + 1], qk[0][:, c, :], ALU.add,
                                                       ALU.subtract).then_inc(qk_lo, 1)
                    v.wait_ge(qkv_done, 3 * (b.n + 1))
                    for t in range(TT):
                        nc.vector.tensor_tensor(
                            v_ones[b.par][:, t, :, 0:D],
                            m_ps[1][:, SEQ + NKV * t:SEQ + NKV * t + NKV].rearrange("p (g d) -> p g d", d=D),
                            bias_v[:, :].rearrange("p (g d) -> p g d", d=D), ALU.add).then_inc(v_ready, 1)

                for n in range(2):
                    layernorm_stats(At(0, n))
                    layernorm(At(0, n))
                    split_projections(At(0, n))
                    if n == 0:
                        for g in range(KV_HEADS):
                            take_max(At(0, 0), g)

                def body(b):
                    for step in range(KV_HEADS + 2):
                        if step == 0 and within(b.plus(2)):
                            layernorm_stats(b.plus(2))
                        if step == 2 and within(b.plus(2)):
                            layernorm(b.plus(2))
                        if step >= 2 and step % 2 == 0:
                            normalize(b, step // 2 - 1)
                        if step >= 2 and within(b.plus(1)):
                            take_max(b.plus(1), step - 2)
                    residual(b)
                    if within(b.plus(2)):
                        split_projections(b.plus(2))

                batches(v, body)

            @block.scalar
            def _(act):
                def exponentials(b, g):
                    for kt in range(TT):
                        s = 2 * (KV_HEADS * b.n + g) + kt
                        act.wait_ge(score_done, s + 1)
                        if kt == 0 and not (early(b, 1) and g < 2):
                            act.wait_ge(pv_done, KV_HEADS * b.n + g - 1)
                        nc.scalar.activation(prob[g % 2][kt][:, :], s_ps[kt][:, :], ACT.Exp,
                                             scale=D ** -0.5 / S2).then_inc(prob_ready, 1)

                def high_att(b, p):
                    act.wait_ge(att_ready, PAIRS * b.n + p + 1)
                    if p == 0 and not early(b, 1):
                        act.wait_ge(y_done, TT * b.n)
                    nc.scalar.activation(att16[0][:, p, :], att[:, p, :], ACT.Copy).then_inc(att_hi, 1)

                def cast_max(b):
                    act.wait_ge(max_t, b.n + 1)
                    if not early(b, 1):
                        prev = b.plus(-1)
                        act.wait_ge(max_placed[prev.par], 16 * (prev.half + 1))
                    nc.scalar.activation(max_row[:, :], c_ps[0:HEADS * TT, 0:P], ACT.Copy, scale=1.0 / S2).then_inc(max_cast, 1)

                def high_parts(b):
                    for i in range(2):
                        act.wait_ge(xt_done, 2 * b.n + i + 1)
                        nc.scalar.activation(xT[0][:, 2 * i:2 * i + 2, :], m_ps[i][:, :].rearrange("p (c s) -> p c s", s=SEQ),
                                             ACT.Copy).then_inc(xt_hi, 1)
                    if not early(b, 1):
                        act.wait_ge(left, 32 * b.n)
                    for c, bank in enumerate((c_ps, c_ps, m_ps[0], m_ps[0], m_ps[1])):
                        act.wait_ge(qkv_done, 3 * b.n + c // 2 + 1)
                        nc.scalar.activation(qk[0][:, c, :], bank[:, SEQ * (c % 2):SEQ * (c % 2) + SEQ], ACT.Identity,
                                             bias=bias_qk[:, c:c + 1]).then_inc(qk_hi, 1)

                high_parts(At(0, 0))
                cast_max(At(0, 0))
                high_parts(At(0, 1))

                def body(b):
                    for g in range(KV_HEADS):
                        exponentials(b, g)
                        if g in (3, 5):
                            high_att(b, (g - 3) // 2)
                    high_att(b, 2)
                    high_att(b, 3)
                    if within(b.plus(1)):
                        cast_max(b.plus(1))
                    if within(b.plus(2)):
                        high_parts(b.plus(2))

                batches(act, body)

            @block.tensor
            def _(pe):
                def products(dst, lhs, rhs, n, start=True, stop=True, skip=False):
                    for j in range(n):
                        for i, (a, b_) in enumerate(((0, 0), (0, 1), (1, 0))):
                            last = nc.tensor.matmul(dst, lhs(a, j), rhs(b_, j), start=start and j == 0 and i == 0,
                                                    stop=stop and j == n - 1 and i == 2)
                    return last

                def project(b):
                    pe.wait_ge(norm_ready, b.n + 1)
                    if not early(b, 2):
                        pe.wait_ge(y_added, TT * (b.n - 1))
                    if not early(b, 1):
                        pe.wait_ge(max_cast, b.n)
                    for i in range(2):
                        for c in range(2):
                            for t in range(TT):
                                last = nc.tensor.transpose(m_ps[i][:, SEQ * c + P * t:SEQ * c + P * t + P],
                                                           x_norm[:, t, P * (2 * i + c):P * (2 * i + c) + P], ident[:, :])
                        last.then_inc(xt_done, 1)
                    pe.wait_ge(xt_lo, 2 * (b.n + 1))
                    for c, bank in enumerate((c_ps, c_ps, m_ps[0], m_ps[0], m_ps[1])):
                        last = products(bank[:, SEQ * (c % 2):SEQ * (c % 2) + SEQ],
                                        lambda z, j: w_qkv[z][:, j, P * c:P * c + P], lambda z, j: xT[z][:, j, :], KC)
                        if c % 2 and c < NQ:
                            last.then_inc(qkv_done, 1)
                    for t in range(TT):
                        last = products(m_ps[1][:, SEQ + NKV * t:SEQ + NKV * t + NKV],
                                        lambda z, j: xT[z][:, j, P * t:P * t + P],
                                        lambda z, j: w_qkv[z][:, j, E + NKV:E + 2 * NKV], KC)
                    last.then_inc(qkv_done, 1)

                def max_scores(b, g):
                    if g == 0:
                        pe.wait_ge(stacked[b.par], 8 * 16 * (b.half + 1))
                        pe.wait_ge(qk_lo, (NQ + 1) * (b.n + 1))
                        pe.wait_ge(v_ready, TT * (b.n + 1))
                    st = stack[b.par]
                    for u in range(MU):
                        n = (b.n * KV_HEADS + g) * MU + u
                        qt, pair = u // 2, u % 2
                        if not (early(b, 1) and g == 0 and u < 2):
                            pe.wait_ge(max_taken, n - 1)
                        for e in range(2):
                            last = nc.tensor.matmul(m_ps[u % 2][:, SEQ * e:SEQ * e + SEQ],
                                                    st[0:STACK, GROUP * g + 2 * pair + e, P * qt:P * qt + P],
                                                    st[0:STACK, HEADS + g, :], start=True, stop=True)
                        last.then_inc(max_done, 1)

                def transpose_max(b):
                    pe.wait_ge(max_taken, KV_HEADS * MU * (b.n + 1))
                    nc.tensor.transpose(c_ps[:, 0:P], row_max[:, :], ident[:, :]).then_inc(max_t, 1)

                def scores(b, g):
                    st = stack[b.par]
                    if g == 0:
                        pe.wait_ge(max_placed[b.par], 16 * (b.half + 1))
                    for kt in range(TT):
                        s = 2 * (KV_HEADS * b.n + g) + kt
                        if not (early(b, 1) and g == 0):
                            pe.wait_ge(prob_ready, s - 1)
                        for pair in range(2):
                            h = GROUP * g + 2 * pair
                            last = nc.tensor.matmul(s_ps[kt][:, 512 * pair:512 * pair + 512],
                                                    st[0:MAX_ROW + 1, HEADS + g, P * kt:P * kt + P],
                                                    st[0:MAX_ROW + 1, h:h + 2, :], start=True, stop=True)
                        last.then_inc(score_done, 1)

                def weighted_values(b, g):
                    pe.wait_ge(prob_ready, 2 * (KV_HEADS * b.n + g) + 2)
                    if g % 2 == 0 and not (early(b, 1) and g == 0):
                        pe.wait_ge(o_chain, O_LINKS * (PAIRS * b.n + g // 2 - 1) + 1)
                    for kt in range(TT):
                        for j in range(GROUP):
                            last = nc.tensor.matmul(o_ps[32 * j:32 * j + 32, SEQ * (g % 2):SEQ * (g % 2) + SEQ],
                                                    v_ones[b.par][:, kt, g, :],
                                                    prob[g % 2][kt][:, SEQ * j:SEQ * j + SEQ],
                                                    start=kt == 0, stop=kt == TT - 1)
                    last.then_inc(pv_done, 1)

                def output(b):
                    pe.wait_ge(att_lo, PAIRS * (b.n + 1))
                    if within(b.plus(1)):
                        pe.wait_ge(max_cast, b.n + 2)
                    for t, bank in enumerate((c_ps, m_ps[0])):
                        products(bank[:, :], lambda z, j: att16[z][:, j, P * t:P * t + P],
                                 lambda z, j: w_o[z][:, j, :], PAIRS).then_inc(y_done, 1)

                project(At(0, 0))
                for g in range(KV_HEADS):
                    max_scores(At(0, 0), g)
                transpose_max(At(0, 0))
                project(At(0, 1))

                def body(b):
                    for step in range(KV_HEADS + 2):
                        if step < KV_HEADS:
                            scores(b, step)
                        if 1 <= step <= KV_HEADS:
                            weighted_values(b, step - 1)
                        if step >= 2 and within(b.plus(1)):
                            max_scores(b.plus(1), step - 2)
                    if within(b.plus(1)):
                        transpose_max(b.plus(1))
                    output(b)
                    if within(b.plus(2)):
                        project(b.plus(2))

                batches(pe, body)
def cross_attention(nc, x1, context, gamma, xc_scratch, x2):
    HPT = X_HEADS // TT
    KT = E // P
    SLOTS = 2 * X_HEADS
    STACK = 3 * X_D
    MAX_ROW = STACK

    with ExitStack() as ctx:
        sb = lambda name, shape, dt=F32: ctx.enter_context(nc.sbuf_tensor("x_" + name, shape, dt))
        ps = lambda name, n=512: ctx.enter_context(nc.psum_tensor("x_" + name, [P, n], F32))
        sem = lambda name: ctx.enter_context(nc.semaphore("x_" + name))
        two = lambda f, name, *a: [f(f"{name}{i}", *a) for i in range(2)]

        ones, ident = sb("ones", [P, P]), sb("ident", [P, P])
        gam = sb("gam", [P, 1])
        x_in, c_in = two(sb, "x_in", [P, TT, E]), two(sb, "c_in", [P, TT, E])
        x_norm = sb("x_norm", [P, TT, E])
        stats, mean, rstd = sb("stats", [P, TT, 6]), sb("mean", [P, TT]), sb("rstd", [P, TT])
        m_const, m_tmp = sb("m_const", [P, len(MOMENT_CONSTANTS), TT]), sb("m_tmp", [P, 2, TT])
        x16, c16 = two(sb, "x16", [P, TT, E], F16), two(sb, "c16", [P, TT, E], F16)
        stack = two(sb, "stack", [P, SLOTS, E], F16)
        v_t = two(sb, "v_t", [P, KT, SEQ])
        row_max, max_row = sb("row_max", [P, X_HEADS * KT]), sb("max_row", [X_HEADS * KT, P], F16)
        prob = [[sb(f"prob{t}{j}", [P, KT, E]) for j in range(HPT)] for t in range(TT)]
        s_t, s_rec, s_inv = sb("s_t", [P, E // 32, 32]), sb("s_rec", [P, E // 32]), sb("s_inv", [P, E])
        o_norm = sb("o_norm", [P, E])
        x_res = two(sb, "x_res", [P, TT, E])

        s_ps = two(ps, "s", 1024)
        m_ps = two(ps, "m")
        o_ps, r_ps = ps("o"), ps("r")

        ones_made, ident_ready, gam_loaded, fixed_ready = (
            sem("ones_made"), sem("ident_ready"), sem("gam_loaded"), sem("fixed_ready"))
        x_loaded, c_loaded = two(sem, "x_loaded"), two(sem, "c_loaded")
        res_loaded, stored = two(sem, "res_loaded"), two(sem, "stored")
        stats_ready, m_chain, norm_ready = sem("stats_ready"), sem("m_chain"), sem("norm_ready")
        x_hi, c_hi, split_ready = sem("x_hi"), sem("c_hi"), sem("split_ready")
        left, stacked = sem("left"), two(sem, "stacked")
        vt_done, vt_ready = sem("vt_done"), sem("vt_ready")
        max_done, max_taken, max_t, max_cast, max_placed = (
            sem("max_done"), sem("max_taken"), sem("max_t"), sem("max_cast"), two(sem, "max_placed"))
        score_done, prob_ready, pv_done = sem("score_done"), sem("prob_ready"), sem("pv_done")
        n_chain, y_added = sem("n_chain"), sem("y_added")
        N_LINKS = 4
        UNITS = 2 * X_HEADS

        with nc.Block() as block:
            @block.sync
            def _(sp):
                sp.dma_start(gam[:, :], gamma.rearrange("(o n) -> o n", o=1).to_broadcast([P, 1]),
                             allow_slow_non_contiguous=True).then_inc(gam_loaded, 16)
                sp.wait_ge(gam_loaded, 16)

            @block.gpsimd
            def _(gp):
                identity_matrix(gp, ones, ident, ones_made, ident_ready)

            @block.vector
            def _(v):
                moment_constants(nc.vector, m_const, fixed_ready)
                for st in stack:
                    nc.vector.memset(st[MAX_ROW:MAX_ROW + 1, X_HEADS:SLOTS, :], -1.0).then_inc(fixed_ready, 1)

        tiled = lambda t: t.rearrange("b (t p) e -> b p t e", p=P)
        x1b, ctxb, x2b = tiled(x1), tiled(context), tiled(x2)

        known = lambda b: isinstance(b.n, int)
        early = lambda b, n: known(b) and b.n < n
        within = lambda b: not known(b) or b.n < BATCH

        def batches(eng, body):
            body(At(0, 0))
            body(At(0, 1))
            with eng.Fori(1, BATCH // 2 - 2) as k:
                body(At(k, 0))
                body(At(k, 1))
            for k in (BATCH // 2 - 2, BATCH // 2 - 1):
                body(At(k, 0))
                body(At(k, 1))

        with nc.Block() as block:
            @block.sync
            def _(sp):
                def load(b):
                    sp.dma_start(x_in[b.par][:, :, :], x1b[b.n]).then_inc(x_loaded[b.par], 16)
                    sp.dma_start(c_in[b.par][:, :, :], ctxb[b.n]).then_inc(c_loaded[b.par], 16)

                def leave(b):
                    sp.wait_ge(split_ready, 4 * (b.n + 1))
                    for w, pair in enumerate((x16, c16)):
                        for z in range(2):
                            sp.dma_start(xc_scratch[b.n, w, z].rearrange("(t p) e -> p t e", p=P),
                                         pair[z][:, :, :]).then_inc(left, 16)

                def enter(b):
                    sp.wait_ge(left, 64 * (b.n + 1))
                    st = stack[b.par]
                    src = [[xc_scratch[b.n, w, z].rearrange("(h d) e -> d h e", d=X_D) for z in range(2)] for w in range(2)]
                    for row, x_half, c_half in ((0, 0, 0), (1, 1, 0), (2, 0, 1)):
                        dst = st[X_D * row:X_D * row + X_D, :, :]
                        sp.dma_start(dst[:, 0:X_HEADS, :], src[0][x_half]).then_inc(stacked[b.par], 16)
                        sp.dma_start(dst[:, X_HEADS:SLOTS, :], src[1][c_half]).then_inc(stacked[b.par], 16)

                def place_max(b):
                    sp.wait_ge(max_cast, b.n + 1)
                    dst = stack[b.par][MAX_ROW:MAX_ROW + 1, 0:X_HEADS, :]
                    sp.dma_start(dst.rearrange("o h (q t) -> o (h q) t", t=P),
                                 max_row[:, :]).then_inc(max_placed[b.par], 16)

                def load_res(b):
                    if not early(b, 2):
                        sp.wait_ge(stored[b.par], 16 * b.half)
                    sp.dma_start(x_res[b.par][:, :, :], x1b[b.n]).then_inc(res_loaded[b.par], 16)

                def store(b):
                    sp.wait_ge(y_added, TT * (b.n + 1))
                    sp.dma_start(x2b[b.n], x_res[b.par][:, :, :]).then_inc(stored[b.par], 16)

                load(At(0, 0))
                load(At(0, 1))
                leave(At(0, 0))
                enter(At(0, 0))
                leave(At(0, 1))
                enter(At(0, 1))
                place_max(At(0, 0))
                load(At(1, 0))

                def body(b):
                    load_res(b)
                    if within(b.plus(2)):
                        leave(b.plus(2))
                    if within(b.plus(1)):
                        place_max(b.plus(1))
                    if within(b.plus(2)):
                        enter(b.plus(2))
                    if within(b.plus(3)):
                        load(b.plus(3))
                    store(b)

                batches(sp, body)
                for i in range(2):
                    sp.wait_ge(stored[i], 16 * (BATCH // 2))

            @block.gpsimd
            def _(gp):
                chain = Chain(gp, m_chain, MOMENT_LINKS)

                def row_moments(b):
                    gp.wait_ge(stats_ready, TT * (b.n + 1))
                    chain.start(b.n)
                    moments(nc.gpsimd, chain.link, stats, mean[:, :], rstd[:, :], m_const, m_tmp)

                def low_parts(b):
                    for src, pair, hi in ((c_in[b.par], c16, c_hi), (x_norm, x16, x_hi)):
                        gp.wait_ge(hi, b.n + 1)
                        for t in range(TT):
                            nc.gpsimd.tensor_tensor(pair[1][:, t, :], src[:, t, :], pair[0][:, t, :],
                                                    ALU.subtract).then_inc(split_ready, 1)

                for n in range(2):
                    row_moments(At(0, n))
                    low_parts(At(0, n))

                def body(b):
                    if within(b.plus(2)):
                        row_moments(b.plus(2))
                        low_parts(b.plus(2))

                batches(gp, body)

            @block.vector
            def _(v):
                n_links = Chain(v, n_chain, N_LINKS)

                def layernorm_stats(b):
                    v.wait_ge(x_loaded[b.par], 16 * (b.half + 1))
                    for t in range(TT):
                        nc.vector.bn_stats(stats[:, t, :], x_in[b.par][:, t, :]).then_inc(stats_ready, 1)

                def layernorm(b):
                    v.wait_ge(m_chain, MOMENT_LINKS * (b.n + 1))
                    if not early(b, 1):
                        v.wait_ge(split_ready, 4 * b.n)
                    for t in range(TT):
                        last = nc.vector.tensor_scalar(x_norm[:, t, :], x_in[b.par][:, t, :], mean[:, t:t + 1],
                                                       rstd[:, t:t + 1], ALU.subtract, ALU.mult)
                    last.then_inc(norm_ready, 1)

                def take_max(b, h):
                    for qt in range(KT):
                        n = (b.n * X_HEADS + h) * KT + qt
                        v.wait_ge(max_done, n + 1)
                        if h == 0 and qt == 0 and not early(b, 1):
                            v.wait_ge(max_t, b.n)
                        nc.vector.tensor_reduce(row_max[:, KT * h + qt:KT * h + qt + 1], m_ps[qt % 2][:, :],
                                                AX.X, ALU.max).then_inc(max_taken, 1)

                def normalize(b, t):
                    n = TT * b.n + t
                    v.wait_ge(pv_done, n + 1)
                    n_links.start(n)
                    n_links.link(nc.vector.transpose(s_t[:, :, :].rearrange("p a c -> p (a c)"), r_ps[:, :]))
                    n_links.link(nc.vector.reciprocal(s_rec[:, :], s_t[:, :, 0]))
                    n_links.link(nc.vector.transpose(s_inv[:, :], spread(s_rec[:, :], 32)))
                    n_links.link(nc.vector.tensor_tensor(o_norm[:, :], o_ps[:, :], s_inv[:, :], ALU.mult))
                    if t == 0:
                        v.wait_ge(res_loaded[b.par], 16 * (b.half + 1))
                    r = x_res[b.par][:, t, :]
                    nc.vector.scalar_tensor_tensor(r, o_norm[:, :], gam[:, 0:1], r, ALU.mult, ALU.add).then_inc(y_added, 1)

                for n in range(2):
                    layernorm_stats(At(0, n))
                    layernorm(At(0, n))
                for h in range(X_HEADS):
                    take_max(At(0, 0), h)

                def body(b):
                    for step in range(X_HEADS + 2):
                        if step == 0 and within(b.plus(2)):
                            layernorm_stats(b.plus(2))
                        if step == 2 and within(b.plus(2)):
                            layernorm(b.plus(2))
                        if step == X_HEADS:
                            normalize(b, 0)
                        if step >= 2 and within(b.plus(1)):
                            take_max(b.plus(1), step - 2)
                    normalize(b, 1)

                batches(v, body)

            @block.scalar
            def _(act):
                def exponentials(b, h):
                    for u in range(2):
                        s = 2 * (X_HEADS * b.n + h) + u
                        act.wait_ge(score_done, s + 1)
                        if h % HPT == 0 and u == 0 and not early(b, 1):
                            act.wait_ge(pv_done, TT * (b.n - 1) + h // HPT + 1)
                        nc.scalar.activation(prob[h // HPT][h % HPT][:, 2 * u:2 * u + 2, :],
                                             s_ps[u][:, :].rearrange("p (k q) -> p k q", k=2), ACT.Exp,
                                             scale=X_D ** -0.5).then_inc(prob_ready, 1)

                def cast_max(b):
                    act.wait_ge(max_t, b.n + 1)
                    if not early(b, 1):
                        prev = b.plus(-1)
                        act.wait_ge(max_placed[prev.par], 16 * (prev.half + 1))
                    nc.scalar.activation(max_row[:, :], m_ps[0][0:X_HEADS * KT, 0:P], ACT.Copy).then_inc(max_cast, 1)

                def high_parts(b):
                    if not early(b, 1):
                        act.wait_ge(left, 64 * b.n)
                    act.wait_ge(c_loaded[b.par], 16 * (b.half + 1))
                    nc.scalar.activation(c16[0][:, :, :], c_in[b.par][:, :, :], ACT.Copy).then_inc(c_hi, 1)
                    act.wait_ge(norm_ready, b.n + 1)
                    nc.scalar.activation(x16[0][:, :, :], x_norm[:, :, :], ACT.Copy).then_inc(x_hi, 1)

                def keep_vt(b):
                    if not early(b, 2):
                        act.wait_ge(pv_done, TT * (b.n - 1))
                    for i in range(2):
                        act.wait_ge(vt_done, 2 * b.n + i + 1)
                        nc.scalar.activation(v_t[b.par][:, 2 * i:2 * i + 2, :], m_ps[i][:, :].rearrange("p (k s) -> p k s", s=SEQ),
                                             ACT.Copy).then_inc(vt_ready, 1)

                high_parts(At(0, 0))
                high_parts(At(0, 1))
                keep_vt(At(0, 0))
                cast_max(At(0, 0))
                keep_vt(At(0, 1))

                def body(b):
                    for h in range(X_HEADS):
                        exponentials(b, h)
                        if h == 4 and within(b.plus(2)):
                            high_parts(b.plus(2))
                    if within(b.plus(1)):
                        cast_max(b.plus(1))
                    if within(b.plus(2)):
                        keep_vt(b.plus(2))

                batches(act, body)

            @block.tensor
            def _(pe):
                def transpose_context(b):
                    pe.wait_ge(c_loaded[b.par], 16 * (b.half + 1))
                    if not early(b, 1):
                        pe.wait_ge(max_cast, b.n)
                    for i in range(2):
                        for k in range(2):
                            for t in range(TT):
                                last = nc.tensor.transpose(m_ps[i][:, SEQ * k + P * t:SEQ * k + P * t + P],
                                                           c_in[b.par][:, t, P * (2 * i + k):P * (2 * i + k) + P], ident[:, :])
                        last.then_inc(vt_done, 1)

                def max_scores(b, h):
                    if h == 0:
                        pe.wait_ge(stacked[b.par], 6 * 16 * (b.half + 1))
                        pe.wait_ge(vt_ready, 2 * (b.n + 1))
                    st = stack[b.par]
                    for qt in range(KT):
                        n = (b.n * X_HEADS + h) * KT + qt
                        if not (early(b, 1) and h == 0 and qt < 2):
                            pe.wait_ge(max_taken, n - 1)
                        nc.tensor.matmul(m_ps[qt % 2][:, :], st[0:STACK, h, P * qt:P * qt + P],
                                         st[0:STACK, X_HEADS + h, :], start=True, stop=True).then_inc(max_done, 1)

                def transpose_max(b):
                    pe.wait_ge(max_taken, X_HEADS * KT * (b.n + 1))
                    nc.tensor.transpose(m_ps[0][0:X_HEADS * KT, 0:P], row_max[:, :], ident[:, :]).then_inc(max_t, 1)

                def scores(b, h):
                    st = stack[b.par]
                    if h == 0:
                        pe.wait_ge(max_placed[b.par], 16 * (b.half + 1))
                    for u in range(2):
                        s = 2 * (X_HEADS * b.n + h) + u
                        if not (early(b, 1) and h == 0):
                            pe.wait_ge(prob_ready, s - 1)
                        for k in range(2):
                            kt = 2 * u + k
                            last = nc.tensor.matmul(s_ps[u][:, E * k:E * k + E],
                                                    st[0:MAX_ROW + 1, X_HEADS + h, P * kt:P * kt + P],
                                                    st[0:MAX_ROW + 1, h, :], start=True, stop=True)
                        last.then_inc(score_done, 1)

                def weighted_values(b, t, kt):
                    if kt == 0:
                        pe.wait_ge(prob_ready, 2 * (X_HEADS * b.n + HPT * (t + 1)))
                        if not (early(b, 1) and t == 0):
                            pe.wait_ge(n_chain, N_LINKS * (TT * b.n + t))
                    for dst, summed in ((o_ps, False), (r_ps, True)):
                        for j in range(HPT):
                            row = X_D * (HPT * t + j)
                            lhs = ones[:, 0:X_D] if summed else v_t[b.par][:, kt, row:row + X_D]
                            last = nc.tensor.matmul(dst[X_D * j:X_D * j + X_D, :], lhs, prob[t][j][:, kt, :],
                                                    start=kt == 0, stop=kt == KT - 1)
                    if kt == KT - 1:
                        last.then_inc(pv_done, 1)

                transpose_context(At(0, 0))
                for h in range(X_HEADS):
                    max_scores(At(0, 0), h)
                transpose_max(At(0, 0))
                transpose_context(At(0, 1))

                def body(b):
                    for step in range(X_HEADS + 2):
                        if step < X_HEADS:
                            scores(b, step)
                        if HPT <= step < X_HEADS:
                            weighted_values(b, 0, step - HPT)
                        if step >= X_HEADS:
                            for kt in range(2):
                                weighted_values(b, 1, 2 * (step - X_HEADS) + kt)
                        if step >= 2 and within(b.plus(1)):
                            max_scores(b.plus(1), step - 2)
                    if within(b.plus(1)):
                        transpose_max(b.plus(1))
                    if within(b.plus(2)):
                        transpose_context(b.plus(2))

                batches(pe, body)
def decoder_block(nc, x, context, wq, bq, wk, bk, wv, bv, wo, bo, gamma, gate_w, up_w, down_w, out):
    scratch = lambda name, shape, dt=F32: nc.dram_tensor(name, shape, dt, kind="Internal").ap()
    x1, x2 = scratch("x1", (BATCH, SEQ, E)), scratch("x2", (BATCH, SEQ, E))
    qk = scratch("qk_halves", (BATCH, 2, E + KV_HEADS * D, SEQ), F16)
    xc = scratch("xc_halves", (BATCH, 2, 2, SEQ, E), F16)
    self_attention(nc, x, wq, bq, wk, bk, wv, bv, wo, bo, qk, x1)
    cross_attention(nc, x1, context, gamma, xc, x2)
    rows = lambda t: t.rearrange("b s e -> (b s) e")
    feed_forward(nc, rows(x2), gate_w, up_w, down_w, rows(out))


_INS = ["x", "ctx_2048", "L0_attn_Wq", "L0_attn_bq", "L0_attn_Wk", "L0_attn_bk", "L0_attn_Wv", "L0_attn_bv",
        "L0_attn_Wo", "L0_attn_bo", "L0_xattn_gamma", "L0_ffn_gate_w", "L0_ffn_up_w", "L0_ffn_down_w"]


def kernel(**inputs):
    import numpy as _np
    import concourse.bacc as _bacc
    from concourse.bass_utils import run_bass_kernel_spmd as _run

    nc = _bacc.Bacc("TRN2", target_bir_lowering=False, num_devices=1)
    arrays, args = {}, []
    for name in _INS:
        a = _np.ascontiguousarray(inputs[name])
        if a.ndim == 0:
            a = a.reshape(1)
        arrays[f"in_{name}_dram"] = a
        args.append(nc.dram_tensor(f"in_{name}_dram", a.shape, mybir.dt.from_np(a.dtype), kind="ExternalInput").ap())
    args.append(nc.dram_tensor("out_0_dram", (BATCH, SEQ, E), F32, kind="ExternalOutput").ap())
    decoder_block(nc, *args)
    r = _run(nc, [arrays], core_ids=[0])
    return r.results[0]["out_0_dram"]
```

```python
from contextlib import ExitStack

import concourse.bass as bass
from concourse import mybir

F32 = mybir.dt.float32
F16 = mybir.dt.float16
U32 = mybir.dt.uint32
I32 = mybir.dt.int32
ALU = mybir.AluOpType
ACT = mybir.ActivationFunctionType
AX = mybir.AxisListType

P = 128
BATCH, SEQ, E = 16, 256, 512
KC = E // P
TT = SEQ // P
HEADS, KV_HEADS, D = 32, 8, 16
GROUP = HEADS // KV_HEADS
X_HEADS, X_D = 8, 32
FF = 2048
LN_EPS = 1e-5
W_SCALE = 64.0
MX_BLOCK, MX_MAX, MX_EPS = 32, 448.0, 1e-30
FP8_MIN_EXP = 2.0 ** -6
EXP_MASK = 0x7F800000
HALF_BIT = 0x00400000
MX_SHIFT = 2.0 ** 20


class At:

    def __init__(self, k, off):
        self.k, self.off = k, off
        self.n = k * 2 + off
        self.par = off % 2
        self.half = k + off // 2

    def plus(self, m):
        return At(self.k, self.off + m)


class Chain:

    def __init__(self, eng, sem, per):
        self.eng, self.sem, self.per = eng, sem, per
        self.base, self.count = 0, 0

    def start(self, n):
        assert self.count in (0, self.per), (self.count, self.per)
        self.base, self.count = n * self.per, 0

    def link(self, ins):
        self.count += 1
        ins.then_inc(self.sem, 1)
        self.eng.wait_ge(self.sem, self.base + self.count)


def identity_matrix(gp, ones, ident, made, ready):
    gp.memset(ones[:, :], 1.0).then_inc(made, 1)
    gp.wait_ge(made, 1)
    gp.affine_select(ident[:, :], ones[:, :], pattern=[[-1, P]], compare_op=ALU.is_equal, fill=0.0,
                     base=0, channel_multiplier=1).then_inc(ready, 1)


MOMENT_CONSTANTS = (0.5, 1.0 / E, 0.25, LN_EPS, -0.5, 1.5)
MOMENT_LINKS = 10 + 5 * 2


def moment_constants(v, tile, done):
    for i, value in enumerate(MOMENT_CONSTANTS):
        v.memset(tile[:, i, :], value).then_inc(done, 1)


def moments(gp, link, stats, mean, rstd, const, t):
    half, inv_e, quarter, eps, neg_half, three_halves = (const[:, i, :] for i in range(6))
    op = gp.tensor_tensor
    link(op(mean, stats[:, :, 1], stats[:, :, 4], ALU.add))
    link(op(mean, mean, half, ALU.mult))
    link(op(t[:, 0], stats[:, :, 1], stats[:, :, 4], ALU.subtract))
    link(op(t[:, 0], t[:, 0], t[:, 0], ALU.mult))
    link(op(t[:, 0], t[:, 0], quarter, ALU.mult))
    link(op(t[:, 1], stats[:, :, 2], stats[:, :, 5], ALU.add))
    link(op(t[:, 1], t[:, 1], inv_e, ALU.mult))
    link(op(t[:, 0], t[:, 0], t[:, 1], ALU.add))
    link(op(t[:, 0], t[:, 0], eps, ALU.add))
    link(op(rstd, t[:, 0], neg_half, ALU.pow))
    for _ in range(2):
        link(op(t[:, 1], rstd, rstd, ALU.mult))
        link(op(t[:, 1], t[:, 1], t[:, 0], ALU.mult))
        link(op(t[:, 1], t[:, 1], half, ALU.mult))
        link(op(t[:, 1], three_halves, t[:, 1], ALU.subtract))
        link(op(rstd, rstd, t[:, 1], ALU.mult))


def blocks(ap):
    return ap.rearrange("p (a b) -> p a b", b=MX_BLOCK)


def spread(ap, n):
    return ap.rearrange("p (a o) -> p a o", o=1).to_broadcast([ap.shape[0], ap.shape[1], n])


def mx_round_links(v, link, src, scale, rscale, work, magic, eps):
    link(v.tensor_reduce(scale, blocks(src), AX.X, ALU.max, apply_absolute_value=True))
    link(v.tensor_scalar(scale, scale, 1.0 / MX_MAX, eps, ALU.mult, ALU.max))
    link(v.reciprocal(rscale, scale))
    link(v.tensor_tensor(blocks(work), blocks(src), spread(rscale, MX_BLOCK), ALU.mult))
    link(v.tensor_scalar(magic.bitcast(U32), work.bitcast(U32), EXP_MASK, HALF_BIT, ALU.bitwise_and,
                         ALU.bitwise_or))
    link(v.tensor_scalar(magic, magic, 1.5 * FP8_MIN_EXP, MX_SHIFT, ALU.max, ALU.mult))
    return v.tensor_tensor(work, work, magic, ALU.add)


MX_ROUND_LINKS = 6


class WeightQuantizer:

    def __init__(self, nc, sb, sem, name, piece, kept):
        self.nc, self.piece, self.kept = nc, piece, kept
        tile = lambda what, shape: sb(f"{name}_{what}", shape)
        self.src, self.work, self.magic_t = tile("in", [P, E]), tile("work", [P, E]), tile("magic", [P, E])
        self.scale = [tile(f"scale{i}", [P, E // MX_BLOCK]) for i in range(3)]
        self.loaded, self.scaled, self.divided, self.magic_ready, self.quantized, self.stored = (
            sem(f"{name}_{what}") for what in ("loaded", "scaled", "divided", "magic_ready", "quantized", "stored"))
        self.v_chain, self.gp_chain = sem(f"{name}_v_chain"), sem(f"{name}_gp_chain")

    def load(self, sp, b):
        if not (isinstance(b.n, int) and b.n < 1):
            sp.wait_ge(self.divided, b.n)
        dst, src = self.src[:, :], self.piece(b.n)
        if len(src.shape) == 3:
            dst = dst.rearrange("p (r e) -> p r e", r=src.shape[1])
        sp.dma_start(dst, src).then_inc(self.loaded, 16)

    def scales(self, v, b):
        ops, (scale, inverse, scaled_up), first = self.nc.vector, (t[:, :] for t in self.scale), 3 * b.n
        v.wait_ge(self.loaded, 16 * (b.n + 1))
        if not (isinstance(b.n, int) and b.n < 1):
            v.wait_ge(self.quantized, b.n)
        ops.tensor_reduce(scale, blocks(self.src[:, :]), AX.X, ALU.max,
                          apply_absolute_value=True).then_inc(self.v_chain, 1)
        v.wait_ge(self.v_chain, first + 1)
        ops.tensor_scalar(scale, scale, 1.0 / MX_MAX, MX_EPS, ALU.mult, ALU.max).then_inc(self.v_chain, 1)
        v.wait_ge(self.v_chain, first + 2)
        ops.reciprocal(inverse, scale).then_inc(self.scaled, 1)
        ops.tensor_scalar(scaled_up, scale, W_SCALE, None, ALU.mult).then_inc(self.scaled, 1)

    def divide(self, gp, b):
        gp.wait_ge(self.scaled, 2 * (b.n + 1))
        if not (isinstance(b.n, int) and b.n < 1):
            gp.wait_ge(self.stored, 16 * b.n)
        self.nc.gpsimd.tensor_tensor(blocks(self.work[:, :]), blocks(self.src[:, :]),
                                     spread(self.scale[1][:, :], MX_BLOCK), ALU.mult).then_inc(self.divided, 1)

    def magic(self, v, b):
        magic, work = self.magic_t[:, :], self.work[:, :]
        v.wait_ge(self.divided, b.n + 1)
        self.nc.vector.tensor_scalar(magic.bitcast(U32), work.bitcast(U32), EXP_MASK, HALF_BIT, ALU.bitwise_and,
                                     ALU.bitwise_or).then_inc(self.v_chain, 1)
        v.wait_ge(self.v_chain, 3 * b.n + 3)
        self.nc.vector.tensor_scalar(magic, magic, 1.5 * FP8_MIN_EXP, MX_SHIFT, ALU.max,
                                     ALU.mult).then_inc(self.magic_ready, 1)

    def round(self, gp, b):
        ops, magic, work = self.nc.gpsimd, self.magic_t[:, :], self.work[:, :]
        gp.wait_ge(self.magic_ready, b.n + 1)
        ops.tensor_tensor(work, work, magic, ALU.add).then_inc(self.gp_chain, 1)
        gp.wait_ge(self.gp_chain, 2 * b.n + 1)
        ops.tensor_tensor(work, work, magic, ALU.subtract).then_inc(self.gp_chain, 1)
        gp.wait_ge(self.gp_chain, 2 * b.n + 2)
        ops.tensor_tensor(blocks(work), blocks(work), spread(self.scale[2][:, :], MX_BLOCK),
                          ALU.mult).then_inc(self.quantized, 1)

    def store(self, sp, b):
        sp.wait_ge(self.quantized, b.n + 1)
        sp.dma_start(self.kept(b.n), self.work[:, :]).then_inc(self.stored, 16)


def feed_forward(nc, x2, weights, out):
    TILES = x2.shape[0] // P
    NB = E // MX_BLOCK
    CH = FF // E
    LOT = 4
    GU_LOTS = 2 * FF // P // LOT
    LOTS = GU_LOTS + FF // P // LOT

    with ExitStack() as ctx:
        sb = lambda name, shape, dt=F32: ctx.enter_context(nc.sbuf_tensor("f_" + name, shape, dt))
        ps = lambda name: ctx.enter_context(nc.psum_tensor("f_" + name, [P, 512], F32))
        sem = lambda name: ctx.enter_context(nc.semaphore("f_" + name))

        ones, ident = sb("ones", [P, P]), sb("ident", [P, P])
        wgu = [sb(f"wgu{i}", [P, KC, 2 * FF], F16) for i in range(2)]
        wdn = [sb(f"wdn{i}", [P, FF // P, E], F16) for i in range(2)]
        w_in = [sb(f"w_in{i}", [P, LOT, E]) for i in range(2)]
        x_in = [sb(f"x_in{i}", [P, E]) for i in range(2)]
        x_res = [sb(f"x_res{i}", [P, E]) for i in range(2)]
        x_norm, x_work, x_magic = sb("x_norm", [P, E]), sb("x_work", [P, E]), sb("x_magic", [P, E])
        x_stats, x_mean, x_rstd = sb("x_stats", [P, 1, 6]), sb("x_mean", [P, 1]), sb("x_rstd", [P, 1])
        m_const, m_tmp = sb("m_const", [P, len(MOMENT_CONSTANTS), 1]), sb("m_tmp", [P, 2, 1])
        x_scales = sb("x_scales", [P, 2, NB])
        xT = [[sb(f"xT{i}{h}", [P, KC, P], F16) for h in "hl"] for i in range(2)]
        sg = [sb(f"sg{i}", [P, E]) for i in range(2)]
        h = [sb(f"h{i}", [P, E]) for i in range(2)]
        h_work = [sb(f"h_work{i}", [P, E]) for i in range(2)]
        h_magic = [sb(f"h_magic{i}", [P, E]) for i in range(2)]
        h_scales = [sb(f"h_scales{i}", [P, 2, NB]) for i in range(2)]
        hT = [[sb(f"hT{i}{x}", [P, KC, P], F16) for x in "hl"] for i in range(2)]
        y = [sb(f"y{i}", [P, E]) for i in range(2)]

        g_ps, u_ps, d_ps = ([ps(f"{n}{i}") for i in range(2)] for n in ("g", "u", "d"))
        t_ps, xt_ps = ps("t"), ps("xt")

        ones_made, ident_ready, const_ready = sem("ones_made"), sem("ident_ready"), sem("const_ready")
        w_loaded = [sem(f"w_loaded{i}") for i in range(2)]
        w_transposed, w_hi, w_lo = sem("w_transposed"), sem("w_hi"), sem("w_lo")
        w_ps = g_ps + u_ps

        with nc.Block() as block:
            def each_lot(eng, body):
                body(At(0, 0), True)
                body(At(0, 1), True)
                with eng.Fori(1, GU_LOTS // 2) as k:
                    body(At(k, 0), True)
                    body(At(k, 1), True)
                with eng.Fori(GU_LOTS // 2, LOTS // 2) as k:
                    body(At(k, 0), False)
                    body(At(k, 1), False)

            def target(z, a, i, gate_up):
                n = a.n * LOT + i
                if gate_up:
                    return wgu[z][:, :, bass.ds(n * P, P)]
                n = n - GU_LOTS * LOT
                return wdn[z][:, bass.ds(n, 1), :].rearrange("p o (r e) -> p (o r) e", e=P)

            @block.gpsimd
            def _(gp):
                identity_matrix(gp, ones, ident, ones_made, ident_ready)

            @block.sync
            def _(sp):
                def body(a, gate_up):
                    if not (isinstance(a.n, int) and a.n < 2):
                        sp.wait_ge(w_transposed, LOT * (a.n - 1))
                    sp.dma_start(w_in[a.par][:, :, :], weights.rearrange("(l i) p e -> l p i e", i=LOT)[a.n]
                                 ).then_inc(w_loaded[a.par], 16)

                each_lot(sp, body)

            @block.tensor
            def _(pe):
                pe.wait_ge(ident_ready, 1)

                def body(a, gate_up):
                    for i in range(LOT):
                        if i == 0:
                            pe.wait_ge(w_loaded[a.par], 16 * (a.half + 1))
                        if not (isinstance(a.n, int) and a.n < 1):
                            pe.wait_ge(w_lo, LOT * a.n + i - LOT + 1)
                        for j in range(KC):
                            last = nc.tensor.transpose(w_ps[i][:, P * j:P * j + P], w_in[a.par][:, i, P * j:P * j + P],
                                                       ident[:, :])
                        last.then_inc(w_transposed, 1)

                each_lot(pe, body)

            @block.scalar
            def _(act):
                def body(a, gate_up):
                    for i in range(LOT):
                        act.wait_ge(w_transposed, LOT * a.n + i + 1)
                        nc.scalar.activation(target(0, a, i, gate_up), w_ps[i][:, :].rearrange("p (a b) -> p a b", b=P),
                                             ACT.Copy).then_inc(w_hi, 1)

                each_lot(act, body)

            @block.vector
            def _(v):
                moment_constants(nc.vector, m_const, const_ready)

                def body(a, gate_up):
                    for i in range(LOT):
                        v.wait_ge(w_hi, LOT * a.n + i + 1)
                        nc.vector.tensor_tensor(target(1, a, i, gate_up), w_ps[i][:, :].rearrange("p (a b) -> p a b", b=P),
                                                target(0, a, i, gate_up), ALU.subtract).then_inc(w_lo, 1)

                each_lot(v, body)

        x_loaded = [sem(f"x_loaded{i}") for i in range(2)]
        res_loaded = [sem(f"res_loaded{i}") for i in range(2)]
        stats_ready, x_pool = sem("stats_ready"), sem("x_pool")
        x_chain, x_rounded, xd_ready = sem("x_chain"), sem("x_rounded"), sem("xd_ready")
        xt_done, xt_hi, xt_lo = sem("xt_done"), sem("xt_hi"), sem("xt_lo")
        gate_done, up_done, silu_done = sem("gate_done"), sem("up_done"), sem("silu_done")
        h_chain, h_made, h_rounded, h_pool, hd_ready = (sem("h_chain"), sem("h_made"), sem("h_rounded"),
                                                        sem("h_pool"), sem("hd_ready"))
        ht_done, ht_hi, ht_lo = sem("ht_done"), sem("ht_hi"), sem("ht_lo")
        down_step, y_made = sem("down_step"), sem("y_made")
        stored = [sem(f"stored{i}") for i in range(2)]

        x2_t = x2.rearrange("(t p) e -> t p e", p=P)
        out_t = out.rearrange("(t p) e -> t p e", p=P)

        def tiles(eng, body):
            body(At(0, 0))
            body(At(0, 1))
            with eng.Fori(1, TILES // 2 - 1) as k:
                body(At(k, 0))
                body(At(k, 1))
            body(At(TILES // 2 - 1, 0))
            body(At(TILES // 2 - 1, 1))

        def early(t, n):
            return isinstance(t.n, int) and t.n < n

        def final(t):
            return isinstance(t.n, int) and t.n == TILES - 1

        with nc.Block() as block:
            @block.sync
            def _(sp):
                def load_x(t):
                    if not early(t, 2):
                        sp.wait_ge(x_rounded, t.n - 1)
                    sp.dma_start(x_in[t.par][:, :], x2_t[t.n]).then_inc(x_loaded[t.par], 16)

                def store(t):
                    sp.wait_ge(y_made, t.n + 1)
                    sp.dma_start(out_t[t.n], y[t.par][:, :]).then_inc(stored[t.par], 16)

                load_x(At(0, 0))

                def body(t):
                    if not final(t):
                        load_x(t.plus(1))
                    if not early(t, 2):
                        sp.wait_ge(y_made, t.n - 1)
                    sp.dma_start(x_res[t.par][:, :], x2_t[t.n]).then_inc(res_loaded[t.par], 16)
                    if not early(t, 1):
                        store(t.plus(-1))

                tiles(sp, body)
                store(At(TILES // 2 - 1, 1))
                for i in range(2):
                    sp.wait_ge(stored[i], 16 * (TILES // 2))

            @block.gpsimd
            def _(gp):
                chain = Chain(gp, x_pool, MOMENT_LINKS + 1)

                def rstd(t):
                    gp.wait_ge(stats_ready, t.n + 1)
                    chain.start(t.n)
                    moments(nc.gpsimd, chain.link, x_stats, x_mean[:, :], x_rstd[:, :], m_const, m_tmp)

                def x_dequant(t):
                    gp.wait_ge(x_rounded, t.n + 1)
                    chain.link(nc.gpsimd.tensor_tensor(x_work[:, :], x_work[:, :], x_magic[:, :], ALU.subtract))
                    nc.gpsimd.tensor_tensor(blocks(x_work[:, :]), blocks(x_work[:, :]),
                                            spread(x_scales[:, 0, :], MX_BLOCK), ALU.mult).then_inc(xd_ready, 1)

                def h_dequant(t, c):
                    s = t.n * CH + c
                    gp.wait_ge(h_rounded, s + 1)
                    w = h_work[c % 2]
                    nc.gpsimd.tensor_tensor(w[:, :], w[:, :], h_magic[c % 2][:, :], ALU.subtract).then_inc(h_pool, 1)
                    gp.wait_ge(h_pool, s + 1)
                    nc.gpsimd.tensor_tensor(blocks(w[:, :]), blocks(w[:, :]),
                                            spread(h_scales[c % 2][:, 0, :], MX_BLOCK), ALU.mult).then_inc(hd_ready, 1)

                rstd(At(0, 0))
                x_dequant(At(0, 0))

                def body(t):
                    for c in range(CH):
                        if c == 0 and not final(t):
                            rstd(t.plus(1))
                        h_dequant(t, c)
                        if c == 1 and not final(t):
                            x_dequant(t.plus(1))

                tiles(gp, body)

            @block.vector
            def _(v):
                x_links = Chain(v, x_chain, 1 + MX_ROUND_LINKS)
                h_links = Chain(v, h_chain, 1 + MX_ROUND_LINKS)

                def x_stats_of(t):
                    v.wait_ge(x_loaded[t.par], 16 * (t.half + 1))
                    nc.vector.bn_stats(x_stats[:, 0, :], x_in[t.par][:, :]).then_inc(stats_ready, 1)

                def x_round(t):
                    v.wait_ge(x_pool, (MOMENT_LINKS + 1) * t.n + MOMENT_LINKS)
                    x_links.start(t.n)
                    if not early(t, 1):
                        v.wait_ge(xt_done, t.n)
                    x_links.link(nc.vector.tensor_scalar(x_norm[:, :], x_in[t.par][:, :], x_mean[:, 0:1],
                                                         x_rstd[:, 0:1], ALU.subtract, ALU.mult))
                    mx_round_links(nc.vector, x_links.link, x_norm[:, :], x_scales[:, 0, :], x_scales[:, 1, :],
                                   x_work[:, :], x_magic[:, :], MX_EPS).then_inc(x_rounded, 1)

                def x_low(t):
                    v.wait_ge(xt_hi, t.n + 1)
                    nc.vector.tensor_tensor(xT[t.par][1][:, :, :], xt_ps[:, :].rearrange("p (a b) -> p a b", b=P),
                                            xT[t.par][0][:, :, :], ALU.subtract).then_inc(xt_lo, 1)

                def h_round(t, c):
                    s, i = t.n * CH + c, c % 2
                    v.wait_ge(up_done, s + 1)
                    v.wait_ge(silu_done, s + 1)
                    h_links.start(s)
                    link_h = nc.vector.tensor_tensor(h[i][:, :], u_ps[i][:, :], sg[i][:, :], ALU.mult)
                    h_links.link(link_h)
                    if not (early(t, 1) and c < 2):
                        v.wait_ge(ht_done, s - 1)
                    mx_round_links(nc.vector, h_links.link, h[i][:, :], h_scales[i][:, 0, :], h_scales[i][:, 1, :],
                                   h_work[i][:, :], h_magic[i][:, :], W_SCALE * MX_EPS).then_inc(h_rounded, 1)

                def h_low(t, c):
                    s, i = t.n * CH + c, c % 2
                    v.wait_ge(ht_hi, s + 1)
                    if not (early(t, 1) and c < 2):
                        v.wait_ge(down_step, s - 1)
                    nc.vector.tensor_tensor(hT[i][1][:, :, :], t_ps[:, :].rearrange("p (a b) -> p a b", b=P),
                                            hT[i][0][:, :, :], ALU.subtract).then_inc(ht_lo, 1)

                def y_of(t):
                    v.wait_ge(down_step, CH * t.n + CH)
                    v.wait_ge(res_loaded[t.par], 16 * (t.half + 1))
                    if not early(t, 2):
                        v.wait_ge(stored[t.par], 16 * t.half)
                    nc.vector.scalar_tensor_tensor(y[t.par][:, :], d_ps[t.par][:, :], W_SCALE ** -2, x_res[t.par][:, :],
                                                   ALU.mult, ALU.add).then_inc(y_made, 1)

                x_stats_of(At(0, 0))
                x_round(At(0, 0))
                x_low(At(0, 0))

                def body(t):
                    for c in range(CH):
                        if c == 0 and not final(t):
                            x_stats_of(t.plus(1))
                        if c == 1 and not final(t):
                            x_round(t.plus(1))
                        h_round(t, c)
                        if c >= 2:
                            h_low(t, c - 2)
                        elif not early(t, 1):
                            h_low(t.plus(-1), CH + c - 2)
                        if c == 2 and not early(t, 1):
                            y_of(t.plus(-1))
                        if c == 2 and not final(t):
                            x_low(t.plus(1))

                tiles(v, body)
                last = At(TILES // 2 - 1, 1)
                h_low(last, 2)
                h_low(last, 3)
                y_of(last)

            @block.scalar
            def _(act):
                def x_high(t):
                    act.wait_ge(xt_done, t.n + 1)
                    nc.scalar.activation(xT[t.par][0][:, :, :], xt_ps[:, :].rearrange("p (a b) -> p a b", b=P),
                                         ACT.Copy).then_inc(xt_hi, 1)

                def silu(t, c):
                    s, i = t.n * CH + c, c % 2
                    act.wait_ge(gate_done, s + 1)
                    if not (early(t, 1) and c < 2):
                        act.wait_ge(h_chain, (1 + MX_ROUND_LINKS) * (s - 2) + 1)
                    nc.scalar.activation(sg[i][:, :], g_ps[i][:, :], ACT.Silu, scale=1.0 / W_SCALE).then_inc(silu_done, 1)

                def h_high(t, c):
                    s, i = t.n * CH + c, c % 2
                    act.wait_ge(ht_done, s + 1)
                    if not (early(t, 1) and c < 2):
                        act.wait_ge(down_step, s - 1)
                    nc.scalar.activation(hT[i][0][:, :, :], t_ps[:, :].rearrange("p (a b) -> p a b", b=P),
                                         ACT.Copy).then_inc(ht_hi, 1)

                x_high(At(0, 0))

                def body(t):
                    for c in range(CH):
                        silu(t, c)
                        if c >= 2:
                            h_high(t, c - 2)
                        elif not early(t, 1):
                            h_high(t.plus(-1), CH + c - 2)
                        if c == 2 and not final(t):
                            x_high(t.plus(1))

                tiles(act, body)
                last = At(TILES // 2 - 1, 1)
                h_high(last, 2)
                h_high(last, 3)

            @block.tensor
            def _(pe):
                def x_transpose(t):
                    pe.wait_ge(xd_ready, t.n + 1)
                    if not early(t, 1):
                        pe.wait_ge(xt_lo, t.n)
                    for j in range(KC):
                        last = nc.tensor.transpose(xt_ps[:, P * j:P * j + P], x_work[:, P * j:P * j + P], ident[:, :])
                    last.then_inc(xt_done, 1)

                def three_products(dst, a_hi, a_lo, b_hi, b_lo, n, start=True, stop=True):
                    last = None
                    for j in range(n):
                        for i, (a, b) in enumerate(((a_hi, b_hi), (a_hi, b_lo), (a_lo, b_hi))):
                            last = nc.tensor.matmul(dst, a(j), b(j), start=start and j == 0 and i == 0,
                                                    stop=stop and j == n - 1 and i == 2)
                    return last

                def gate_up(t, c):
                    s, i = t.n * CH + c, c % 2
                    if c == 0:
                        pe.wait_ge(xt_lo, t.n + 1)
                    if not (early(t, 1) and c < 2):
                        pe.wait_ge(silu_done, s - 1)
                    x_hi, x_lo = (lambda j, z=z: xT[t.par][z][:, j, :] for z in range(2))
                    for base, dst, done in ((0, g_ps, gate_done), (FF, u_ps, up_done)):
                        if base and not (early(t, 1) and c < 2):
                            pe.wait_ge(h_chain, (1 + MX_ROUND_LINKS) * (s - 2) + 1)
                        lo = base + E * c
                        w_hi_, w_lo_ = (lambda j, z=z: wgu[z][:, j, lo:lo + E] for z in range(2))
                        three_products(dst[i][:, :], x_hi, x_lo, w_hi_, w_lo_, KC).then_inc(done, 1)

                def h_transpose(t, c):
                    s, i = t.n * CH + c, c % 2
                    pe.wait_ge(hd_ready, s + 1)
                    if not (early(t, 1) and c < 1):
                        pe.wait_ge(ht_lo, s)
                    for j in range(KC):
                        last = nc.tensor.transpose(t_ps[:, P * j:P * j + P], h_work[i][:, P * j:P * j + P], ident[:, :])
                    last.then_inc(ht_done, 1)

                def down(t, c):
                    s, i = t.n * CH + c, c % 2
                    pe.wait_ge(ht_lo, s + 1)
                    if c == 0 and not early(t, 2):
                        pe.wait_ge(y_made, t.n - 1)
                    h_hi, h_lo = (lambda j, z=z: hT[i][z][:, j, :] for z in range(2))
                    w_hi_, w_lo_ = (lambda j, z=z: wdn[z][:, KC * c + j, :] for z in range(2))
                    three_products(d_ps[t.par][:, :], h_hi, h_lo, w_hi_, w_lo_, KC, start=c == 0,
                                   stop=c == CH - 1).then_inc(down_step, 1)

                x_transpose(At(0, 0))

                def body(t):
                    for c in range(CH):
                        gate_up(t, c)
                        if c >= 2:
                            h_transpose(t, c - 2)
                        elif not early(t, 1):
                            h_transpose(t.plus(-1), CH + c - 2)
                        if c == 3:
                            down(t, 0)
                        elif not early(t, 1):
                            down(t.plus(-1), c + 1)
                        if c == 2 and not final(t):
                            x_transpose(t.plus(1))

                tiles(pe, body)
                last = At(TILES // 2 - 1, 1)
                down(last, 1)
                h_transpose(last, 2)
                down(last, 2)
                h_transpose(last, 3)
                down(last, 3)
def split_weights(nc, block, parts, loaded, hi_done, lo_done, fixed):
    @block.sync
    def _(sp):
        for loads, *_ in parts:
            for dst, src in loads:
                sp.dma_start(dst, src).then_inc(loaded, 16)

    @block.scalar
    def _(act):
        act.wait_ge(loaded, 16 * sum(len(p[0]) for p in parts))
        for _, src, hi, _ in parts:
            nc.scalar.activation(hi, src, ACT.Copy, scale=W_SCALE).then_inc(hi_done, 1)

    @block.vector
    def _(v):
        fixed()
        v.wait_ge(loaded, 16 * sum(len(p[0]) for p in parts))
        for n, (_, src, hi, lo) in enumerate(parts):
            v.wait_ge(hi_done, n + 1)
            nc.vector.scalar_tensor_tensor(lo, src, W_SCALE, hi, ALU.mult, ALU.subtract).then_inc(lo_done, 1)


def self_attention(nc, x, wq, bq, wk, bk, wv, bv, wo, bo, qk_scratch, x1, gate_w, up_w, kept):
    NQ = E // P
    NKV = KV_HEADS * D
    SLOTS = HEADS + KV_HEADS
    STACK = 96
    MAX_ROW = STACK
    S2 = W_SCALE ** 2
    PAIRS = KV_HEADS // 2
    MU = 2 * TT
    UNITS = KV_HEADS * MU
    LAST = KV_HEADS - 1

    with ExitStack() as ctx:
        sb = lambda name, shape, dt=F32: ctx.enter_context(nc.sbuf_tensor("a_" + name, shape, dt))
        ps = lambda name, n=512: ctx.enter_context(nc.psum_tensor("a_" + name, [P, n], F32))
        sem = lambda name: ctx.enter_context(nc.semaphore("a_" + name))
        two = lambda f, name, *a: [f(f"{name}{i}", *a) for i in range(2)]

        ones, ident = sb("ones", [P, P]), sb("ident", [P, P])
        w_qkv = two(sb, "w_qkv", [P, KC, E + 2 * NKV], F16)
        w_o = two(sb, "w_o", [P, PAIRS, E], F16)
        bias_qk = sb("bias_qk", [P, NQ + 1])
        bias_v, bias_o = sb("bias_v", [P, NKV]), sb("bias_o", [P, E])
        x_in = two(sb, "x_in", [P, TT, E])
        x_norm = sb("x_norm", [P, TT, E])
        stats, mean, rstd = sb("stats", [P, TT, 6]), sb("mean", [P, TT]), sb("rstd", [P, TT])
        m_const, m_tmp = sb("m_const", [P, len(MOMENT_CONSTANTS), TT]), sb("m_tmp", [P, 2, TT])
        xT = two(sb, "xT", [P, KC, SEQ], F16)
        qk = two(sb, "qk", [P, NQ + 1, SEQ], F16)
        stack = two(sb, "stack", [P, SLOTS, SEQ], F16)
        v_raw = sb("v_raw", [P, TT, NKV])
        v_ones = two(sb, "v_ones", [P, TT, KV_HEADS, 2 * D])
        row_max, max_row = sb("row_max", [P, P]), sb("max_row", [HEADS * TT, P], F16)
        prob = [two(sb, f"prob{g}", [P, GROUP * SEQ]) for g in range(2)]
        o_t, o_norm = sb("o_t", [P, 2, SEQ // 32, 32]), sb("o_norm", [P, SEQ // 32, 2, D])
        o_rec = sb("o_rec", [P, 2, SEQ // 32])
        att = sb("att", [P, PAIRS, SEQ])
        att16 = two(sb, "att16", [P, PAIRS, SEQ], F16)
        x_res = two(sb, "x_res", [P, TT, E])

        s_ps = two(ps, "s", 1024)
        m_ps = two(ps, "m")
        o_ps, c_ps = ps("o"), ps("c")

        ones_made, ident_ready = sem("ones_made"), sem("ident_ready")
        loaded, hi_done, lo_done, bias_loaded, bias_ready = (
            sem("w_loaded"), sem("w_hi"), sem("w_lo"), sem("bias_loaded"), sem("bias_ready"))
        fixed_ready = sem("fixed_ready")

        with ExitStack() as prep, nc.Block() as block:
            stage = prep.enter_context(nc.sbuf_tensor("a_stage", [P, KC, E + 2 * NKV], F32))
            stage_o = prep.enter_context(nc.sbuf_tensor("a_stage_o", [P, PAIRS, E], F32))
            rows = lambda w: w.rearrange("(c p) n -> p c n", p=P)
            wo_rows = wo.rearrange("(gp g2 j d) n -> j g2 d gp n", gp=PAIRS, g2=2, j=GROUP)
            wo_loads = [(stage_o[32 * j + D * g2:32 * j + D * g2 + D, :, :], wo_rows[j, g2])
                        for j in range(GROUP) for g2 in range(2)]
            def constants():
                moment_constants(nc.vector, m_const, fixed_ready)
                for st in stack:
                    nc.vector.memset(st[64:STACK, :, :].bitcast(U32), 0).then_inc(fixed_ready, 1)
                    nc.vector.memset(st[MAX_ROW:MAX_ROW + 1, HEADS:SLOTS, :], -S2).then_inc(fixed_ready, 1)
                nc.vector.memset(row_max[:, HEADS * TT:P], 0.0).then_inc(fixed_ready, 1)
                for t in v_ones:
                    nc.vector.memset(t[:, :, :, D:2 * D], 1.0).then_inc(fixed_ready, 1)

            split_weights(nc, block, [
                ([(stage[:, :, 0:E], rows(wq)), (stage[:, :, E:E + NKV], rows(wk)),
                  (stage[:, :, E + NKV:E + 2 * NKV], rows(wv))], stage[:, :, :], w_qkv[0][:, :, :], w_qkv[1][:, :, :]),
                (wo_loads, stage_o[:, :, :], w_o[0][:, :, :], w_o[1][:, :, :]),
            ], loaded, hi_done, lo_done, constants)

            @block.gpsimd
            def _(gp):
                gp.dma_start(bias_qk[:, 0:NQ], bq.rearrange("(c p) -> p c", p=P), allow_slow_non_contiguous=True).then_inc(bias_loaded, 16)
                gp.dma_start(bias_qk[:, NQ:NQ + 1], bk.rearrange("(c p) -> p c", p=P), allow_slow_non_contiguous=True).then_inc(bias_loaded, 16)
                gp.dma_start(bias_v[:, :], bv.rearrange("(o n) -> o n", o=1).to_broadcast([P, NKV])).then_inc(bias_loaded, 16)
                gp.dma_start(bias_o[:, :], bo.rearrange("(o n) -> o n", o=1).to_broadcast([P, E])).then_inc(bias_loaded, 16)
                identity_matrix(gp, ones, ident, ones_made, ident_ready)
                gp.wait_ge(bias_loaded, 64)
                nc.gpsimd.tensor_scalar(bias_qk[:, :], bias_qk[:, :], W_SCALE, None, ALU.mult).then_inc(bias_ready, 1)
                nc.gpsimd.tensor_scalar(bias_v[:, :], bias_v[:, :], W_SCALE, None, ALU.mult).then_inc(bias_ready, 1)

        x_loaded, res_loaded, stored = two(sem, "x_loaded"), two(sem, "res_loaded"), two(sem, "stored")
        stats_ready, m_chain, norm_ready, v_out = sem("stats_ready"), sem("m_chain"), sem("norm_ready"), sem("v_out")
        xt_done, xt_hi, xt_lo = sem("xt_done"), sem("xt_hi"), sem("xt_lo")
        q_done, v_done, qk_hi, qk_lo, v_ready = (
            sem("q_done"), sem("v_done"), sem("qk_hi"), sem("qk_lo"), sem("v_ready"))
        left, stacked = sem("left"), two(sem, "stacked")
        max_done, max_taken, max_t, max_cast, max_placed = (
            sem("max_done"), sem("max_taken"), sem("max_t"), sem("max_cast"), two(sem, "max_placed"))
        score_done, prob_ready, pv_done = sem("score_done"), sem("prob_ready"), sem("pv_done")
        o_chain, att_ready, att_hi, att_lo = sem("o_chain"), sem("att_ready"), sem("att_hi"), sem("att_lo")
        y_done, biased, y_added = sem("y_done"), sem("biased"), sem("y_added")
        O_LINKS = 3

        quantizers = [WeightQuantizer(nc, sb, sem, name, lambda n, w=w: w.rearrange("(n p) e -> n p e", p=P)[n],
                                      lambda n, i=i: kept[n + BATCH * i])
                      for i, (name, w) in enumerate((("gate", gate_w), ("up", up_w)))]

        xb = x.rearrange("b (t p) e -> b p t e", p=P)
        x1b = x1.rearrange("b (t p) e -> b p t e", p=P)

        known = lambda b: isinstance(b.n, int)
        early = lambda b, n: known(b) and b.n < n
        within = lambda b: not known(b) or b.n < BATCH

        def max_unit(step, slot):
            starts = (0, 0, 4, 10, 16, 22, 27, UNITS, UNITS)
            n = starts[step] + slot - (2 if step == 1 else 0)
            return n if starts[step] <= n < starts[step + 1] else None

        def batches(eng, body):
            body(At(0, 0))
            body(At(0, 1))
            with eng.Fori(1, BATCH // 2 - 2) as k:
                body(At(k, 0))
                body(At(k, 1))
            for k in (BATCH // 2 - 2, BATCH // 2 - 1):
                body(At(k, 0))
                body(At(k, 1))

        with nc.Block() as block:
            @block.sync
            def _(sp):
                def load_x(b):
                    if not early(b, 2):
                        sp.wait_ge(norm_ready, b.n - 1)
                    sp.dma_start(x_in[b.par][:, :, :], xb[b.n]).then_inc(x_loaded[b.par], 16)

                def leave(b):
                    sp.wait_ge(qk_lo, (NQ + 1) * (b.n + 1))
                    for z in range(2):
                        sp.dma_start(qk_scratch[b.n, z].rearrange("(c p) s -> p c s", p=P),
                                     qk[z][:, :, :]).then_inc(left, 16)

                def enter(b):
                    if early(b, 2):
                        sp.wait_ge(left, 32 * (b.n + 1))
                    else:
                        sp.wait_ge(score_done, TT * KV_HEADS * (b.n - 1))
                    st = stack[b.par]
                    src = [qk_scratch[b.n, z].rearrange("(h d) s -> d h s", d=D) for z in range(2)]
                    for row, q_half, k_half in ((0, 0, 0), (1, 1, 0), (2, 0, 1), (3, 1, 1)):
                        dst = st[D * row:D * row + D, :, :]
                        sp.dma_start(dst[:, 0:HEADS, :], src[q_half][:, 0:HEADS, :]).then_inc(stacked[b.par], 16)
                        sp.dma_start(dst[:, HEADS:SLOTS, :], src[k_half][:, HEADS:SLOTS, :]).then_inc(stacked[b.par], 16)

                def place_max(b):
                    sp.wait_ge(max_cast, b.n + 1)
                    dst = stack[b.par][MAX_ROW:MAX_ROW + 1, 0:HEADS, :]
                    sp.dma_start(dst.rearrange("o h (q t) -> o (h q) t", t=P),
                                 max_row[:, :]).then_inc(max_placed[b.par], 16)

                def load_res(b):
                    if not early(b, 2):
                        sp.wait_ge(stored[b.par], 16 * b.half)
                    sp.dma_start(x_res[b.par][:, :, :], xb[b.n]).then_inc(res_loaded[b.par], 16)

                def store(b):
                    sp.wait_ge(y_added, TT * (b.n + 1))
                    sp.dma_start(x1b[b.n], x_res[b.par][:, :, :]).then_inc(stored[b.par], 16)

                load_x(At(0, 0))
                load_x(At(0, 1))
                leave(At(0, 0))
                enter(At(0, 0))
                load_x(At(1, 0))
                leave(At(0, 1))
                enter(At(0, 1))
                load_x(At(1, 1))
                for z in quantizers:
                    z.load(sp, At(0, 0))
                place_max(At(0, 0))

                def body(b):
                    if within(b.plus(4)):
                        load_x(b.plus(4))
                    load_res(b)
                    if not early(b, 1):
                        for z in quantizers:
                            z.store(sp, b.plus(-1))
                    if within(b.plus(2)):
                        leave(b.plus(2))
                    if not early(b, 1):
                        store(b.plus(-1))
                    if within(b.plus(1)):
                        for z in quantizers:
                            z.load(sp, b.plus(1))
                    if within(b.plus(1)):
                        place_max(b.plus(1))
                    if within(b.plus(2)):
                        enter(b.plus(2))

                batches(sp, body)
                for z in quantizers:
                    z.store(sp, At(BATCH // 2 - 1, 1))
                    sp.wait_ge(z.stored, 16 * BATCH)
                store(At(BATCH // 2 - 1, 1))
                for i in range(2):
                    sp.wait_ge(stored[i], 16 * (BATCH // 2))

            @block.gpsimd
            def _(gp):
                chain = Chain(gp, m_chain, MOMENT_LINKS)

                def row_moments(b):
                    gp.wait_ge(stats_ready, TT * (b.n + 1))
                    chain.start(b.n)
                    moments(nc.gpsimd, chain.link, stats, mean[:, :], rstd[:, :], m_const, m_tmp)

                def add_bias(b):
                    gp.wait_ge(res_loaded[b.par], 16 * (b.half + 1))
                    r = x_res[b.par]
                    for t in range(TT):
                        nc.gpsimd.tensor_tensor(r[:, t, :], r[:, t, :], bias_o[:, :], ALU.add).then_inc(biased, 1)

                def low_att(b, p):
                    if p == 0 and not early(b, 1):
                        gp.wait_ge(y_done, TT * b.n)
                    gp.wait_ge(att_hi, PAIRS * b.n + p + 1)
                    nc.gpsimd.tensor_tensor(att16[1][:, p, :], att[:, p, :], att16[0][:, p, :],
                                            ALU.subtract).then_inc(att_lo, 1)

                def keep_v(b):
                    gp.wait_ge(v_out, b.n + 1)
                    if not early(b, 2):
                        gp.wait_ge(pv_done, KV_HEADS * (b.n - 1))
                    for t in range(TT):
                        nc.gpsimd.tensor_tensor(
                            v_ones[b.par][:, t, :, 0:D], v_raw[:, t, :].rearrange("p (g d) -> p g d", d=D),
                            bias_v[:, :].rearrange("p (g d) -> p g d", d=D), ALU.add).then_inc(v_ready, 1)

                row_moments(At(0, 0))
                keep_v(At(0, 0))
                row_moments(At(0, 1))
                keep_v(At(0, 1))
                row_moments(At(1, 0))

                def body(b):
                    if not early(b, 1) and within(b.plus(1)):
                        keep_v(b.plus(1))
                    if within(b.plus(3)):
                        row_moments(b.plus(3))
                    if not early(b, 1):
                        low_att(b.plus(-1), 2)
                        low_att(b.plus(-1), 3)
                    add_bias(b)
                    for z in quantizers:
                        z.divide(gp, b)
                    low_att(b, 0)
                    for z in quantizers:
                        z.round(gp, b)
                    low_att(b, 1)

                batches(gp, body)
                last = At(BATCH // 2 - 1, 1)
                low_att(last, 2)
                low_att(last, 3)

            @block.vector
            def _(v):
                def layernorm_stats(b):
                    v.wait_ge(x_loaded[b.par], 16 * (b.half + 1))
                    for t in range(TT):
                        nc.vector.bn_stats(stats[:, t, :], x_in[b.par][:, t, :]).then_inc(stats_ready, 1)

                def layernorm(b):
                    v.wait_ge(m_chain, MOMENT_LINKS * (b.n + 1))
                    if not early(b, 1):
                        v.wait_ge(xt_done, 2 * b.n)
                    for t in range(TT):
                        last = nc.vector.tensor_scalar(x_norm[:, t, :], x_in[b.par][:, t, :], mean[:, t:t + 1],
                                                       rstd[:, t:t + 1], ALU.subtract, ALU.mult)
                    last.then_inc(norm_ready, 1)

                def take_max(b, unit):
                    if unit is None or not within(b):
                        return
                    g, u = unit // MU, unit % MU
                    qt, pair = u // 2, u % 2
                    first = (GROUP * g + 2 * pair) * TT + qt
                    v.wait_ge(max_done, UNITS * b.n + unit + 1)
                    if unit == 0 and not early(b, 1):
                        v.wait_ge(max_t, b.n)
                    nc.vector.tensor_reduce(row_max[:, first:first + TT + 1:TT],
                                            m_ps[u % 2][:, :].rearrange("p (h k) -> p h k", h=2),
                                            AX.X, ALU.max).then_inc(max_taken, 1)

                def normalize(b, p, part):
                    done = O_LINKS * (PAIRS * b.n + p) + part
                    if part == 0:
                        v.wait_ge(pv_done, KV_HEADS * b.n + 2 * p + 2)
                        nc.vector.transpose(o_t[:, :, :, :].rearrange("p a b c -> p (a b c)"),
                                            o_ps[:, :]).then_inc(o_chain, 1)
                    elif part == 1:
                        v.wait_ge(o_chain, done)
                        nc.vector.reciprocal(o_rec[:, :, :], o_t[:, :, :, D]).then_inc(o_chain, 1)
                    elif part == 2:
                        v.wait_ge(o_chain, done)
                        nc.vector.tensor_tensor(
                            o_norm[:, :, :, :].rearrange("p b a d -> p a b d"), o_t[:, :, :, 0:D],
                            o_rec[:, :, :].rearrange("p a (b o) -> p a b o", o=1).to_broadcast([P, 2, SEQ // 32, D]),
                            ALU.mult).then_inc(o_chain, 1)
                    else:
                        v.wait_ge(o_chain, done)
                        if not early(b, 1):
                            v.wait_ge(att_lo, PAIRS * (b.n - 1) + p + 1)
                        nc.vector.transpose(att[:, p, :], o_norm[:, :, :, :].rearrange("p b a d -> p (b a d)")
                                            ).then_inc(att_ready, 1)

                def residual(b, t):
                    v.wait_ge(biased, TT * b.n + t + 1)
                    v.wait_ge(y_done, TT * b.n + t + 1)
                    r = x_res[b.par][:, t, :]
                    nc.vector.scalar_tensor_tensor(r, c_ps[:, :], W_SCALE ** -2, r, ALU.mult, ALU.add).then_inc(y_added, 1)

                def low_x(b, i):
                    v.wait_ge(xt_hi, 2 * b.n + i + 1)
                    nc.vector.tensor_tensor(xT[1][:, 2 * i:2 * i + 2, :], c_ps[:, :].rearrange("p (c s) -> p c s", s=SEQ),
                                            xT[0][:, 2 * i:2 * i + 2, :], ALU.subtract).then_inc(xt_lo, 1)

                def low_qk(b, c):
                    if c == 0 and not early(b, 1):
                        v.wait_ge(left, 32 * b.n)
                    if c < NQ:
                        v.wait_ge(qk_hi, (NQ + 1) * b.n + c // 2 * 2 + 2)
                    else:
                        v.wait_ge(v_out, b.n + 1)
                    nc.vector.scalar_tensor_tensor(qk[1][:, c, :], c_ps[:, SEQ * (c % 2):SEQ * (c % 2) + SEQ],
                                                   bias_qk[:, c:c + 1], qk[0][:, c, :], ALU.add,
                                                   ALU.subtract).then_inc(qk_lo, 1)

                def split(b):
                    low_x(b, 0)
                    low_x(b, 1)
                    for c in range(NQ + 1):
                        low_qk(b, c)

                def take_bank(b, g):
                    ahead, far = b.plus(2), b.plus(3)
                    if g in (0, 1) and within(ahead):
                        low_qk(ahead, 2 * g)
                        low_qk(ahead, 2 * g + 1)
                    if g == 2 and within(ahead):
                        low_qk(ahead, NQ)
                    if g in (3, 4) and not early(b, 1):
                        residual(b.plus(-1), g - 3)
                    if g in (6, 7) and within(far):
                        low_x(far, g - 6)

                for n in range(3):
                    layernorm_stats(At(n // 2, n % 2))
                    layernorm(At(n // 2, n % 2))
                    if n < 2:
                        split(At(0, n))
                    else:
                        low_x(At(1, 0), 0)
                        low_x(At(1, 0), 1)
                    if n == 0:
                        for unit in range(UNITS):
                            take_max(At(0, 0), unit)

                def body(b):
                    for g in range(KV_HEADS):
                        done = b if g >= 3 else b.plus(-1)
                        pair = (g - 3) // 2 % PAIRS
                        ready = g % 2 == 1 and not early(done, 0)
                        take_bank(b, g)
                        for slot in range(6):
                            if ready and slot < 4:
                                normalize(done, pair, slot)
                            take_max(b.plus(1), max_unit(g, slot))
                        if g == 0 and within(b.plus(3)):
                            layernorm_stats(b.plus(3))
                        if g == 0:
                            for z in quantizers:
                                z.scales(v, b)
                        if g in (4, 5):
                            quantizers[g - 4].magic(v, b)
                        if g == 3 and within(b.plus(3)):
                            layernorm(b.plus(3))

                batches(v, body)
                last = At(BATCH // 2 - 1, 1)
                for part in range(4):
                    normalize(last, PAIRS - 1, part)
                for t in range(TT):
                    residual(last, t)

            @block.scalar
            def _(act):
                def exponentials(b, g, kt):
                    s = 2 * (KV_HEADS * b.n + g) + kt
                    act.wait_ge(score_done, s + 1)
                    if kt == 0 and not (early(b, 1) and g < 2):
                        act.wait_ge(pv_done, KV_HEADS * b.n + g - 1)
                    nc.scalar.activation(prob[g % 2][kt][:, :], s_ps[kt][:, :], ACT.Exp,
                                             scale=D ** -0.5 / S2).then_inc(prob_ready, 1)

                def high_att(b, p):
                    act.wait_ge(att_ready, PAIRS * b.n + p + 1)
                    if p == 0 and not early(b, 1):
                        act.wait_ge(y_done, TT * b.n)
                    nc.scalar.activation(att16[0][:, p, :], att[:, p, :], ACT.Copy).then_inc(att_hi, 1)

                def cast_max(b):
                    act.wait_ge(max_t, b.n + 1)
                    if not early(b, 1) and within(b.plus(1)):
                        act.wait_ge(left, 32 * (b.n + 2))
                    if not early(b, 1):
                        prev = b.plus(-1)
                        act.wait_ge(max_placed[prev.par], 16 * (prev.half + 1))
                    nc.scalar.activation(max_row[:, :], m_ps[0][0:HEADS * TT, 0:P], ACT.Copy, scale=1.0 / S2).then_inc(max_cast, 1)

                def high_x(b, i):
                    act.wait_ge(xt_done, 2 * b.n + i + 1)
                    nc.scalar.activation(xT[0][:, 2 * i:2 * i + 2, :], c_ps[:, :].rearrange("p (c s) -> p c s", s=SEQ),
                                         ACT.Copy).then_inc(xt_hi, 1)

                def high_qk(b, c):
                    if c == 0 and not early(b, 1):
                        act.wait_ge(left, 32 * b.n)
                    if c < NQ:
                        act.wait_ge(q_done, 2 * b.n + c // 2 + 1)
                    else:
                        act.wait_ge(v_done, b.n + 1)
                    nc.scalar.activation(qk[0][:, c, :], c_ps[:, SEQ * (c % 2):SEQ * (c % 2) + SEQ], ACT.Identity,
                                         bias=bias_qk[:, c:c + 1]).then_inc(qk_hi, 1)

                def copy_v(b):
                    act.wait_ge(v_done, b.n + 1)
                    if not early(b, 1):
                        act.wait_ge(v_ready, TT * b.n)
                    nc.scalar.activation(v_raw[:, :, :], c_ps[:, SEQ:2 * SEQ].rearrange("p (t n) -> p t n", n=NKV),
                                         ACT.Copy).then_inc(v_out, 1)

                def high_parts(b):
                    high_x(b, 0)
                    high_x(b, 1)
                    for c in range(NQ + 1):
                        high_qk(b, c)
                    copy_v(b)

                high_parts(At(0, 0))
                cast_max(At(0, 0))
                high_parts(At(0, 1))
                high_x(At(1, 0), 0)
                high_x(At(1, 0), 1)
                high_qk(At(1, 0), 0)
                high_qk(At(1, 0), 1)

                def body(b):
                    ahead, far = b.plus(2), b.plus(3)
                    for g in range(KV_HEADS):
                        exponentials(b, g, 0)
                        if g == LAST and within(b.plus(1)):
                            cast_max(b.plus(1))
                        exponentials(b, g, 1)
                        if g in (0, 1) and not early(b, 1):
                            high_att(b.plus(-1), 2 + g)
                        if g == 0 and within(ahead):
                            high_qk(ahead, 2)
                            high_qk(ahead, 3)
                        if g == 1 and within(ahead):
                            high_qk(ahead, NQ)
                            copy_v(ahead)
                        if g in (4, 6):
                            high_att(b, (g - 4) // 2)
                        if g in (5, 6) and within(far):
                            high_x(far, g - 5)
                        if g == LAST and within(far):
                            high_qk(far, 0)
                            high_qk(far, 1)

                batches(act, body)
                last = At(BATCH // 2 - 1, 1)
                high_att(last, 2)
                high_att(last, 3)

            @block.tensor
            def _(pe):
                def products(dst, lhs, rhs, first, end, n):
                    for j in range(first, end):
                        for i, (a, b_) in enumerate(((0, 0), (0, 1), (1, 0))):
                            last = nc.tensor.matmul(dst, lhs(a, j), rhs(b_, j), start=j == 0 and i == 0,
                                                    stop=j == n - 1 and i == 2)
                    return last

                def transpose_x(b, i, c):
                    if i == 0 and c == 0:
                        pe.wait_ge(norm_ready, b.n + 1)
                        if not early(b, 1):
                            pe.wait_ge(qk_lo, (NQ + 1) * b.n)
                        if not early(b, 4):
                            pe.wait_ge(y_added, TT * (b.n - 3))
                    elif c == 0:
                        pe.wait_ge(xt_lo, 2 * b.n + i)
                    for t in range(TT):
                        last = nc.tensor.transpose(c_ps[:, SEQ * c + P * t:SEQ * c + P * t + P],
                                                   x_norm[:, t, P * (2 * i + c):P * (2 * i + c) + P], ident[:, :])
                    if c == 1:
                        last.then_inc(xt_done, 1)

                def project_qk(b, c):
                    if c == 0:
                        pe.wait_ge(xt_lo, 2 * (b.n + 1))
                    elif c % 2 == 0:
                        pe.wait_ge(qk_lo, (NQ + 1) * b.n + c)
                    last = products(c_ps[:, SEQ * (c % 2):SEQ * (c % 2) + SEQ],
                                    lambda z, j: w_qkv[z][:, j, P * c:P * c + P], lambda z, j: xT[z][:, j, :], 0, KC, KC)
                    if c % 2:
                        last.then_inc(q_done, 1)

                def project_v(b):
                    for t in range(TT):
                        last = products(c_ps[:, SEQ + NKV * t:SEQ + NKV * t + NKV],
                                        lambda z, j: xT[z][:, j, P * t:P * t + P],
                                        lambda z, j: w_qkv[z][:, j, E + NKV:E + 2 * NKV], 0, KC, KC)
                    last.then_inc(v_done, 1)

                def project(b):
                    for i in range(2):
                        transpose_x(b, i, 0)
                        transpose_x(b, i, 1)
                    for c in range(NQ + 1):
                        project_qk(b, c)
                    project_v(b)

                def max_scores(b, unit):
                    if unit is None or not within(b):
                        return
                    if unit == 0:
                        pe.wait_ge(stacked[b.par], 8 * 16 * (b.half + 1))
                        if not early(b, 1):
                            pe.wait_ge(max_cast, b.n)
                    st, g, u = stack[b.par], unit // MU, unit % MU
                    qt, pair = u // 2, u % 2
                    if not (early(b, 1) and unit < 2):
                        pe.wait_ge(max_taken, UNITS * b.n + unit - 1)
                    for e in range(2):
                        last = nc.tensor.matmul(m_ps[u % 2][:, SEQ * e:SEQ * e + SEQ],
                                                st[0:STACK, GROUP * g + 2 * pair + e, P * qt:P * qt + P],
                                                st[0:STACK, HEADS + g, :], start=True, stop=True)
                    last.then_inc(max_done, 1)

                def transpose_max(b):
                    pe.wait_ge(max_taken, UNITS * (b.n + 1))
                    nc.tensor.transpose(m_ps[0][:, 0:P], row_max[:, :], ident[:, :]).then_inc(max_t, 1)

                def scores(b, g, kt):
                    st = stack[b.par]
                    if g == 0 and kt == 0:
                        pe.wait_ge(max_placed[b.par], 16 * (b.half + 1))
                    s = 2 * (KV_HEADS * b.n + g) + kt
                    if not (early(b, 1) and g == 0):
                        pe.wait_ge(prob_ready, s - 1)
                    for pair in range(2):
                        h = GROUP * g + 2 * pair
                        last = nc.tensor.matmul(s_ps[kt][:, 512 * pair:512 * pair + 512],
                                                st[0:MAX_ROW + 1, HEADS + g, P * kt:P * kt + P],
                                                st[0:MAX_ROW + 1, h:h + 2, :], start=True, stop=True)
                    last.then_inc(score_done, 1)

                def weighted_values(b, g, kt):
                    if kt == 0:
                        if g == 0:
                            pe.wait_ge(v_ready, TT * (b.n + 1))
                        pe.wait_ge(prob_ready, 2 * (KV_HEADS * b.n + g) + 2)
                        if g % 2 == 0 and not (early(b, 1) and g == 0):
                            pe.wait_ge(o_chain, O_LINKS * (PAIRS * b.n + g // 2 - 1) + 1)
                    for j in range(GROUP):
                        last = nc.tensor.matmul(o_ps[32 * j:32 * j + 32, SEQ * (g % 2):SEQ * (g % 2) + SEQ],
                                                v_ones[b.par][:, kt, g, :],
                                                prob[g % 2][kt][:, SEQ * j:SEQ * j + SEQ],
                                                start=kt == 0, stop=kt == TT - 1)
                    if kt == TT - 1:
                        last.then_inc(pv_done, 1)

                def output(b, t, half):
                    if half == 0:
                        if t == 0:
                            pe.wait_ge(att_lo, PAIRS * (b.n + 1))
                            if within(b.plus(3)):
                                pe.wait_ge(qk_lo, (NQ + 1) * (b.n + 4))
                        else:
                            pe.wait_ge(y_added, TT * b.n + t)
                    last = products(c_ps[:, :], lambda z, j: att16[z][:, j, P * t:P * t + P],
                                    lambda z, j: w_o[z][:, j, :], 2 * half, 2 * half + 2, PAIRS)
                    if half == 1:
                        last.then_inc(y_done, 1)

                def fill_bank(b, g, half):
                    ahead, far = b.plus(2), b.plus(3)
                    if g == 0 and within(ahead):
                        project_qk(ahead, 2 + half)
                    if g == 1 and within(ahead):
                        if half == 0:
                            project_qk(ahead, NQ)
                        else:
                            project_v(ahead)
                    if g in (2, 3) and not early(b, 1):
                        output(b.plus(-1), g - 2, half)
                    if g in (5, 6) and within(far):
                        transpose_x(far, g - 5, half)
                    if g == LAST and within(far):
                        project_qk(far, half)

                project(At(0, 0))
                for unit in range(UNITS):
                    max_scores(At(0, 0), unit)
                transpose_max(At(0, 0))
                project(At(0, 1))
                for i in range(2):
                    for c in range(2):
                        transpose_x(At(1, 0), i, c)
                for c in range(2):
                    project_qk(At(1, 0), c)

                def body(b):
                    for g in range(KV_HEADS):
                        step = lambda slot: max_scores(b.plus(1), max_unit(g, slot))
                        prev = b if g else b.plus(-1)
                        scores(b, g, 0)
                        step(0)
                        scores(b, g, 1)
                        step(1)
                        if g == LAST and within(b.plus(1)):
                            transpose_max(b.plus(1))
                        if not early(prev, 0):
                            weighted_values(prev, (g - 1) % KV_HEADS, 0)
                        step(2)
                        if not early(prev, 0):
                            weighted_values(prev, (g - 1) % KV_HEADS, 1)
                        step(3)
                        fill_bank(b, g, 0)
                        step(4)
                        fill_bank(b, g, 1)
                        step(5)

                batches(pe, body)
                last = At(BATCH // 2 - 1, 1)
                for kt in range(TT):
                    weighted_values(last, LAST, kt)
                for t in range(TT):
                    for half in range(2):
                        output(last, t, half)
def cross_attention(nc, x1, context, gamma, xc_scratch, x2, down_w, kept):
    HPT = X_HEADS // TT
    KT = E // P
    SLOTS = 2 * X_HEADS
    STACK = 3 * X_D
    MAX_ROW = STACK
    UNITS = X_HEADS * KT
    LAST = X_HEADS - 1

    with ExitStack() as ctx:
        sb = lambda name, shape, dt=F32: ctx.enter_context(nc.sbuf_tensor("x_" + name, shape, dt))
        ps = lambda name, n=512: ctx.enter_context(nc.psum_tensor("x_" + name, [P, n], F32))
        sem = lambda name: ctx.enter_context(nc.semaphore("x_" + name))
        two = lambda f, name, *a: [f(f"{name}{i}", *a) for i in range(2)]

        ones, ident = sb("ones", [P, P]), sb("ident", [P, P])
        gam = sb("gam", [P, 1])
        x_in, c_in = two(sb, "x_in", [P, TT, E]), two(sb, "c_in", [P, TT, E])
        x_norm = sb("x_norm", [P, TT, E])
        stats, mean, rstd = sb("stats", [P, TT, 6]), sb("mean", [P, TT]), sb("rstd", [P, TT])
        m_const, m_tmp = sb("m_const", [P, len(MOMENT_CONSTANTS), TT]), sb("m_tmp", [P, 2, TT])
        x16, c16 = two(sb, "x16", [P, TT, E], F16), two(sb, "c16", [P, TT, E], F16)
        stack = two(sb, "stack", [P, SLOTS, E], F16)
        v_t = two(sb, "v_t", [P, KT, SEQ])
        row_max, max_row = sb("row_max", [P, X_HEADS * KT]), sb("max_row", [X_HEADS * KT, P], F16)
        prob = [[sb(f"prob{t}{j}", [P, KT, E]) for j in range(HPT)] for t in range(TT)]
        s_t, s_rec, s_inv = sb("s_t", [P, E // 32, 32]), sb("s_rec", [P, E // 32]), sb("s_inv", [P, E])
        o_gam, o_norm = sb("o_gam", [P, E]), sb("o_norm", [P, E])
        x_res = two(sb, "x_res", [P, TT, E])

        s_ps = two(ps, "s", 1024)
        m_ps = two(ps, "m")
        o_ps, r_ps = ps("o"), ps("r")

        ones_made, ident_ready, gam_loaded, fixed_ready = (
            sem("ones_made"), sem("ident_ready"), sem("gam_loaded"), sem("fixed_ready"))
        x_loaded, c_loaded = two(sem, "x_loaded"), two(sem, "c_loaded")
        res_loaded, stored = two(sem, "res_loaded"), two(sem, "stored")
        stats_ready, m_chain, norm_ready = sem("stats_ready"), sem("m_chain"), sem("norm_ready")
        x_hi, c_hi, split_ready = sem("x_hi"), sem("c_hi"), sem("split_ready")
        left, stacked = sem("left"), two(sem, "stacked")
        vt_done, vt_ready = sem("vt_done"), sem("vt_ready")
        max_done, max_taken, max_t, max_cast, max_placed = (
            sem("max_done"), sem("max_taken"), sem("max_t"), sem("max_cast"), two(sem, "max_placed"))
        score_done, prob_ready, pv_done = sem("score_done"), sem("prob_ready"), sem("pv_done")
        n_chain, o_taken, y_added = sem("n_chain"), sem("o_taken"), sem("y_added")
        N_LINKS = 4

        with nc.Block() as block:
            @block.sync
            def _(sp):
                sp.dma_start(gam[:, :], gamma.rearrange("(o n) -> o n", o=1).to_broadcast([P, 1]),
                             allow_slow_non_contiguous=True).then_inc(gam_loaded, 16)
                sp.wait_ge(gam_loaded, 16)

            @block.gpsimd
            def _(gp):
                identity_matrix(gp, ones, ident, ones_made, ident_ready)

            @block.vector
            def _(v):
                moment_constants(nc.vector, m_const, fixed_ready)
                for st in stack:
                    nc.vector.memset(st[MAX_ROW:MAX_ROW + 1, X_HEADS:SLOTS, :], -1.0).then_inc(fixed_ready, 1)

        quantizer = WeightQuantizer(nc, sb, sem, "down",
                                    lambda n: down_w.rearrange("(r p) (n e) -> n p r e", p=P, e=P)[n],
                                    lambda n: kept[n])

        tiled = lambda t: t.rearrange("b (t p) e -> b p t e", p=P)
        x1b, ctxb, x2b = tiled(x1), tiled(context), tiled(x2)

        known = lambda b: isinstance(b.n, int)
        early = lambda b, n: known(b) and b.n < n
        within = lambda b: not known(b) or b.n < BATCH

        def max_unit(step, slot):
            starts = (0, 0, 4, 10, 16, 22, 27, UNITS, UNITS)
            n = starts[step] + slot - (2 if step == 1 else 0)
            return n if starts[step] <= n < starts[step + 1] else None

        def batches(eng, body):
            body(At(0, 0))
            body(At(0, 1))
            with eng.Fori(1, BATCH // 2 - 2) as k:
                body(At(k, 0))
                body(At(k, 1))
            for k in (BATCH // 2 - 2, BATCH // 2 - 1):
                body(At(k, 0))
                body(At(k, 1))

        with nc.Block() as block:
            @block.sync
            def _(sp):
                def load(b):
                    if not early(b, 2):
                        sp.wait_ge(vt_done, 2 * (b.n - 1))
                    sp.dma_start(x_in[b.par][:, :, :], x1b[b.n]).then_inc(x_loaded[b.par], 16)
                    sp.dma_start(c_in[b.par][:, :, :], ctxb[b.n]).then_inc(c_loaded[b.par], 16)

                def leave(b):
                    sp.wait_ge(split_ready, 4 * (b.n + 1))
                    for w, pair in enumerate((x16, c16)):
                        for z in range(2):
                            sp.dma_start(xc_scratch[b.n, w, z].rearrange("(t p) e -> p t e", p=P),
                                         pair[z][:, :, :]).then_inc(left, 16)

                def enter(b):
                    if early(b, 2):
                        sp.wait_ge(left, 64 * (b.n + 1))
                    else:
                        sp.wait_ge(score_done, 2 * X_HEADS * (b.n - 1))
                    st = stack[b.par]
                    src = [[xc_scratch[b.n, w, z].rearrange("(h d) e -> d h e", d=X_D) for z in range(2)] for w in range(2)]
                    for row, x_half, c_half in ((0, 0, 0), (1, 1, 0), (2, 0, 1)):
                        dst = st[X_D * row:X_D * row + X_D, :, :]
                        sp.dma_start(dst[:, 0:X_HEADS, :], src[0][x_half]).then_inc(stacked[b.par], 16)
                        sp.dma_start(dst[:, X_HEADS:SLOTS, :], src[1][c_half]).then_inc(stacked[b.par], 16)

                def place_max(b):
                    sp.wait_ge(max_cast, b.n + 1)
                    dst = stack[b.par][MAX_ROW:MAX_ROW + 1, 0:X_HEADS, :]
                    sp.dma_start(dst.rearrange("o h (q t) -> o (h q) t", t=P),
                                 max_row[:, :]).then_inc(max_placed[b.par], 16)

                def load_res(b):
                    if not early(b, 2):
                        sp.wait_ge(stored[b.par], 16 * b.half)
                    sp.dma_start(x_res[b.par][:, :, :], x1b[b.n]).then_inc(res_loaded[b.par], 16)

                def store(b):
                    sp.wait_ge(y_added, TT * (b.n + 1))
                    sp.dma_start(x2b[b.n], x_res[b.par][:, :, :]).then_inc(stored[b.par], 16)

                load(At(0, 0))
                load(At(0, 1))
                leave(At(0, 0))
                enter(At(0, 0))
                leave(At(0, 1))
                enter(At(0, 1))
                quantizer.load(sp, At(0, 0))
                place_max(At(0, 0))

                def body(b):
                    if within(b.plus(2)):
                        load(b.plus(2))
                    load_res(b)
                    if not early(b, 1):
                        quantizer.store(sp, b.plus(-1))
                        store(b.plus(-1))
                    if within(b.plus(1)):
                        quantizer.load(sp, b.plus(1))
                    if within(b.plus(2)):
                        leave(b.plus(2))
                    if within(b.plus(1)):
                        place_max(b.plus(1))
                    if within(b.plus(2)):
                        enter(b.plus(2))

                batches(sp, body)
                quantizer.store(sp, At(BATCH // 2 - 1, 1))
                sp.wait_ge(quantizer.stored, 16 * BATCH)
                store(At(BATCH // 2 - 1, 1))
                for i in range(2):
                    sp.wait_ge(stored[i], 16 * (BATCH // 2))

            @block.gpsimd
            def _(gp):
                chain = Chain(gp, m_chain, MOMENT_LINKS)

                def row_moments(b):
                    gp.wait_ge(stats_ready, TT * (b.n + 1))
                    chain.start(b.n)
                    moments(nc.gpsimd, chain.link, stats, mean[:, :], rstd[:, :], m_const, m_tmp)

                def low_parts(b, src, pair, hi):
                    gp.wait_ge(hi, b.n + 1)
                    for t in range(TT):
                        nc.gpsimd.tensor_tensor(pair[1][:, t, :], src[:, t, :], pair[0][:, t, :],
                                                ALU.subtract).then_inc(split_ready, 1)

                def add(b, t):
                    gp.wait_ge(n_chain, N_LINKS * (TT * b.n + t + 1))
                    if t == 0:
                        gp.wait_ge(res_loaded[b.par], 16 * (b.half + 1))
                    r = x_res[b.par][:, t, :]
                    nc.gpsimd.tensor_tensor(r, o_norm[:, :], r, ALU.add).then_inc(y_added, 1)

                for n in range(2):
                    row_moments(At(0, n))
                    low_parts(At(0, n), c_in[n], c16, c_hi)
                    low_parts(At(0, n), x_norm, x16, x_hi)

                def body(b):
                    ahead = b.plus(2)
                    if not early(b, 1):
                        add(b.plus(-1), 0)
                    if within(ahead):
                        row_moments(ahead)
                        low_parts(ahead, c_in[b.par], c16, c_hi)
                    quantizer.divide(gp, b)
                    if not early(b, 1):
                        add(b.plus(-1), 1)
                    if within(ahead):
                        low_parts(ahead, x_norm, x16, x_hi)
                    quantizer.round(gp, b)

                batches(gp, body)
                for t in range(TT):
                    add(At(BATCH // 2 - 1, 1), t)

            @block.vector
            def _(v):
                def layernorm_stats(b):
                    v.wait_ge(x_loaded[b.par], 16 * (b.half + 1))
                    for t in range(TT):
                        nc.vector.bn_stats(stats[:, t, :], x_in[b.par][:, t, :]).then_inc(stats_ready, 1)

                def layernorm(b):
                    v.wait_ge(m_chain, MOMENT_LINKS * (b.n + 1))
                    if not early(b, 1):
                        v.wait_ge(split_ready, 4 * b.n)
                    for t in range(TT):
                        last = nc.vector.tensor_scalar(x_norm[:, t, :], x_in[b.par][:, t, :], mean[:, t:t + 1],
                                                       rstd[:, t:t + 1], ALU.subtract, ALU.mult)
                    last.then_inc(norm_ready, 1)

                def take_max(b, unit):
                    if unit is None or not within(b):
                        return
                    h, qt = unit // KT, unit % KT
                    v.wait_ge(max_done, UNITS * b.n + unit + 1)
                    if unit == 0 and not early(b, 1):
                        v.wait_ge(max_t, b.n)
                    nc.vector.tensor_reduce(row_max[:, KT * h + qt:KT * h + qt + 1], m_ps[qt % 2][:, :],
                                            AX.X, ALU.max).then_inc(max_taken, 1)

                def normalize(b, t, part):
                    n = TT * b.n + t
                    if part == 0:
                        v.wait_ge(pv_done, n + 1)
                        nc.vector.transpose(s_t[:, :, :].rearrange("p a c -> p (a c)"), r_ps[:, :]).then_inc(n_chain, 1)
                    elif part == 1:
                        v.wait_ge(n_chain, N_LINKS * n + 1)
                        nc.vector.reciprocal(s_rec[:, :], s_t[:, :, 0]).then_inc(n_chain, 1)
                    elif part == 2:
                        v.wait_ge(n_chain, N_LINKS * n + 2)
                        nc.vector.transpose(s_inv[:, :], spread(s_rec[:, :], 32)).then_inc(n_chain, 1)
                    else:
                        v.wait_ge(n_chain, N_LINKS * n + 3)
                        v.wait_ge(o_taken, n + 1)
                        if not (early(b, 1) and t == 0):
                            v.wait_ge(y_added, n)
                        nc.vector.tensor_tensor(o_norm[:, :], o_gam[:, :], s_inv[:, :], ALU.mult).then_inc(n_chain, 1)

                for n in range(2):
                    layernorm_stats(At(0, n))
                    layernorm(At(0, n))
                for unit in range(UNITS):
                    take_max(At(0, 0), unit)

                def body(b):
                    for h in range(X_HEADS):
                        for slot in range(6):
                            if h in (0, 4) and slot < 4 and not early(b, 1):
                                normalize(b.plus(-1), h // 4, slot)
                            take_max(b.plus(1), max_unit(h, slot))
                        if h == 0:
                            quantizer.scales(v, b)
                        if h == 5:
                            quantizer.magic(v, b)
                        if h == 1 and within(b.plus(2)):
                            layernorm_stats(b.plus(2))
                        if h == 3 and within(b.plus(2)):
                            layernorm(b.plus(2))

                batches(v, body)
                for t in range(TT):
                    for part in range(N_LINKS):
                        normalize(At(BATCH // 2 - 1, 1), t, part)

            @block.scalar
            def _(act):
                def exponentials(b, h, u):
                    s = 2 * (X_HEADS * b.n + h) + u
                    act.wait_ge(score_done, s + 1)
                    if h % HPT == 0 and u == 0 and not early(b, 1):
                        act.wait_ge(pv_done, TT * (b.n - 1) + h // HPT + 1)
                    nc.scalar.activation(prob[h // HPT][h % HPT][:, 2 * u:2 * u + 2, :],
                                         s_ps[u][:, :].rearrange("p (k q) -> p k q", k=2), ACT.Exp,
                                         scale=X_D ** -0.5).then_inc(prob_ready, 1)

                def take_o(b, t):
                    n = TT * b.n + t
                    act.wait_ge(pv_done, n + 1)
                    if not (early(b, 1) and t == 0):
                        act.wait_ge(n_chain, N_LINKS * n)
                    nc.scalar.activation(o_gam[:, :], o_ps[:, :], ACT.Copy, scale=gam[:, 0:1]).then_inc(o_taken, 1)

                def cast_max(b):
                    act.wait_ge(max_t, b.n + 1)
                    if not early(b, 1) and within(b.plus(1)):
                        act.wait_ge(left, 64 * (b.n + 2))
                    if not early(b, 1):
                        prev = b.plus(-1)
                        act.wait_ge(max_placed[prev.par], 16 * (prev.half + 1))
                    nc.scalar.activation(max_row[:, :], m_ps[0][0:X_HEADS * KT, 0:P], ACT.Copy).then_inc(max_cast, 1)

                def high_context(b):
                    if not early(b, 1):
                        act.wait_ge(left, 64 * b.n)
                    act.wait_ge(c_loaded[b.par], 16 * (b.half + 1))
                    nc.scalar.activation(c16[0][:, :, :], c_in[b.par][:, :, :], ACT.Copy).then_inc(c_hi, 1)

                def high_tokens(b):
                    act.wait_ge(norm_ready, b.n + 1)
                    nc.scalar.activation(x16[0][:, :, :], x_norm[:, :, :], ACT.Copy).then_inc(x_hi, 1)

                def keep_vt(b, i):
                    if i == 1 and not early(b, 2):
                        act.wait_ge(pv_done, TT * (b.n - 1))
                    act.wait_ge(vt_done, 2 * b.n + 2 - i)
                    nc.scalar.activation(v_t[b.par][:, 2 * i:2 * i + 2, :], m_ps[i][:, :].rearrange("p (k s) -> p k s", s=SEQ),
                                         ACT.Copy).then_inc(vt_ready, 1)

                high_context(At(0, 0))
                high_tokens(At(0, 0))
                high_context(At(0, 1))
                high_tokens(At(0, 1))
                keep_vt(At(0, 0), 1)
                keep_vt(At(0, 0), 0)
                cast_max(At(0, 0))

                def body(b):
                    for h in range(X_HEADS):
                        if h in (0, 4) and not early(b, 1):
                            take_o(b.plus(-1), h // 4)
                        exponentials(b, h, 0)
                        if h == LAST and within(b.plus(1)):
                            cast_max(b.plus(1))
                        exponentials(b, h, 1)
                        if h == LAST and within(b.plus(1)):
                            keep_vt(b.plus(1), 1)
                        if h == 0 and not early(b, 1):
                            keep_vt(b, 0)
                        if h == 2 and within(b.plus(2)):
                            high_context(b.plus(2))
                        if h == 4 and within(b.plus(2)):
                            high_tokens(b.plus(2))

                batches(act, body)
                for t in range(TT):
                    take_o(At(BATCH // 2 - 1, 1), t)

            @block.tensor
            def _(pe):
                def transpose_context(b, i):
                    if i == 1:
                        pe.wait_ge(c_loaded[b.par], 16 * (b.half + 1))
                    if not early(b, 1):
                        if i == 1:
                            pe.wait_ge(max_taken, UNITS * (b.n + 1))
                        else:
                            pe.wait_ge(max_cast, b.n + 1)
                    for k in range(2):
                        for t in range(TT):
                            last = nc.tensor.transpose(m_ps[i][:, SEQ * k + P * t:SEQ * k + P * t + P],
                                                       c_in[b.par][:, t, P * (2 * i + k):P * (2 * i + k) + P], ident[:, :])
                    last.then_inc(vt_done, 1)

                def max_scores(b, unit):
                    if unit is None or not within(b):
                        return
                    if unit == 0:
                        pe.wait_ge(stacked[b.par], 6 * 16 * (b.half + 1))
                        pe.wait_ge(vt_ready, 2 * (b.n if not early(b, 1) else 1))
                    st, h, qt = stack[b.par], unit // KT, unit % KT
                    if not (early(b, 1) and unit < 2):
                        pe.wait_ge(max_taken, UNITS * b.n + unit - 1)
                    nc.tensor.matmul(m_ps[qt % 2][:, :], st[0:STACK, h, P * qt:P * qt + P],
                                     st[0:STACK, X_HEADS + h, :], start=True, stop=True).then_inc(max_done, 1)

                def transpose_max(b):
                    pe.wait_ge(max_taken, UNITS * (b.n + 1))
                    nc.tensor.transpose(m_ps[0][0:X_HEADS * KT, 0:P], row_max[:, :], ident[:, :]).then_inc(max_t, 1)

                def scores(b, h, u):
                    st = stack[b.par]
                    if h == 0 and u == 0:
                        pe.wait_ge(max_placed[b.par], 16 * (b.half + 1))
                    s = 2 * (X_HEADS * b.n + h) + u
                    if not (early(b, 1) and h == 0):
                        pe.wait_ge(prob_ready, s - 1)
                    for k in range(2):
                        kt = 2 * u + k
                        last = nc.tensor.matmul(s_ps[u][:, E * k:E * k + E],
                                                st[0:MAX_ROW + 1, X_HEADS + h, P * kt:P * kt + P],
                                                st[0:MAX_ROW + 1, h, :], start=True, stop=True)
                    last.then_inc(score_done, 1)

                def weighted_values(b, t, kt, summed):
                    n = TT * b.n + t
                    if kt == 0 and not summed:
                        pe.wait_ge(prob_ready, 2 * (X_HEADS * b.n + HPT * (t + 1)))
                        pe.wait_ge(vt_ready, 2 * (b.n + 1))
                        if not (early(b, 1) and t == 0):
                            pe.wait_ge(o_taken, n)
                    if kt == 0 and summed and not (early(b, 1) and t == 0):
                        pe.wait_ge(n_chain, N_LINKS * (n - 1) + 1)
                    for j in range(HPT):
                        row = X_D * (HPT * t + j)
                        lhs = ones[:, 0:X_D] if summed else v_t[b.par][:, kt, row:row + X_D]
                        last = nc.tensor.matmul((r_ps if summed else o_ps)[X_D * j:X_D * j + X_D, :], lhs,
                                                prob[t][j][:, kt, :], start=kt == 0, stop=kt == KT - 1)
                    if kt == KT - 1 and summed:
                        last.then_inc(pv_done, 1)

                transpose_context(At(0, 0), 1)
                transpose_context(At(0, 0), 0)
                for unit in range(UNITS):
                    max_scores(At(0, 0), unit)
                transpose_max(At(0, 0))

                def body(b):
                    for h in range(X_HEADS):
                        step = lambda slot: max_scores(b.plus(1), max_unit(h, slot))
                        owner, t = (b.plus(-1), 1) if h < HPT else (b, 0)
                        weighted = not early(owner, 0)
                        scores(b, h, 0)
                        step(0)
                        scores(b, h, 1)
                        step(1)
                        if h == 0 and not early(b, 1):
                            transpose_context(b, 0)
                        if h == LAST and within(b.plus(1)):
                            transpose_max(b.plus(1))
                        if weighted:
                            weighted_values(owner, t, h % HPT, False)
                        step(2)
                        if h == LAST and within(b.plus(1)):
                            transpose_context(b.plus(1), 1)
                        step(3)
                        if weighted:
                            weighted_values(owner, t, h % HPT, True)
                        step(4)
                        step(5)

                batches(pe, body)
                for kt in range(KT):
                    for summed in (False, True):
                        weighted_values(At(BATCH // 2 - 1, 1), 1, kt, summed)
def decoder_block(nc, x, context, wq, bq, wk, bk, wv, bv, wo, bo, gamma, gate_w, up_w, down_w, out):
    scratch = lambda name, shape, dt=F32: nc.dram_tensor(name, shape, dt, kind="Internal").ap()
    x1, x2 = scratch("x1", (BATCH, SEQ, E)), scratch("x2", (BATCH, SEQ, E))
    qk = scratch("qk_halves", (BATCH, 2, E + KV_HEADS * D, SEQ), F16)
    xc = scratch("xc_halves", (BATCH, 2, 2, SEQ, E), F16)
    weights = scratch("weights", (3 * FF // P, P, E))
    gate_up = 2 * FF // P
    self_attention(nc, x, wq, bq, wk, bk, wv, bv, wo, bo, qk, x1, gate_w, up_w, weights[0:gate_up])
    cross_attention(nc, x1, context, gamma, xc, x2, down_w, weights[gate_up:])
    rows = lambda t: t.rearrange("b s e -> (b s) e")
    feed_forward(nc, rows(x2), weights, rows(out))


_INS = ["x", "ctx_2048", "L0_attn_Wq", "L0_attn_bq", "L0_attn_Wk", "L0_attn_bk", "L0_attn_Wv", "L0_attn_bv",
        "L0_attn_Wo", "L0_attn_bo", "L0_xattn_gamma", "L0_ffn_gate_w", "L0_ffn_up_w", "L0_ffn_down_w"]


def kernel(**inputs):
    import numpy as _np
    import concourse.bacc as _bacc
    from concourse.bass_utils import run_bass_kernel_spmd as _run

    nc = _bacc.Bacc("TRN2", target_bir_lowering=False, num_devices=1)
    arrays, args = {}, []
    for name in _INS:
        a = _np.ascontiguousarray(inputs[name])
        if a.ndim == 0:
            a = a.reshape(1)
        arrays[f"in_{name}_dram"] = a
        args.append(nc.dram_tensor(f"in_{name}_dram", a.shape, mybir.dt.from_np(a.dtype), kind="ExternalInput").ap())
    args.append(nc.dram_tensor("out_0_dram", (BATCH, SEQ, E), F32, kind="ExternalOutput").ap())
    decoder_block(nc, *args)
    r = _run(nc, [arrays], core_ids=[0])
    return r.results[0]["out_0_dram"]
```

```python
from contextlib import ExitStack

import concourse.bass as bass
from concourse import mybir

F32 = mybir.dt.float32
F16 = mybir.dt.float16
U32 = mybir.dt.uint32
ALU = mybir.AluOpType
ACT = mybir.ActivationFunctionType
AX = mybir.AxisListType

P = 128
BATCH, SEQ, E = 16, 256, 512
KC = E // P
TT = SEQ // P
HEADS, KV_HEADS, D = 32, 8, 16
GROUP = HEADS // KV_HEADS
X_HEADS, X_D = 8, 32
FF = 2048
LN_EPS = 1e-5
W_SCALE = 64.0
BANKS = 3
LAST_USE = [max(n for n in range(32) if n % BANKS == i) - 32 for i in range(BANKS)]
MX_BLOCK, MX_MAX, MX_EPS = 32, 448.0, 1e-30
FP8_MIN_EXP = 2.0 ** -6
EXP_MASK = 0x7F800000
HALF_BIT = 0x00400000
MX_SHIFT = 2.0 ** 20


class At:

    def __init__(self, k, off):
        self.k, self.off = k, off
        self.n = k * 2 + off
        self.par = off % 2
        self.half = k + off // 2

    def plus(self, m):
        return At(self.k, self.off + m)


class Chain:

    def __init__(self, eng, sem, per):
        self.eng, self.sem, self.per = eng, sem, per
        self.base, self.count = 0, 0

    def start(self, n):
        assert self.count in (0, self.per), (self.count, self.per)
        self.base, self.count = n * self.per, 0

    def link(self, ins):
        self.count += 1
        ins.then_inc(self.sem, 1)
        self.eng.wait_ge(self.sem, self.base + self.count)


def identity_matrix(gp, ones, ident, made, ready):
    gp.memset(ones[:, :], 1.0).then_inc(made, 1)
    gp.wait_ge(made, 1)
    gp.affine_select(ident[:, :], ones[:, :], pattern=[[-1, P]], compare_op=ALU.is_equal, fill=0.0,
                     base=0, channel_multiplier=1).then_inc(ready, 1)


MOMENT_CONSTANTS = (0.5, 1.0 / E, 0.25, LN_EPS, -0.5, 1.5)
MOMENT_LINKS = 10 + 5 * 2


def moment_constants(v, tile, done):
    for i, value in enumerate(MOMENT_CONSTANTS):
        v.memset(tile[:, i, :], value).then_inc(done, 1)


def moments(gp, link, stats, mean, rstd, const, t):
    half, inv_e, quarter, eps, neg_half, three_halves = (const[:, i, :] for i in range(6))
    op = gp.tensor_tensor
    link(op(mean, stats[:, :, 1], stats[:, :, 4], ALU.add))
    link(op(mean, mean, half, ALU.mult))
    link(op(t[:, 0], stats[:, :, 1], stats[:, :, 4], ALU.subtract))
    link(op(t[:, 0], t[:, 0], t[:, 0], ALU.mult))
    link(op(t[:, 0], t[:, 0], quarter, ALU.mult))
    link(op(t[:, 1], stats[:, :, 2], stats[:, :, 5], ALU.add))
    link(op(t[:, 1], t[:, 1], inv_e, ALU.mult))
    link(op(t[:, 0], t[:, 0], t[:, 1], ALU.add))
    link(op(t[:, 0], t[:, 0], eps, ALU.add))
    link(op(rstd, t[:, 0], neg_half, ALU.pow))
    for _ in range(2):
        link(op(t[:, 1], rstd, rstd, ALU.mult))
        link(op(t[:, 1], t[:, 1], t[:, 0], ALU.mult))
        link(op(t[:, 1], t[:, 1], half, ALU.mult))
        link(op(t[:, 1], three_halves, t[:, 1], ALU.subtract))
        link(op(rstd, rstd, t[:, 1], ALU.mult))


def blocks(ap):
    return ap.rearrange("p (a b) -> p a b", b=MX_BLOCK)


def spread(ap, n):
    return ap.rearrange("p (a o) -> p a o", o=1).to_broadcast([ap.shape[0], ap.shape[1], n])


def mx_round_links(v, link, src, scale, rscale, work, magic, eps):
    link(v.tensor_reduce(scale, blocks(src), AX.X, ALU.max, apply_absolute_value=True))
    link(v.tensor_scalar(scale, scale, 1.0 / MX_MAX, eps, ALU.mult, ALU.max))
    link(v.reciprocal(rscale, scale))
    link(v.tensor_tensor(blocks(work), blocks(src), spread(rscale, MX_BLOCK), ALU.mult))
    link(v.tensor_scalar(magic.bitcast(U32), work.bitcast(U32), EXP_MASK, HALF_BIT, ALU.bitwise_and,
                         ALU.bitwise_or))
    link(v.tensor_scalar(magic, magic, 1.5 * FP8_MIN_EXP, MX_SHIFT, ALU.max, ALU.mult))
    return v.tensor_tensor(work, work, magic, ALU.add)


MX_ROUND_LINKS = 6


class WeightQuantizer:

    def __init__(self, nc, sb, sem, name, piece, kept):
        self.nc, self.piece, self.kept = nc, piece, kept
        tile = lambda what, shape: sb(f"{name}_{what}", shape)
        self.src, self.work, self.magic_t = tile("in", [P, E]), tile("work", [P, E]), tile("magic", [P, E])
        self.scale, self.inverse = tile("scale", [P, E // MX_BLOCK]), tile("inverse", [P, E // MX_BLOCK])
        self.scaled_up = [tile(f"scaled_up{i}", [P, E // MX_BLOCK]) for i in range(2)]
        self.loaded, self.scaled, self.divided, self.magic_ready, self.quantized, self.stored = (
            sem(f"{name}_{what}") for what in ("loaded", "scaled", "divided", "magic_ready", "quantized", "stored"))
        self.v_chain, self.gp_chain = sem(f"{name}_v_chain"), sem(f"{name}_gp_chain")

    def load(self, sp, b):
        if not (isinstance(b.n, int) and b.n < 1):
            sp.wait_ge(self.divided, b.n)
        dst, src = self.src[:, :], self.piece(b.n)
        if len(src.shape) == 3:
            dst = dst.rearrange("p (r e) -> p r e", r=src.shape[1])
        sp.dma_start(dst, src).then_inc(self.loaded, 16)

    def scales(self, v, b):
        ops, scale, first = self.nc.vector, self.scale[:, :], 3 * b.n
        v.wait_ge(self.loaded, 16 * (b.n + 1))
        if not (isinstance(b.n, int) and b.n < 1):
            v.wait_ge(self.divided, b.n)
        if not (isinstance(b.n, int) and b.n < 2):
            v.wait_ge(self.quantized, b.n - 1)
        ops.tensor_reduce(scale, blocks(self.src[:, :]), AX.X, ALU.max,
                          apply_absolute_value=True).then_inc(self.v_chain, 1)
        v.wait_ge(self.v_chain, first + 1)
        ops.tensor_scalar(scale, scale, 1.0 / MX_MAX, MX_EPS, ALU.mult, ALU.max).then_inc(self.v_chain, 1)
        v.wait_ge(self.v_chain, first + 2)
        ops.reciprocal(self.inverse[:, :], scale).then_inc(self.scaled, 1)
        ops.tensor_scalar(self.scaled_up[b.par][:, :], scale, W_SCALE, None, ALU.mult).then_inc(self.scaled, 1)

    def divide(self, gp, b):
        gp.wait_ge(self.scaled, 2 * (b.n + 1))
        if not (isinstance(b.n, int) and b.n < 1):
            gp.wait_ge(self.stored, 16 * b.n)
        self.nc.gpsimd.tensor_tensor(blocks(self.work[:, :]), blocks(self.src[:, :]),
                                     spread(self.inverse[:, :], MX_BLOCK), ALU.mult).then_inc(self.divided, 1)

    def magic(self, v, b):
        magic, work = self.magic_t[:, :], self.work[:, :]
        v.wait_ge(self.divided, b.n + 1)
        self.nc.vector.tensor_scalar(magic.bitcast(U32), work.bitcast(U32), EXP_MASK, HALF_BIT, ALU.bitwise_and,
                                     ALU.bitwise_or).then_inc(self.v_chain, 1)
        v.wait_ge(self.v_chain, 3 * b.n + 3)
        self.nc.vector.tensor_scalar(magic, magic, 1.5 * FP8_MIN_EXP, MX_SHIFT, ALU.max,
                                     ALU.mult).then_inc(self.magic_ready, 1)

    def round(self, gp, b):
        ops, magic, work = self.nc.gpsimd, self.magic_t[:, :], self.work[:, :]
        gp.wait_ge(self.magic_ready, b.n + 1)
        ops.tensor_tensor(work, work, magic, ALU.add).then_inc(self.gp_chain, 1)
        gp.wait_ge(self.gp_chain, 2 * b.n + 1)
        ops.tensor_tensor(work, work, magic, ALU.subtract).then_inc(self.gp_chain, 1)
        gp.wait_ge(self.gp_chain, 2 * b.n + 2)
        ops.tensor_tensor(blocks(work), blocks(work), spread(self.scaled_up[b.par][:, :], MX_BLOCK),
                          ALU.mult).then_inc(self.quantized, 1)

    def store(self, sp, b):
        sp.wait_ge(self.quantized, b.n + 1)
        sp.dma_start(self.kept(b.n), self.work[:, :]).then_inc(self.stored, 16)


def feed_forward(nc, x2, weights, out):
    TILES = x2.shape[0] // P
    NB = E // MX_BLOCK
    CH = FF // E
    LOT = 4
    GU_LOTS = 2 * FF // P // LOT
    LOTS = GU_LOTS + FF // P // LOT

    with ExitStack() as ctx:
        sb = lambda name, shape, dt=F32: ctx.enter_context(nc.sbuf_tensor("f_" + name, shape, dt))
        ps = lambda name: ctx.enter_context(nc.psum_tensor("f_" + name, [P, 512], F32))
        sem = lambda name: ctx.enter_context(nc.semaphore("f_" + name))

        ones, ident = sb("ones", [P, P]), sb("ident", [P, P])
        wgu = [sb(f"wgu{i}", [P, KC, 2 * FF], F16) for i in range(2)]
        wdn = [sb(f"wdn{i}", [P, FF // P, E], F16) for i in range(2)]
        w_in = [sb(f"w_in{i}", [P, LOT, E]) for i in range(2)]
        x_in = [sb(f"x_in{i}", [P, E]) for i in range(2)]
        x_res = [sb(f"x_res{i}", [P, E]) for i in range(2)]
        x_norm, x_work, x_magic = sb("x_norm", [P, E]), sb("x_work", [P, E]), sb("x_magic", [P, E])
        x_stats, x_mean, x_rstd = sb("x_stats", [P, 1, 6]), sb("x_mean", [P, 1]), sb("x_rstd", [P, 1])
        m_const, m_tmp = sb("m_const", [P, len(MOMENT_CONSTANTS), 1]), sb("m_tmp", [P, 2, 1])
        x_scales = sb("x_scales", [P, 2, NB])
        xT = [[sb(f"xT{i}{h}", [P, KC, P], F16) for h in "hl"] for i in range(2)]
        sg = [sb(f"sg{i}", [P, E]) for i in range(2)]
        h = [sb(f"h{i}", [P, E]) for i in range(2)]
        h_work = [sb(f"h_work{i}", [P, E]) for i in range(2)]
        h_magic = [sb(f"h_magic{i}", [P, E]) for i in range(2)]
        h_scales = [sb(f"h_scales{i}", [P, 2, NB]) for i in range(2)]
        hT = [[sb(f"hT{i}{x}", [P, KC, P], F16) for x in "hl"] for i in range(2)]
        y = [sb(f"y{i}", [P, E]) for i in range(2)]

        g_ps, u_ps, d_ps = ([ps(f"{n}{i}") for i in range(2)] for n in ("g", "u", "d"))
        t_ps, xt_ps = ps("t"), ps("xt")

        ones_made, ident_ready, const_ready = sem("ones_made"), sem("ident_ready"), sem("const_ready")
        w_loaded = [sem(f"w_loaded{i}") for i in range(2)]
        w_transposed, w_hi, w_lo = sem("w_transposed"), sem("w_hi"), sem("w_lo")
        w_ps = g_ps + u_ps

        def each_lot(eng, body):
            body(At(0, 0), True)
            body(At(0, 1), True)
            with eng.Fori(1, GU_LOTS // 2) as k:
                body(At(k, 0), True)
                body(At(k, 1), True)
            with eng.Fori(GU_LOTS // 2, LOTS // 2) as k:
                body(At(k, 0), False)
                body(At(k, 1), False)

        def target(z, a, i, gate_up):
            n = a.n * LOT + i
            if gate_up:
                return wgu[z][:, :, bass.ds(n * P, P)]
            n = n - GU_LOTS * LOT
            return wdn[z][:, bass.ds(n, 1), :].rearrange("p o (r e) -> p (o r) e", e=P)

        x_loaded = [sem(f"x_loaded{i}") for i in range(2)]
        res_loaded = [sem(f"res_loaded{i}") for i in range(2)]
        stats_ready, x_pool = sem("stats_ready"), sem("x_pool")
        x_chain, x_rounded, xd_ready = sem("x_chain"), sem("x_rounded"), sem("xd_ready")
        xt_done, xt_hi, xt_lo = sem("xt_done"), sem("xt_hi"), sem("xt_lo")
        gate_done, up_done, silu_done = sem("gate_done"), sem("up_done"), sem("silu_done")
        h_chain, h_rounded, h_pool, hd_ready = (sem("h_chain"), sem("h_rounded"), sem("h_pool"), sem("hd_ready"))
        ht_done, ht_hi, ht_lo = sem("ht_done"), sem("ht_hi"), sem("ht_lo")
        down_step, y_made = sem("down_step"), sem("y_made")
        stored = [sem(f"stored{i}") for i in range(2)]

        x2_t = x2.rearrange("(t p) e -> t p e", p=P)
        out_t = out.rearrange("(t p) e -> t p e", p=P)

        def tiles(eng, body):
            body(At(0, 0))
            body(At(0, 1))
            with eng.Fori(1, TILES // 2 - 1) as k:
                body(At(k, 0))
                body(At(k, 1))
            body(At(TILES // 2 - 1, 0))
            body(At(TILES // 2 - 1, 1))

        def early(t, n):
            return isinstance(t.n, int) and t.n < n

        def final(t):
            return isinstance(t.n, int) and t.n == TILES - 1

        with nc.Block() as block:
            @block.sync
            def _(sp):
                def load_x(t):
                    if not early(t, 2):
                        sp.wait_ge(x_rounded, t.n - 1)
                    sp.dma_start(x_in[t.par][:, :], x2_t[t.n]).then_inc(x_loaded[t.par], 16)

                def store(t):
                    sp.wait_ge(y_made, t.n + 1)
                    sp.dma_start(out_t[t.n], y[t.par][:, :]).then_inc(stored[t.par], 16)

                def load_lot(a, gate_up):
                    if not (isinstance(a.n, int) and a.n < 2):
                        sp.wait_ge(w_transposed, LOT * (a.n - 1))
                    sp.dma_start(w_in[a.par][:, :, :], weights.rearrange("(l i) p e -> l p i e", i=LOT)[a.n]
                                 ).then_inc(w_loaded[a.par], 16)

                load_x(At(0, 0))
                each_lot(sp, load_lot)

                def body(t):
                    if not final(t):
                        load_x(t.plus(1))
                    if not early(t, 2):
                        sp.wait_ge(y_made, t.n - 1)
                    sp.dma_start(x_res[t.par][:, :], x2_t[t.n]).then_inc(res_loaded[t.par], 16)
                    if not early(t, 1):
                        store(t.plus(-1))

                tiles(sp, body)
                store(At(TILES // 2 - 1, 1))
                for i in range(2):
                    sp.wait_ge(stored[i], 16 * (TILES // 2))

            @block.gpsimd
            def _(gp):
                chain = Chain(gp, x_pool, MOMENT_LINKS + 1)

                def rstd(t):
                    gp.wait_ge(stats_ready, t.n + 1)
                    chain.start(t.n)
                    moments(nc.gpsimd, chain.link, x_stats, x_mean[:, :], x_rstd[:, :], m_const, m_tmp)

                def x_dequant(t):
                    gp.wait_ge(x_rounded, t.n + 1)
                    chain.link(nc.gpsimd.tensor_tensor(x_work[:, :], x_work[:, :], x_magic[:, :], ALU.subtract))
                    nc.gpsimd.tensor_tensor(blocks(x_work[:, :]), blocks(x_work[:, :]),
                                            spread(x_scales[:, 0, :], MX_BLOCK), ALU.mult).then_inc(xd_ready, 1)

                def h_dequant(t, c):
                    s = t.n * CH + c
                    gp.wait_ge(h_rounded, s + 1)
                    w = h_work[c % 2]
                    nc.gpsimd.tensor_tensor(w[:, :], w[:, :], h_magic[c % 2][:, :], ALU.subtract).then_inc(h_pool, 1)
                    gp.wait_ge(h_pool, s + 1)
                    nc.gpsimd.tensor_tensor(blocks(w[:, :]), blocks(w[:, :]),
                                            spread(h_scales[c % 2][:, 0, :], MX_BLOCK), ALU.mult).then_inc(hd_ready, 1)

                identity_matrix(gp, ones, ident, ones_made, ident_ready)
                rstd(At(0, 0))
                x_dequant(At(0, 0))

                def body(t):
                    for c in range(CH):
                        if c == 0 and not final(t):
                            rstd(t.plus(1))
                        h_dequant(t, c)
                        if c == 1 and not final(t):
                            x_dequant(t.plus(1))

                tiles(gp, body)

            @block.vector
            def _(v):
                x_links = Chain(v, x_chain, 1 + MX_ROUND_LINKS)
                h_links = Chain(v, h_chain, 1 + MX_ROUND_LINKS)

                def x_stats_of(t):
                    v.wait_ge(x_loaded[t.par], 16 * (t.half + 1))
                    nc.vector.bn_stats(x_stats[:, 0, :], x_in[t.par][:, :]).then_inc(stats_ready, 1)

                def x_round(t):
                    v.wait_ge(x_pool, (MOMENT_LINKS + 1) * t.n + MOMENT_LINKS)
                    x_links.start(t.n)
                    if not early(t, 1):
                        v.wait_ge(xt_done, t.n)
                    x_links.link(nc.vector.tensor_scalar(x_norm[:, :], x_in[t.par][:, :], x_mean[:, 0:1],
                                                         x_rstd[:, 0:1], ALU.subtract, ALU.mult))
                    mx_round_links(nc.vector, x_links.link, x_norm[:, :], x_scales[:, 0, :], x_scales[:, 1, :],
                                   x_work[:, :], x_magic[:, :], MX_EPS).then_inc(x_rounded, 1)

                def x_low(t):
                    v.wait_ge(xt_hi, t.n + 1)
                    nc.vector.tensor_tensor(xT[t.par][1][:, :, :], xt_ps[:, :].rearrange("p (a b) -> p a b", b=P),
                                            xT[t.par][0][:, :, :], ALU.subtract).then_inc(xt_lo, 1)

                def h_round(t, c):
                    s, i = t.n * CH + c, c % 2
                    v.wait_ge(up_done, s + 1)
                    v.wait_ge(silu_done, s + 1)
                    h_links.start(s)
                    link_h = nc.vector.tensor_tensor(h[i][:, :], u_ps[i][:, :], sg[i][:, :], ALU.mult)
                    h_links.link(link_h)
                    if not (early(t, 1) and c < 2):
                        v.wait_ge(ht_done, s - 1)
                    mx_round_links(nc.vector, h_links.link, h[i][:, :], h_scales[i][:, 0, :], h_scales[i][:, 1, :],
                                   h_work[i][:, :], h_magic[i][:, :], W_SCALE * MX_EPS).then_inc(h_rounded, 1)

                def h_low(t, c):
                    s, i = t.n * CH + c, c % 2
                    v.wait_ge(ht_hi, s + 1)
                    if not (early(t, 1) and c < 2):
                        v.wait_ge(down_step, s - 1)
                    nc.vector.tensor_tensor(hT[i][1][:, :, :], t_ps[:, :].rearrange("p (a b) -> p a b", b=P),
                                            hT[i][0][:, :, :], ALU.subtract).then_inc(ht_lo, 1)

                def y_of(t):
                    v.wait_ge(down_step, CH * t.n + CH)
                    v.wait_ge(res_loaded[t.par], 16 * (t.half + 1))
                    if not early(t, 2):
                        v.wait_ge(stored[t.par], 16 * t.half)
                    nc.vector.scalar_tensor_tensor(y[t.par][:, :], d_ps[t.par][:, :], W_SCALE ** -2, x_res[t.par][:, :],
                                                   ALU.mult, ALU.add).then_inc(y_made, 1)

                def low_lot(a, gate_up):
                    for i in range(LOT):
                        v.wait_ge(w_hi, LOT * a.n + i + 1)
                        nc.vector.tensor_tensor(target(1, a, i, gate_up), w_ps[i][:, :].rearrange("p (a b) -> p a b", b=P),
                                                target(0, a, i, gate_up), ALU.subtract).then_inc(w_lo, 1)
                    if isinstance(a.n, int) and a.n == 1:
                        x_round(At(0, 0))

                moment_constants(nc.vector, m_const, const_ready)
                x_stats_of(At(0, 0))
                each_lot(v, low_lot)
                x_low(At(0, 0))

                def body(t):
                    for c in range(CH):
                        if c == 0 and not final(t):
                            x_stats_of(t.plus(1))
                        if c == 1 and not final(t):
                            x_round(t.plus(1))
                        h_round(t, c)
                        if c >= 2:
                            h_low(t, c - 2)
                        elif not early(t, 1):
                            h_low(t.plus(-1), CH + c - 2)
                        if c == 2 and not early(t, 1):
                            y_of(t.plus(-1))
                        if c == 2 and not final(t):
                            x_low(t.plus(1))

                tiles(v, body)
                last = At(TILES // 2 - 1, 1)
                h_low(last, 2)
                h_low(last, 3)
                y_of(last)

            @block.scalar
            def _(act):
                def x_high(t):
                    act.wait_ge(xt_done, t.n + 1)
                    nc.scalar.activation(xT[t.par][0][:, :, :], xt_ps[:, :].rearrange("p (a b) -> p a b", b=P),
                                         ACT.Copy).then_inc(xt_hi, 1)

                def silu(t, c):
                    s, i = t.n * CH + c, c % 2
                    act.wait_ge(gate_done, s + 1)
                    if not (early(t, 1) and c < 2):
                        act.wait_ge(h_chain, (1 + MX_ROUND_LINKS) * (s - 2) + 1)
                    nc.scalar.activation(sg[i][:, :], g_ps[i][:, :], ACT.Silu, scale=1.0 / W_SCALE).then_inc(silu_done, 1)

                def h_high(t, c):
                    s, i = t.n * CH + c, c % 2
                    act.wait_ge(ht_done, s + 1)
                    if not (early(t, 1) and c < 2):
                        act.wait_ge(down_step, s - 1)
                    nc.scalar.activation(hT[i][0][:, :, :], t_ps[:, :].rearrange("p (a b) -> p a b", b=P),
                                         ACT.Copy).then_inc(ht_hi, 1)

                def high_lot(a, gate_up):
                    for i in range(LOT):
                        act.wait_ge(w_transposed, LOT * a.n + i + 1)
                        nc.scalar.activation(target(0, a, i, gate_up), w_ps[i][:, :].rearrange("p (a b) -> p a b", b=P),
                                             ACT.Copy).then_inc(w_hi, 1)

                each_lot(act, high_lot)
                x_high(At(0, 0))

                def body(t):
                    for c in range(CH):
                        silu(t, c)
                        if c >= 2:
                            h_high(t, c - 2)
                        elif not early(t, 1):
                            h_high(t.plus(-1), CH + c - 2)
                        if c == 2 and not final(t):
                            x_high(t.plus(1))

                tiles(act, body)
                last = At(TILES // 2 - 1, 1)
                h_high(last, 2)
                h_high(last, 3)

            @block.tensor
            def _(pe):
                def x_transpose(t):
                    pe.wait_ge(xd_ready, t.n + 1)
                    if not early(t, 1):
                        pe.wait_ge(xt_lo, t.n)
                    for j in range(KC):
                        last = nc.tensor.transpose(xt_ps[:, P * j:P * j + P], x_work[:, P * j:P * j + P], ident[:, :])
                    last.then_inc(xt_done, 1)

                def three_products(dst, a_hi, a_lo, b_hi, b_lo, n, start=True, stop=True):
                    last = None
                    for j in range(n):
                        for i, (a, b) in enumerate(((a_hi, b_hi), (a_hi, b_lo), (a_lo, b_hi))):
                            last = nc.tensor.matmul(dst, a(j), b(j), start=start and j == 0 and i == 0,
                                                    stop=stop and j == n - 1 and i == 2)
                    return last

                def gate_up(t, c):
                    s, i = t.n * CH + c, c % 2
                    if c == 0:
                        pe.wait_ge(xt_lo, t.n + 1)
                    if not (early(t, 1) and c < 2):
                        pe.wait_ge(silu_done, s - 1)
                    x_hi, x_lo = (lambda j, z=z: xT[t.par][z][:, j, :] for z in range(2))
                    for base, dst, done in ((0, g_ps, gate_done), (FF, u_ps, up_done)):
                        if base and not (early(t, 1) and c < 2):
                            pe.wait_ge(h_chain, (1 + MX_ROUND_LINKS) * (s - 2) + 1)
                        lo = base + E * c
                        w_hi_, w_lo_ = (lambda j, z=z: wgu[z][:, j, lo:lo + E] for z in range(2))
                        three_products(dst[i][:, :], x_hi, x_lo, w_hi_, w_lo_, KC).then_inc(done, 1)

                def h_transpose(t, c):
                    s, i = t.n * CH + c, c % 2
                    pe.wait_ge(hd_ready, s + 1)
                    if not (early(t, 1) and c < 1):
                        pe.wait_ge(ht_lo, s)
                    for j in range(KC):
                        last = nc.tensor.transpose(t_ps[:, P * j:P * j + P], h_work[i][:, P * j:P * j + P], ident[:, :])
                    last.then_inc(ht_done, 1)

                def down(t, c):
                    s, i = t.n * CH + c, c % 2
                    pe.wait_ge(ht_lo, s + 1)
                    if c == 0 and not early(t, 2):
                        pe.wait_ge(y_made, t.n - 1)
                    h_hi, h_lo = (lambda j, z=z: hT[i][z][:, j, :] for z in range(2))
                    w_hi_, w_lo_ = (lambda j, z=z: wdn[z][:, KC * c + j, :] for z in range(2))
                    three_products(d_ps[t.par][:, :], h_hi, h_lo, w_hi_, w_lo_, KC, start=c == 0,
                                   stop=c == CH - 1).then_inc(down_step, 1)

                def transpose_lot(a, gate_up):
                    for i in range(LOT):
                        if i == 0:
                            pe.wait_ge(w_loaded[a.par], 16 * (a.half + 1))
                        if not (isinstance(a.n, int) and a.n < 1):
                            pe.wait_ge(w_lo, LOT * a.n + i - LOT + 1)
                        for j in range(KC):
                            last = nc.tensor.transpose(w_ps[i][:, P * j:P * j + P], w_in[a.par][:, i, P * j:P * j + P],
                                                       ident[:, :])
                        last.then_inc(w_transposed, 1)

                pe.wait_ge(ident_ready, 1)
                each_lot(pe, transpose_lot)
                x_transpose(At(0, 0))
                pe.wait_ge(w_lo, LOT * LOTS)

                def body(t):
                    for c in range(CH):
                        gate_up(t, c)
                        if c >= 2:
                            h_transpose(t, c - 2)
                        elif not early(t, 1):
                            h_transpose(t.plus(-1), CH + c - 2)
                        if c == 3:
                            down(t, 0)
                        elif not early(t, 1):
                            down(t.plus(-1), c + 1)
                        if c == 2 and not final(t):
                            x_transpose(t.plus(1))

                tiles(pe, body)
                last = At(TILES // 2 - 1, 1)
                down(last, 1)
                h_transpose(last, 2)
                down(last, 2)
                h_transpose(last, 3)
                down(last, 3)
def self_attention(nc, x, wq, bq, wk, bk, wv, bv, wo, bo, qk_scratch, x1, gate_w, up_w, kept):
    NQ = E // P
    NKV = KV_HEADS * D
    SLOTS = HEADS + KV_HEADS
    STACK = 96
    MAX_ROW = STACK
    S2 = W_SCALE ** 2
    PAIRS = KV_HEADS // 2
    MU = 2 * TT
    UNITS = KV_HEADS * MU
    SLOTS_OF_STEP = 7
    LAST = KV_HEADS - 1

    with ExitStack() as ctx:
        sb = lambda name, shape, dt=F32: ctx.enter_context(nc.sbuf_tensor("a_" + name, shape, dt))
        ps = lambda name, n=512: ctx.enter_context(nc.psum_tensor("a_" + name, [P, n], F32))
        sem = lambda name: ctx.enter_context(nc.semaphore("a_" + name))
        two = lambda f, name, *a: [f(f"{name}{i}", *a) for i in range(2)]

        ones, ident = sb("ones", [P, P]), sb("ident", [P, P])
        w_qkv = two(sb, "w_qkv", [P, KC, E + 2 * NKV], F16)
        w_o = two(sb, "w_o", [P, PAIRS, E], F16)
        bias_qk = sb("bias_qk", [P, NQ + 1])
        bias_v, bias_o = sb("bias_v", [P, NKV]), sb("bias_o", [P, E])
        x_in = two(sb, "x_in", [P, TT, E])
        x_norm = sb("x_norm", [P, TT, E])
        stats, mean, rstd = sb("stats", [P, TT, 6]), sb("mean", [P, TT]), sb("rstd", [P, TT])
        m_const, m_tmp = sb("m_const", [P, len(MOMENT_CONSTANTS), TT]), sb("m_tmp", [P, 2, TT])
        xT = two(sb, "xT", [P, KC, SEQ], F16)
        qk = two(sb, "qk", [P, NQ + 1, SEQ], F16)
        stack = two(sb, "stack", [P, SLOTS, SEQ], F16)
        v_raw = sb("v_raw", [P, TT, NKV])
        v_ones = two(sb, "v_ones", [P, TT, KV_HEADS, 2 * D])
        row_max, max_row = sb("row_max", [P, P]), sb("max_row", [HEADS * TT, P], F16)
        prob = [two(sb, f"prob{g}", [P, GROUP * SEQ]) for g in range(2)]
        o_t, o_norm = sb("o_t", [P, 2, SEQ // 32, 32]), sb("o_norm", [P, SEQ // 32, 2, D])
        o_rec = sb("o_rec", [P, 2, SEQ // 32])
        att = sb("att", [P, PAIRS, SEQ])
        att16 = two(sb, "att16", [P, PAIRS, SEQ], F16)
        x_res = two(sb, "x_res", [P, TT, E])
        stage_qkv, stage_o = sb("stage_qkv", [P, KC, E + 2 * NKV]), sb("stage_o", [P, PAIRS, E])

        s_ps, m_ps = ([ps(f"{name}{i}") for i in range(BANKS)] for name in "sm")
        o_ps, c_ps = ps("o"), ps("c")

        ones_made, ident_ready = sem("ones_made"), sem("ident_ready")
        w_loaded, w_hi, w_lo = two(sem, "w_loaded"), sem("w_hi"), sem("w_lo")
        bias_loaded, bias_ready, fixed_ready, stack_ready = (
            sem("bias_loaded"), sem("bias_ready"), sem("fixed_ready"), sem("stack_ready"))

        rows = lambda w: w.rearrange("(c p) n -> p c n", p=P)
        wo_rows = wo.rearrange("(gp g2 j d) n -> j g2 d gp n", gp=PAIRS, g2=2, j=GROUP)
        across = lambda v: v.rearrange("(o n) -> o n", o=1).to_broadcast([P, v.shape[0]])

        x_loaded, res_loaded, stored = two(sem, "x_loaded"), two(sem, "res_loaded"), two(sem, "stored")
        stats_ready, m_chain, norm_ready, v_out = sem("stats_ready"), sem("m_chain"), sem("norm_ready"), sem("v_out")
        xt_done, xt_hi, xt_lo = sem("xt_done"), sem("xt_hi"), sem("xt_lo")
        q_done, v_done, qk_hi, qk_lo, v_ready = (
            sem("q_done"), sem("v_done"), sem("qk_hi"), sem("qk_lo"), sem("v_ready"))
        left, stacked = sem("left"), two(sem, "stacked")
        max_done, max_taken, max_t, max_cast, max_placed = (
            sem("max_done"), sem("max_taken"), sem("max_t"), sem("max_cast"), two(sem, "max_placed"))
        score_done, prob_ready, pv_done = sem("score_done"), sem("prob_ready"), sem("pv_done")
        o_chain, att_ready, att_hi, att_lo = sem("o_chain"), sem("att_ready"), sem("att_hi"), sem("att_lo")
        y_done, biased, y_added = sem("y_done"), sem("biased"), sem("y_added")
        O_LINKS = 3

        quantizers = [WeightQuantizer(nc, sb, sem, name, lambda n, w=w: w.rearrange("(n p) e -> n p e", p=P)[n],
                                      lambda n, i=i: kept[n + BATCH * i])
                      for i, (name, w) in enumerate((("gate", gate_w), ("up", up_w)))]

        xb = x.rearrange("b (t p) e -> b p t e", p=P)
        x1b = x1.rearrange("b (t p) e -> b p t e", p=P)

        known = lambda b: isinstance(b.n, int)
        early = lambda b, n: known(b) and b.n < n
        within = lambda b: not known(b) or b.n < BATCH

        def max_unit(step, slot):
            starts = (0, 0, 5, 12, 19, 23, 28, UNITS, UNITS)
            n = starts[step] + slot - (2 if step == 1 else 0)
            return n if starts[step] <= n < starts[step + 1] else None

        def batches(eng, body):
            body(At(0, 0))
            body(At(0, 1))
            with eng.Fori(1, BATCH // 2 - 2) as k:
                body(At(k, 0))
                body(At(k, 1))
            for k in (BATCH // 2 - 2, BATCH // 2 - 1):
                body(At(k, 0))
                body(At(k, 1))

        with nc.Block() as block:
            @block.sync
            def _(sp):
                def load_x(b):
                    if not early(b, 2):
                        sp.wait_ge(norm_ready, b.n - 1)
                    sp.dma_start(x_in[b.par][:, :, :], xb[b.n]).then_inc(x_loaded[b.par], 16)

                def leave(b):
                    sp.wait_ge(qk_lo, (NQ + 1) * (b.n + 1))
                    for z in range(2):
                        sp.dma_start(qk_scratch[b.n, z].rearrange("(c p) s -> p c s", p=P),
                                     qk[z][:, :, :]).then_inc(left, 16)

                def enter(b):
                    if early(b, 2):
                        sp.wait_ge(left, 32 * (b.n + 1))
                    else:
                        sp.wait_ge(score_done, UNITS * (b.n - 1))
                    st = stack[b.par]
                    src = [qk_scratch[b.n, z].rearrange("(h d) s -> d h s", d=D) for z in range(2)]
                    for row, q_half, k_half in ((0, 0, 0), (1, 1, 0), (2, 0, 1), (3, 1, 1)):
                        dst = st[D * row:D * row + D, :, :]
                        sp.dma_start(dst[:, 0:HEADS, :], src[q_half][:, 0:HEADS, :]).then_inc(stacked[b.par], 16)
                        sp.dma_start(dst[:, HEADS:SLOTS, :], src[k_half][:, HEADS:SLOTS, :]).then_inc(stacked[b.par], 16)

                def place_max(b):
                    sp.wait_ge(max_cast, b.n + 1)
                    dst = stack[b.par][MAX_ROW:MAX_ROW + 1, 0:HEADS, :]
                    sp.dma_start(dst.rearrange("o h (q t) -> o (h q) t", t=P),
                                 max_row[:, :]).then_inc(max_placed[b.par], 16)

                def load_res(b):
                    if not early(b, 2):
                        sp.wait_ge(stored[b.par], 16 * b.half)
                    sp.dma_start(x_res[b.par][:, :, :], xb[b.n]).then_inc(res_loaded[b.par], 16)

                def store(b):
                    sp.wait_ge(y_added, TT * (b.n + 1))
                    sp.dma_start(x1b[b.n], x_res[b.par][:, :, :]).then_inc(stored[b.par], 16)

                load_x(At(0, 0))
                for first, w in ((0, wq), (E, wk), (E + NKV, wv)):
                    sp.dma_start(stage_qkv[:, :, first:first + w.shape[1]], rows(w)).then_inc(w_loaded[0], 16)
                load_x(At(0, 1))
                for j in range(GROUP):
                    for g2 in range(2):
                        sp.dma_start(stage_o[32 * j + D * g2:32 * j + D * g2 + D, :, :], wo_rows[j, g2]).then_inc(w_loaded[1], 16)
                load_x(At(1, 0))
                leave(At(0, 0))
                enter(At(0, 0))
                leave(At(0, 1))
                enter(At(0, 1))
                load_x(At(1, 1))
                for z in quantizers:
                    z.load(sp, At(0, 0))
                place_max(At(0, 0))

                def body(b):
                    if within(b.plus(4)):
                        load_x(b.plus(4))
                    load_res(b)
                    if within(b.plus(2)):
                        leave(b.plus(2))
                    if not early(b, 1):
                        for z in quantizers:
                            z.store(sp, b.plus(-1))
                        store(b.plus(-1))
                    if within(b.plus(1)):
                        for z in quantizers:
                            z.load(sp, b.plus(1))
                    if within(b.plus(1)):
                        place_max(b.plus(1))
                    if within(b.plus(2)):
                        enter(b.plus(2))

                batches(sp, body)
                for z in quantizers:
                    z.store(sp, At(BATCH // 2 - 1, 1))
                    sp.wait_ge(z.stored, 16 * BATCH)
                store(At(BATCH // 2 - 1, 1))
                for i in range(2):
                    sp.wait_ge(stored[i], 16 * (BATCH // 2))

            @block.gpsimd
            def _(gp):
                chain = Chain(gp, m_chain, MOMENT_LINKS)

                def row_moments(b):
                    gp.wait_ge(stats_ready, TT * (b.n + 1))
                    chain.start(b.n)
                    moments(nc.gpsimd, chain.link, stats, mean[:, :], rstd[:, :], m_const, m_tmp)

                def add_bias(b):
                    gp.wait_ge(res_loaded[b.par], 16 * (b.half + 1))
                    r = x_res[b.par]
                    for t in range(TT):
                        nc.gpsimd.tensor_tensor(r[:, t, :], r[:, t, :], bias_o[:, :], ALU.add).then_inc(biased, 1)

                def low_att(b, p):
                    if p == 0 and not early(b, 1):
                        gp.wait_ge(y_done, TT * b.n)
                    gp.wait_ge(att_hi, PAIRS * b.n + p + 1)
                    nc.gpsimd.tensor_tensor(att16[1][:, p, :], att[:, p, :], att16[0][:, p, :],
                                            ALU.subtract).then_inc(att_lo, 1)

                def keep_v(b):
                    gp.wait_ge(v_out, b.n + 1)
                    if not early(b, 2):
                        gp.wait_ge(pv_done, KV_HEADS * (b.n - 1))
                    for t in range(TT):
                        nc.gpsimd.tensor_tensor(
                            v_ones[b.par][:, t, :, 0:D], v_raw[:, t, :].rearrange("p (g d) -> p g d", d=D),
                            bias_v[:, :].rearrange("p (g d) -> p g d", d=D), ALU.add).then_inc(v_ready, 1)

                gp.dma_start(bias_qk[:, 0:NQ], bq.rearrange("(c p) -> p c", p=P), allow_slow_non_contiguous=True).then_inc(bias_loaded, 16)
                gp.dma_start(bias_qk[:, NQ:NQ + 1], bk.rearrange("(c p) -> p c", p=P), allow_slow_non_contiguous=True).then_inc(bias_loaded, 16)
                gp.dma_start(bias_v[:, :], across(bv)).then_inc(bias_loaded, 16)
                gp.dma_start(bias_o[:, :], across(bo)).then_inc(bias_loaded, 16)
                identity_matrix(gp, ones, ident, ones_made, ident_ready)
                row_moments(At(0, 0))
                gp.wait_ge(bias_loaded, 64)
                nc.gpsimd.tensor_scalar(bias_qk[:, :], bias_qk[:, :], W_SCALE, None, ALU.mult).then_inc(bias_ready, 1)
                nc.gpsimd.tensor_scalar(bias_v[:, :], bias_v[:, :], W_SCALE, None, ALU.mult).then_inc(bias_ready, 1)
                gp.wait_ge(bias_ready, 2)
                row_moments(At(0, 1))
                for n, st in enumerate(stack):
                    if n:
                        gp.wait_ge(stack_ready, 2 * n)
                    nc.gpsimd.memset(st[64:STACK, :, :].bitcast(U32), 0).then_inc(stack_ready, 1)
                    gp.wait_ge(stack_ready, 2 * n + 1)
                    nc.gpsimd.memset(st[MAX_ROW:MAX_ROW + 1, HEADS:SLOTS, :], -S2).then_inc(stack_ready, 1)
                gp.wait_ge(stack_ready, 4)
                keep_v(At(0, 0))
                row_moments(At(1, 0))
                keep_v(At(0, 1))

                def body(b):
                    if not early(b, 1) and within(b.plus(1)):
                        keep_v(b.plus(1))
                    if within(b.plus(3)):
                        row_moments(b.plus(3))
                    if not early(b, 1):
                        low_att(b.plus(-1), 2)
                        low_att(b.plus(-1), 3)
                        for z in quantizers:
                            z.round(gp, b.plus(-1))
                    add_bias(b)
                    for z in quantizers:
                        z.divide(gp, b)
                    low_att(b, 0)
                    low_att(b, 1)

                batches(gp, body)
                last = At(BATCH // 2 - 1, 1)
                low_att(last, 2)
                low_att(last, 3)
                for z in quantizers:
                    z.round(gp, last)

            @block.vector
            def _(v):
                def layernorm_stats(b):
                    v.wait_ge(x_loaded[b.par], 16 * (b.half + 1))
                    for t in range(TT):
                        nc.vector.bn_stats(stats[:, t, :], x_in[b.par][:, t, :]).then_inc(stats_ready, 1)

                def layernorm(b):
                    v.wait_ge(m_chain, MOMENT_LINKS * (b.n + 1))
                    if not early(b, 1):
                        v.wait_ge(xt_done, 2 * b.n)
                    for t in range(TT):
                        last = nc.vector.tensor_scalar(x_norm[:, t, :], x_in[b.par][:, t, :], mean[:, t:t + 1],
                                                       rstd[:, t:t + 1], ALU.subtract, ALU.mult)
                    last.then_inc(norm_ready, 1)

                def take_max(b, unit):
                    if unit is None or not within(b):
                        return
                    g, u = unit // MU, unit % MU
                    qt, pair = u // 2, u % 2
                    first = (GROUP * g + 2 * pair) * TT + qt
                    v.wait_ge(max_done, UNITS * b.n + unit + 1)
                    if unit == 0 and not early(b, 1):
                        v.wait_ge(max_t, b.n)
                    nc.vector.tensor_reduce(row_max[:, first:first + TT + 1:TT],
                                            m_ps[unit % BANKS][:, :].rearrange("p (h k) -> p h k", h=2),
                                            AX.X, ALU.max).then_inc(max_taken, 1)

                def normalize(b, p, part):
                    done = O_LINKS * (PAIRS * b.n + p) + part
                    if part == 0:
                        v.wait_ge(pv_done, KV_HEADS * b.n + 2 * p + 2)
                        nc.vector.transpose(o_t[:, :, :, :].rearrange("p a b c -> p (a b c)"),
                                            o_ps[:, :]).then_inc(o_chain, 1)
                    elif part == 1:
                        v.wait_ge(o_chain, done)
                        nc.vector.reciprocal(o_rec[:, :, :], o_t[:, :, :, D]).then_inc(o_chain, 1)
                    elif part == 2:
                        v.wait_ge(o_chain, done)
                        nc.vector.tensor_tensor(
                            o_norm[:, :, :, :].rearrange("p b a d -> p a b d"), o_t[:, :, :, 0:D],
                            o_rec[:, :, :].rearrange("p a (b o) -> p a b o", o=1).to_broadcast([P, 2, SEQ // 32, D]),
                            ALU.mult).then_inc(o_chain, 1)
                    else:
                        v.wait_ge(o_chain, done)
                        if not early(b, 1):
                            v.wait_ge(att_lo, PAIRS * (b.n - 1) + p + 1)
                        nc.vector.transpose(att[:, p, :], o_norm[:, :, :, :].rearrange("p b a d -> p (b a d)")
                                            ).then_inc(att_ready, 1)

                def residual(b, t):
                    v.wait_ge(biased, TT * b.n + t + 1)
                    v.wait_ge(y_done, TT * b.n + t + 1)
                    r = x_res[b.par][:, t, :]
                    nc.vector.scalar_tensor_tensor(r, c_ps[:, :], W_SCALE ** -2, r, ALU.mult, ALU.add).then_inc(y_added, 1)

                def low_x(b, i):
                    v.wait_ge(xt_hi, 2 * b.n + i + 1)
                    nc.vector.tensor_tensor(xT[1][:, 2 * i:2 * i + 2, :], c_ps[:, :].rearrange("p (c s) -> p c s", s=SEQ),
                                            xT[0][:, 2 * i:2 * i + 2, :], ALU.subtract).then_inc(xt_lo, 1)

                def low_qk(b, c):
                    if c == 0 and not early(b, 1):
                        v.wait_ge(left, 32 * b.n)
                    if c < NQ:
                        v.wait_ge(qk_hi, (NQ + 1) * b.n + c // 2 * 2 + 2)
                    else:
                        v.wait_ge(v_out, b.n + 1)
                    nc.vector.scalar_tensor_tensor(qk[1][:, c, :], c_ps[:, SEQ * (c % 2):SEQ * (c % 2) + SEQ],
                                                   bias_qk[:, c:c + 1], qk[0][:, c, :], ALU.add,
                                                   ALU.subtract).then_inc(qk_lo, 1)

                def take_bank(b, g):
                    ahead, far = b.plus(2), b.plus(3)
                    if g in (0, 1) and within(ahead):
                        low_qk(ahead, 2 * g)
                        low_qk(ahead, 2 * g + 1)
                    if g == 2 and within(ahead):
                        low_qk(ahead, NQ)
                    if g in (3, 4) and not early(b, 1):
                        residual(b.plus(-1), g - 3)
                    if g in (6, 7) and within(far):
                        low_x(far, g - 6)

                def low_weight(n, src, pair):
                    v.wait_ge(w_hi, n + 1)
                    nc.vector.scalar_tensor_tensor(pair[1][:, :, :], src[:, :, :], W_SCALE, pair[0][:, :, :],
                                                   ALU.mult, ALU.subtract).then_inc(w_lo, 1)

                moment_constants(nc.vector, m_const, fixed_ready)
                nc.vector.memset(row_max[:, HEADS * TT:P], 0.0).then_inc(fixed_ready, 1)
                for t in v_ones:
                    nc.vector.memset(t[:, :, :, D:2 * D], 1.0).then_inc(fixed_ready, 1)
                layernorm_stats(At(0, 0))
                low_weight(0, stage_qkv, w_qkv)
                layernorm(At(0, 0))
                v.wait_ge(bias_ready, 2)
                layernorm_stats(At(0, 1))
                low_x(At(0, 0), 0)
                low_x(At(0, 0), 1)
                low_qk(At(0, 0), 0)
                low_qk(At(0, 0), 1)
                layernorm(At(0, 1))
                low_weight(1, stage_o, w_o)
                for c in range(2, NQ + 1):
                    low_qk(At(0, 0), c)
                low_x(At(0, 1), 0)
                low_x(At(0, 1), 1)
                for unit in range(UNITS):
                    take_max(At(0, 0), unit)
                    if unit in (7, 15):
                        low_qk(At(0, 1), (unit - 7) // 4)
                        low_qk(At(0, 1), (unit - 7) // 4 + 1)
                    if unit == 7:
                        layernorm_stats(At(1, 0))
                    if unit == 19:
                        layernorm(At(1, 0))
                    if unit == 23:
                        low_qk(At(0, 1), NQ)
                    if unit in (27, 31):
                        low_x(At(1, 0), (unit - 27) // 4)

                def body(b):
                    for g in range(KV_HEADS):
                        done = b if g >= 2 else b.plus(-1)
                        pair = (g // 2 - 1) % PAIRS
                        begins, ready = (g % 2 == i and not early(done, 0) for i in range(2))
                        take_bank(b, g)
                        for slot in range(SLOTS_OF_STEP):
                            if ready and 1 <= slot < 4:
                                normalize(done, pair, slot)
                            if begins and slot == 4:
                                normalize(done, pair, 0)
                            take_max(b.plus(1), max_unit(g, slot))
                        if g == 0 and within(b.plus(3)):
                            layernorm_stats(b.plus(3))
                        if g == 0:
                            for z in quantizers:
                                z.scales(v, b)
                        if g == LAST:
                            for z in quantizers:
                                z.magic(v, b)
                        if g == 4 and within(b.plus(3)):
                            layernorm(b.plus(3))

                batches(v, body)
                last = At(BATCH // 2 - 1, 1)
                for part in range(4):
                    normalize(last, PAIRS - 1, part)
                for t in range(TT):
                    residual(last, t)

            @block.scalar
            def _(act):
                def exponentials(b, g, kt):
                    for pair in range(2):
                        unit = MU * g + 2 * kt + pair
                        act.wait_ge(score_done, UNITS * b.n + unit + 1)
                        if kt == 0 and pair == 0 and not (early(b, 1) and g < 2):
                            act.wait_ge(pv_done, KV_HEADS * b.n + g - 1)
                        nc.scalar.activation(prob[g % 2][kt][:, 512 * pair:512 * pair + 512], s_ps[unit % BANKS][:, :],
                                             ACT.Exp, scale=D ** -0.5 / S2).then_inc(prob_ready, 1)

                def high_att(b, p):
                    act.wait_ge(att_ready, PAIRS * b.n + p + 1)
                    if p == 0 and not early(b, 1):
                        act.wait_ge(y_done, TT * b.n)
                    nc.scalar.activation(att16[0][:, p, :], att[:, p, :], ACT.Copy).then_inc(att_hi, 1)

                def cast_max(b):
                    act.wait_ge(max_t, b.n + 1)
                    if not early(b, 1) and within(b.plus(1)):
                        act.wait_ge(left, 32 * (b.n + 2))
                    if not early(b, 1):
                        prev = b.plus(-1)
                        act.wait_ge(max_placed[prev.par], 16 * (prev.half + 1))
                    nc.scalar.activation(max_row[:, :], m_ps[0][0:HEADS * TT, 0:P], ACT.Copy, scale=1.0 / S2).then_inc(max_cast, 1)

                def high_x(b, i):
                    act.wait_ge(xt_done, 2 * b.n + i + 1)
                    nc.scalar.activation(xT[0][:, 2 * i:2 * i + 2, :], c_ps[:, :].rearrange("p (c s) -> p c s", s=SEQ),
                                         ACT.Copy).then_inc(xt_hi, 1)

                def high_qk(b, c):
                    if c == 0 and not early(b, 1):
                        act.wait_ge(left, 32 * b.n)
                    if c < NQ:
                        act.wait_ge(q_done, 2 * b.n + c // 2 + 1)
                    else:
                        act.wait_ge(v_done, b.n + 1)
                    nc.scalar.activation(qk[0][:, c, :], c_ps[:, SEQ * (c % 2):SEQ * (c % 2) + SEQ], ACT.Identity,
                                         bias=bias_qk[:, c:c + 1]).then_inc(qk_hi, 1)

                def copy_v(b):
                    act.wait_ge(v_done, b.n + 1)
                    if not early(b, 1):
                        act.wait_ge(v_ready, TT * b.n)
                    nc.scalar.activation(v_raw[:, :, :], c_ps[:, SEQ:2 * SEQ].rearrange("p (t n) -> p t n", n=NKV),
                                         ACT.Copy).then_inc(v_out, 1)

                def high_parts(b):
                    high_x(b, 0)
                    high_x(b, 1)
                    for c in range(NQ + 1):
                        high_qk(b, c)
                    copy_v(b)

                for n, (src, pair) in enumerate(((stage_qkv, w_qkv), (stage_o, w_o))):
                    act.wait_ge(w_loaded[n], 16 * (3 if n == 0 else 2 * GROUP))
                    nc.scalar.activation(pair[0][:, :, :], src[:, :, :], ACT.Copy, scale=W_SCALE).then_inc(w_hi, 1)
                act.wait_ge(bias_ready, 2)
                high_parts(At(0, 0))
                high_parts(At(0, 1))
                high_x(At(1, 0), 0)
                high_x(At(1, 0), 1)
                cast_max(At(0, 0))
                high_qk(At(1, 0), 0)
                high_qk(At(1, 0), 1)

                def body(b):
                    ahead, far = b.plus(2), b.plus(3)
                    for g in range(KV_HEADS):
                        exponentials(b, g, 0)
                        if g == LAST and within(b.plus(1)):
                            cast_max(b.plus(1))
                        exponentials(b, g, 1)
                        if g in (0, 1) and not early(b, 1):
                            high_att(b.plus(-1), 2 + g)
                        if g == 0 and within(ahead):
                            high_qk(ahead, 2)
                            high_qk(ahead, 3)
                        if g == 1 and within(ahead):
                            high_qk(ahead, NQ)
                            copy_v(ahead)
                        if g in (4, 6):
                            high_att(b, (g - 4) // 2)
                        if g in (5, 6) and within(far):
                            high_x(far, g - 5)
                        if g == LAST and within(far):
                            high_qk(far, 0)
                            high_qk(far, 1)

                batches(act, body)
                last = At(BATCH // 2 - 1, 1)
                high_att(last, 2)
                high_att(last, 3)

            @block.tensor
            def _(pe):
                def products(dst, lhs, rhs, first, end, n):
                    for j in range(first, end):
                        for i, (a, b_) in enumerate(((0, 0), (0, 1), (1, 0))):
                            last = nc.tensor.matmul(dst, lhs(a, j), rhs(b_, j), start=j == 0 and i == 0,
                                                    stop=j == n - 1 and i == 2)
                    return last

                def transpose_x(b, i, c):
                    if i == 0 and c == 0:
                        pe.wait_ge(norm_ready, b.n + 1)
                        if not early(b, 1):
                            pe.wait_ge(qk_lo, (NQ + 1) * b.n)
                        if not early(b, 4):
                            pe.wait_ge(y_added, TT * (b.n - 3))
                    elif c == 0:
                        pe.wait_ge(xt_lo, 2 * b.n + i)
                    for t in range(TT):
                        last = nc.tensor.transpose(c_ps[:, SEQ * c + P * t:SEQ * c + P * t + P],
                                                   x_norm[:, t, P * (2 * i + c):P * (2 * i + c) + P], ident[:, :])
                    if c == 1:
                        last.then_inc(xt_done, 1)

                def project_qk(b, c):
                    if c == 0:
                        pe.wait_ge(xt_lo, 2 * (b.n + 1))
                    elif c % 2 == 0:
                        pe.wait_ge(qk_lo, (NQ + 1) * b.n + c)
                    last = products(c_ps[:, SEQ * (c % 2):SEQ * (c % 2) + SEQ],
                                    lambda z, j: w_qkv[z][:, j, P * c:P * c + P], lambda z, j: xT[z][:, j, :], 0, KC, KC)
                    if c % 2:
                        last.then_inc(q_done, 1)

                def project_v(b):
                    for t in range(TT):
                        last = products(c_ps[:, SEQ + NKV * t:SEQ + NKV * t + NKV],
                                        lambda z, j: xT[z][:, j, P * t:P * t + P],
                                        lambda z, j: w_qkv[z][:, j, E + NKV:E + 2 * NKV], 0, KC, KC)
                    last.then_inc(v_done, 1)

                def project(b):
                    for i in range(2):
                        transpose_x(b, i, 0)
                        transpose_x(b, i, 1)
                    for c in range(NQ + 1):
                        project_qk(b, c)
                    project_v(b)

                def max_scores(b, unit):
                    if unit is None or not within(b):
                        return
                    if unit == 0:
                        pe.wait_ge(stacked[b.par], 8 * 16 * (b.half + 1))
                        if not early(b, 1):
                            pe.wait_ge(max_cast, b.n)
                    st, g, u = stack[b.par], unit // MU, unit % MU
                    qt, pair = u // 2, u % 2
                    if unit >= BANKS:
                        pe.wait_ge(max_taken, UNITS * b.n + unit - BANKS + 1)
                    for e in range(2):
                        last = nc.tensor.matmul(m_ps[unit % BANKS][:, SEQ * e:SEQ * e + SEQ],
                                                st[0:STACK, GROUP * g + 2 * pair + e, P * qt:P * qt + P],
                                                st[0:STACK, HEADS + g, :], start=True, stop=True)
                    last.then_inc(max_done, 1)

                def transpose_max(b):
                    pe.wait_ge(max_taken, UNITS * (b.n + 1))
                    nc.tensor.transpose(m_ps[0][:, 0:P], row_max[:, :], ident[:, :]).then_inc(max_t, 1)

                def scores(b, g, kt, pair):
                    st, unit, h = stack[b.par], MU * g + 2 * kt + pair, GROUP * g + 2 * pair
                    if unit == 0:
                        pe.wait_ge(max_placed[b.par], 16 * (b.half + 1))
                    if unit >= BANKS:
                        pe.wait_ge(prob_ready, UNITS * b.n + unit - BANKS + 1)
                    elif not early(b, 1):
                        pe.wait_ge(prob_ready, UNITS * b.n + LAST_USE[unit] + 1)
                    nc.tensor.matmul(s_ps[unit % BANKS][:, :], st[0:MAX_ROW + 1, HEADS + g, P * kt:P * kt + P],
                                     st[0:MAX_ROW + 1, h:h + 2, :], start=True, stop=True).then_inc(score_done, 1)

                def weighted_values(b, g, kt):
                    if kt == 0:
                        if g == 0:
                            pe.wait_ge(v_ready, TT * (b.n + 1))
                        pe.wait_ge(prob_ready, UNITS * b.n + MU * (g + 1))
                        if g % 2 == 0 and not (early(b, 1) and g == 0):
                            pe.wait_ge(o_chain, O_LINKS * (PAIRS * b.n + g // 2 - 1) + 1)
                    for j in range(GROUP):
                        last = nc.tensor.matmul(o_ps[32 * j:32 * j + 32, SEQ * (g % 2):SEQ * (g % 2) + SEQ],
                                                v_ones[b.par][:, kt, g, :],
                                                prob[g % 2][kt][:, SEQ * j:SEQ * j + SEQ],
                                                start=kt == 0, stop=kt == TT - 1)
                    if kt == TT - 1:
                        last.then_inc(pv_done, 1)

                def output(b, t, half):
                    if half == 0:
                        if t == 0:
                            if early(b, 1):
                                pe.wait_ge(w_lo, 2)
                            pe.wait_ge(att_lo, PAIRS * (b.n + 1))
                            if within(b.plus(3)):
                                pe.wait_ge(qk_lo, (NQ + 1) * (b.n + 4))
                        else:
                            pe.wait_ge(y_added, TT * b.n + t)
                    last = products(c_ps[:, :], lambda z, j: att16[z][:, j, P * t:P * t + P],
                                    lambda z, j: w_o[z][:, j, :], 2 * half, 2 * half + 2, PAIRS)
                    if half == 1:
                        last.then_inc(y_done, 1)

                def fill_bank(b, g, half):
                    ahead, far = b.plus(2), b.plus(3)
                    if g == 0 and within(ahead):
                        project_qk(ahead, 2 + half)
                    if g == 1 and within(ahead):
                        if half == 0:
                            project_qk(ahead, NQ)
                        else:
                            project_v(ahead)
                    if g in (2, 3) and not early(b, 1):
                        output(b.plus(-1), g - 2, half)
                    if g in (5, 6) and within(far):
                        transpose_x(far, g - 5, half)
                    if g == LAST and within(far):
                        project_qk(far, half)

                pe.wait_ge(ident_ready, 1)
                pe.wait_ge(w_lo, 1)
                project(At(0, 0))
                for i in range(2):
                    transpose_x(At(0, 1), i, 0)
                    transpose_x(At(0, 1), i, 1)
                pe.wait_ge(stack_ready, 4)
                for unit in range(UNITS):
                    if unit in (0, 8):
                        project_qk(At(0, 1), unit // 4)
                        project_qk(At(0, 1), unit // 4 + 1)
                    if unit == 16:
                        project_qk(At(0, 1), NQ)
                        project_v(At(0, 1))
                    if unit in (24, 28):
                        for c in range(2):
                            transpose_x(At(1, 0), (unit - 24) // 4, c)
                    max_scores(At(0, 0), unit)
                transpose_max(At(0, 0))
                for c in range(2):
                    project_qk(At(1, 0), c)

                def body(b):
                    for g in range(KV_HEADS):
                        step = lambda slot: max_scores(b.plus(1), max_unit(g, slot))
                        prev = b if g else b.plus(-1)
                        scores(b, g, 0, 0)
                        step(0)
                        scores(b, g, 0, 1)
                        step(1)
                        if g == LAST and within(b.plus(1)):
                            transpose_max(b.plus(1))
                        if not early(prev, 0):
                            weighted_values(prev, (g - 1) % KV_HEADS, 0)
                        scores(b, g, 1, 0)
                        step(2)
                        if not early(prev, 0):
                            weighted_values(prev, (g - 1) % KV_HEADS, 1)
                        scores(b, g, 1, 1)
                        step(3)
                        fill_bank(b, g, 0)
                        step(4)
                        fill_bank(b, g, 1)
                        step(5)
                        step(6)

                batches(pe, body)
                last = At(BATCH // 2 - 1, 1)
                for kt in range(TT):
                    weighted_values(last, LAST, kt)
                for t in range(TT):
                    for half in range(2):
                        output(last, t, half)
def cross_attention(nc, x1, context, gamma, xc_scratch, x2, down_w, kept):
    HPT = X_HEADS // TT
    KT = E // P
    SLOTS = 2 * X_HEADS
    STACK = 3 * X_D
    MAX_ROW = STACK
    UNITS = X_HEADS * KT
    SLOTS_OF_STEP = 7
    LAST = X_HEADS - 1

    with ExitStack() as ctx:
        sb = lambda name, shape, dt=F32: ctx.enter_context(nc.sbuf_tensor("x_" + name, shape, dt))
        ps = lambda name, n=512: ctx.enter_context(nc.psum_tensor("x_" + name, [P, n], F32))
        sem = lambda name: ctx.enter_context(nc.semaphore("x_" + name))
        two = lambda f, name, *a: [f(f"{name}{i}", *a) for i in range(2)]

        ones, ident = sb("ones", [P, P]), sb("ident", [P, P])
        gam = sb("gam", [P, 1])
        x_in, c_in = two(sb, "x_in", [P, TT, E]), two(sb, "c_in", [P, TT, E])
        x_norm = sb("x_norm", [P, TT, E])
        stats, mean, rstd = sb("stats", [P, TT, 6]), sb("mean", [P, TT]), sb("rstd", [P, TT])
        m_const, m_tmp = sb("m_const", [P, len(MOMENT_CONSTANTS), TT]), sb("m_tmp", [P, 2, TT])
        x16, c16 = two(sb, "x16", [P, TT, E], F16), two(sb, "c16", [P, TT, E], F16)
        stack = two(sb, "stack", [P, SLOTS, E], F16)
        v_t = two(sb, "v_t", [P, KT, SEQ])
        row_max, max_row = sb("row_max", [P, X_HEADS * KT]), sb("max_row", [X_HEADS * KT, P], F16)
        prob = [[sb(f"prob{t}{j}", [P, KT, E]) for j in range(HPT)] for t in range(TT)]
        s_t, s_rec, s_inv = sb("s_t", [P, E // 32, 32]), sb("s_rec", [P, E // 32]), sb("s_inv", [P, E])
        o_gam, o_norm = sb("o_gam", [P, E]), sb("o_norm", [P, E])
        x_res = two(sb, "x_res", [P, TT, E])

        s_ps, m_ps = ([ps(f"{name}{i}") for i in range(BANKS)] for name in "sm")
        o_ps, r_ps = ps("o"), ps("r")

        ones_made, ident_ready, gam_loaded, fixed_ready = (
            sem("ones_made"), sem("ident_ready"), sem("gam_loaded"), sem("fixed_ready"))
        x_loaded, c_loaded = two(sem, "x_loaded"), two(sem, "c_loaded")
        res_loaded, stored = two(sem, "res_loaded"), two(sem, "stored")
        stats_ready, m_chain, norm_ready = sem("stats_ready"), sem("m_chain"), sem("norm_ready")
        x_hi, c_hi, split_ready = sem("x_hi"), sem("c_hi"), sem("split_ready")
        left, stacked = sem("left"), two(sem, "stacked")
        vt_done, vt_ready = sem("vt_done"), sem("vt_ready")
        max_done, max_taken, max_t, max_cast, max_placed = (
            sem("max_done"), sem("max_taken"), sem("max_t"), sem("max_cast"), two(sem, "max_placed"))
        score_done, prob_ready, pv_done = sem("score_done"), sem("prob_ready"), sem("pv_done")
        n_chain, o_taken, y_added = sem("n_chain"), sem("o_taken"), sem("y_added")
        o_scaled = sem("o_scaled")
        N_LINKS = 3

        quantizer = WeightQuantizer(nc, sb, sem, "down",
                                    lambda n: down_w.rearrange("(r p) (n e) -> n p r e", p=P, e=P)[n],
                                    lambda n: kept[n])

        tiled = lambda t: t.rearrange("b (t p) e -> b p t e", p=P)
        x1b, ctxb, x2b = tiled(x1), tiled(context), tiled(x2)

        known = lambda b: isinstance(b.n, int)
        early = lambda b, n: known(b) and b.n < n
        within = lambda b: not known(b) or b.n < BATCH

        def max_unit(step, slot):
            starts = (0, 0, 4, 11, 17, 22, 28, UNITS, UNITS)
            n = starts[step] + slot - (2 if step == 1 else 0)
            return n if starts[step] <= n < starts[step + 1] else None

        def batches(eng, body):
            body(At(0, 0))
            body(At(0, 1))
            with eng.Fori(1, BATCH // 2 - 2) as k:
                body(At(k, 0))
                body(At(k, 1))
            for k in (BATCH // 2 - 2, BATCH // 2 - 1):
                body(At(k, 0))
                body(At(k, 1))

        with nc.Block() as block:
            @block.sync
            def _(sp):
                def load_x(b):
                    if not early(b, 2):
                        sp.wait_ge(norm_ready, b.n - 1)
                    sp.dma_start(x_in[b.par][:, :, :], x1b[b.n]).then_inc(x_loaded[b.par], 16)

                def load_context(b):
                    if not early(b, 2):
                        sp.wait_ge(vt_done, 2 * (b.n - 1))
                    sp.dma_start(c_in[b.par][:, :, :], ctxb[b.n]).then_inc(c_loaded[b.par], 16)

                def leave(b):
                    sp.wait_ge(split_ready, 4 * (b.n + 1))
                    for w, pair in enumerate((x16, c16)):
                        for z in range(2):
                            sp.dma_start(xc_scratch[b.n, w, z].rearrange("(t p) e -> p t e", p=P),
                                         pair[z][:, :, :]).then_inc(left, 16)

                def enter(b):
                    if early(b, 2):
                        sp.wait_ge(left, 64 * (b.n + 1))
                    else:
                        sp.wait_ge(score_done, UNITS * (b.n - 1))
                    st = stack[b.par]
                    src = [[xc_scratch[b.n, w, z].rearrange("(h d) e -> d h e", d=X_D) for z in range(2)] for w in range(2)]
                    for row, x_half, c_half in ((0, 0, 0), (1, 1, 0), (2, 0, 1)):
                        dst = st[X_D * row:X_D * row + X_D, :, :]
                        sp.dma_start(dst[:, 0:X_HEADS, :], src[0][x_half]).then_inc(stacked[b.par], 16)
                        sp.dma_start(dst[:, X_HEADS:SLOTS, :], src[1][c_half]).then_inc(stacked[b.par], 16)

                def place_max(b):
                    sp.wait_ge(max_cast, b.n + 1)
                    dst = stack[b.par][MAX_ROW:MAX_ROW + 1, 0:X_HEADS, :]
                    sp.dma_start(dst.rearrange("o h (q t) -> o (h q) t", t=P),
                                 max_row[:, :]).then_inc(max_placed[b.par], 16)

                def load_res(b):
                    if not early(b, 2):
                        sp.wait_ge(stored[b.par], 16 * b.half)
                    sp.dma_start(x_res[b.par][:, :, :], x1b[b.n]).then_inc(res_loaded[b.par], 16)

                def store(b):
                    sp.wait_ge(y_added, TT * (b.n + 1))
                    sp.dma_start(x2b[b.n], x_res[b.par][:, :, :]).then_inc(stored[b.par], 16)

                for n in range(2):
                    load_x(At(0, n))
                    load_context(At(0, n))
                    if n == 0:
                        sp.dma_start(gam[:, :], gamma.rearrange("(o n) -> o n", o=1).to_broadcast([P, 1]),
                                     allow_slow_non_contiguous=True).then_inc(gam_loaded, 16)
                leave(At(0, 0))
                enter(At(0, 0))
                load_x(At(1, 0))
                leave(At(0, 1))
                enter(At(0, 1))
                quantizer.load(sp, At(0, 0))
                place_max(At(0, 0))

                def body(b):
                    if within(b.plus(3)):
                        load_x(b.plus(3))
                    if within(b.plus(2)):
                        load_context(b.plus(2))
                    load_res(b)
                    if not early(b, 1):
                        quantizer.store(sp, b.plus(-1))
                        store(b.plus(-1))
                    if within(b.plus(1)):
                        quantizer.load(sp, b.plus(1))
                    if within(b.plus(2)):
                        leave(b.plus(2))
                    if within(b.plus(1)):
                        place_max(b.plus(1))
                    if within(b.plus(2)):
                        enter(b.plus(2))

                batches(sp, body)
                quantizer.store(sp, At(BATCH // 2 - 1, 1))
                sp.wait_ge(quantizer.stored, 16 * BATCH)
                store(At(BATCH // 2 - 1, 1))
                for i in range(2):
                    sp.wait_ge(stored[i], 16 * (BATCH // 2))

            @block.gpsimd
            def _(gp):
                chain = Chain(gp, m_chain, MOMENT_LINKS)

                def row_moments(b):
                    gp.wait_ge(stats_ready, TT * (b.n + 1))
                    chain.start(b.n)
                    moments(nc.gpsimd, chain.link, stats, mean[:, :], rstd[:, :], m_const, m_tmp)

                def low_parts(b, src, pair, hi):
                    gp.wait_ge(hi, b.n + 1)
                    for t in range(TT):
                        nc.gpsimd.tensor_tensor(pair[1][:, t, :], src[:, t, :], pair[0][:, t, :],
                                                ALU.subtract).then_inc(split_ready, 1)

                def add(b, t):
                    n = TT * b.n + t
                    gp.wait_ge(n_chain, N_LINKS * (n + 1))
                    gp.wait_ge(o_taken, n + 1)
                    if not (early(b, 1) and t == 0):
                        gp.wait_ge(y_added, n)
                    nc.gpsimd.tensor_tensor(o_norm[:, :], o_gam[:, :], s_inv[:, :], ALU.mult).then_inc(o_scaled, 1)
                    gp.wait_ge(o_scaled, n + 1)
                    if t == 0:
                        gp.wait_ge(res_loaded[b.par], 16 * (b.half + 1))
                    r = x_res[b.par][:, t, :]
                    nc.gpsimd.tensor_tensor(r, o_norm[:, :], r, ALU.add).then_inc(y_added, 1)

                identity_matrix(gp, ones, ident, ones_made, ident_ready)
                row_moments(At(0, 0))
                low_parts(At(0, 0), c_in[0], c16, c_hi)
                row_moments(At(0, 1))
                low_parts(At(0, 1), c_in[1], c16, c_hi)
                low_parts(At(0, 1), x_norm, x16, x_hi)

                def body(b):
                    ahead = b.plus(2)
                    if not early(b, 1):
                        add(b.plus(-1), 0)
                        quantizer.round(gp, b.plus(-1))
                    if within(ahead):
                        row_moments(ahead)
                        low_parts(ahead, c_in[b.par], c16, c_hi)
                    quantizer.divide(gp, b)
                    if not early(b, 1):
                        add(b.plus(-1), 1)
                    if within(ahead):
                        low_parts(ahead, x_norm, x16, x_hi)

                batches(gp, body)
                quantizer.round(gp, At(BATCH // 2 - 1, 1))
                for t in range(TT):
                    add(At(BATCH // 2 - 1, 1), t)

            @block.vector
            def _(v):
                def layernorm_stats(b):
                    v.wait_ge(x_loaded[b.par], 16 * (b.half + 1))
                    for t in range(TT):
                        nc.vector.bn_stats(stats[:, t, :], x_in[b.par][:, t, :]).then_inc(stats_ready, 1)

                def layernorm(b):
                    v.wait_ge(m_chain, MOMENT_LINKS * (b.n + 1))
                    if not early(b, 1):
                        v.wait_ge(split_ready, 4 * b.n)
                    for t in range(TT):
                        last = nc.vector.tensor_scalar(x_norm[:, t, :], x_in[b.par][:, t, :], mean[:, t:t + 1],
                                                       rstd[:, t:t + 1], ALU.subtract, ALU.mult)
                    last.then_inc(norm_ready, 1)

                def take_max(b, unit):
                    if unit is None or not within(b):
                        return
                    v.wait_ge(max_done, UNITS * b.n + unit + 1)
                    if unit == 0 and not early(b, 1):
                        v.wait_ge(max_t, b.n)
                    nc.vector.tensor_reduce(row_max[:, unit:unit + 1], m_ps[unit % BANKS][:, :],
                                            AX.X, ALU.max).then_inc(max_taken, 1)

                def normalize(b, t, part):
                    n = TT * b.n + t
                    if part == 0:
                        v.wait_ge(pv_done, n + 1)
                        nc.vector.transpose(s_t[:, :, :].rearrange("p a c -> p (a c)"), r_ps[:, :]).then_inc(n_chain, 1)
                    elif part == 1:
                        v.wait_ge(n_chain, N_LINKS * n + 1)
                        nc.vector.reciprocal(s_rec[:, :], s_t[:, :, 0]).then_inc(n_chain, 1)
                    else:
                        v.wait_ge(n_chain, N_LINKS * n + 2)
                        if not (early(b, 1) and t == 0):
                            v.wait_ge(o_scaled, n)
                        nc.vector.transpose(s_inv[:, :], spread(s_rec[:, :], 32)).then_inc(n_chain, 1)

                moment_constants(nc.vector, m_const, fixed_ready)
                layernorm_stats(At(0, 0))
                key_row = lambda st: nc.vector.memset(st[MAX_ROW:MAX_ROW + 1, X_HEADS:SLOTS, :], -1.0).then_inc(fixed_ready, 1)
                key_row(stack[0])
                layernorm(At(0, 0))
                v.wait_ge(x_hi, 1)
                for t in range(TT):
                    nc.vector.tensor_tensor(x16[1][:, t, :], x_norm[:, t, :], x16[0][:, t, :],
                                            ALU.subtract).then_inc(split_ready, 1)
                layernorm_stats(At(0, 1))
                key_row(stack[1])
                layernorm(At(0, 1))
                for unit in range(UNITS):
                    take_max(At(0, 0), unit)

                def body(b):
                    for h in range(X_HEADS):
                        for slot in range(SLOTS_OF_STEP):
                            if h in (0, 4) and slot < N_LINKS and not early(b, 1):
                                normalize(b.plus(-1), h // 4, slot)
                            take_max(b.plus(1), max_unit(h, slot))
                        if h == 0:
                            quantizer.scales(v, b)
                            if within(b.plus(2)):
                                layernorm_stats(b.plus(2))
                        if h == LAST:
                            quantizer.magic(v, b)
                        if h == 3 and within(b.plus(2)):
                            layernorm(b.plus(2))

                batches(v, body)
                for t in range(TT):
                    for part in range(N_LINKS):
                        normalize(At(BATCH // 2 - 1, 1), t, part)

            @block.scalar
            def _(act):
                def exponentials(b, h, kt):
                    unit = KT * h + kt
                    act.wait_ge(score_done, UNITS * b.n + unit + 1)
                    if h % HPT == 0 and kt == 0 and not early(b, 1):
                        act.wait_ge(pv_done, TT * (b.n - 1) + h // HPT + 1)
                    nc.scalar.activation(prob[h // HPT][h % HPT][:, kt, :], s_ps[unit % BANKS][:, :], ACT.Exp,
                                         scale=X_D ** -0.5).then_inc(prob_ready, 1)

                def take_o(b, t):
                    n = TT * b.n + t
                    act.wait_ge(pv_done, n + 1)
                    if not (early(b, 1) and t == 0):
                        act.wait_ge(o_scaled, n)
                    nc.scalar.activation(o_gam[:, :], o_ps[:, :], ACT.Copy, scale=gam[:, 0:1]).then_inc(o_taken, 1)

                def cast_max(b):
                    act.wait_ge(max_t, b.n + 1)
                    if not early(b, 1) and within(b.plus(1)):
                        act.wait_ge(left, 64 * (b.n + 2))
                    if not early(b, 1):
                        prev = b.plus(-1)
                        act.wait_ge(max_placed[prev.par], 16 * (prev.half + 1))
                    nc.scalar.activation(max_row[:, :], m_ps[0][0:X_HEADS * KT, 0:P], ACT.Copy).then_inc(max_cast, 1)

                def high_context(b):
                    if not early(b, 1):
                        act.wait_ge(left, 64 * b.n)
                    act.wait_ge(c_loaded[b.par], 16 * (b.half + 1))
                    nc.scalar.activation(c16[0][:, :, :], c_in[b.par][:, :, :], ACT.Copy).then_inc(c_hi, 1)

                def high_tokens(b):
                    act.wait_ge(norm_ready, b.n + 1)
                    nc.scalar.activation(x16[0][:, :, :], x_norm[:, :, :], ACT.Copy).then_inc(x_hi, 1)

                def keep_vt(b, i):
                    if i == 1 and not early(b, 2):
                        act.wait_ge(pv_done, TT * (b.n - 1))
                    act.wait_ge(vt_done, 2 * b.n + 2 - i)
                    nc.scalar.activation(v_t[b.par][:, 2 * i:2 * i + 2, :], m_ps[2 - i][:, :].rearrange("p (k s) -> p k s", s=SEQ),
                                         ACT.Copy).then_inc(vt_ready, 1)

                act.wait_ge(gam_loaded, 16)
                high_context(At(0, 0))
                high_tokens(At(0, 0))
                keep_vt(At(0, 0), 1)
                keep_vt(At(0, 0), 0)
                high_context(At(0, 1))
                high_tokens(At(0, 1))
                cast_max(At(0, 0))

                def body(b):
                    for h in range(X_HEADS):
                        if h in (0, 4) and not early(b, 1):
                            take_o(b.plus(-1), h // 4)
                        exponentials(b, h, 0)
                        exponentials(b, h, 1)
                        if h == LAST and within(b.plus(1)):
                            cast_max(b.plus(1))
                        exponentials(b, h, 2)
                        exponentials(b, h, 3)
                        if h == LAST and within(b.plus(1)):
                            keep_vt(b.plus(1), 1)
                        if h == 0 and not early(b, 1):
                            keep_vt(b, 0)
                        if h == 2 and within(b.plus(2)):
                            high_context(b.plus(2))
                        if h == 4 and within(b.plus(2)):
                            high_tokens(b.plus(2))

                batches(act, body)
                for t in range(TT):
                    take_o(At(BATCH // 2 - 1, 1), t)

            @block.tensor
            def _(pe):
                def transpose_context(b, i):
                    if i == 1:
                        pe.wait_ge(c_loaded[b.par], 16 * (b.half + 1))
                    if not early(b, 1):
                        pe.wait_ge(max_taken, UNITS * (b.n + 1))
                    for k in range(2):
                        for t in range(TT):
                            last = nc.tensor.transpose(m_ps[2 - i][:, SEQ * k + P * t:SEQ * k + P * t + P],
                                                       c_in[b.par][:, t, P * (2 * i + k):P * (2 * i + k) + P], ident[:, :])
                    last.then_inc(vt_done, 1)

                def max_scores(b, unit):
                    if unit is None or not within(b):
                        return
                    if unit == 0:
                        pe.wait_ge(stacked[b.par], 6 * 16 * (b.half + 1))
                        pe.wait_ge(vt_ready, 2 * (1 if early(b, 1) else b.n))
                    st, h, qt = stack[b.par], unit // KT, unit % KT
                    if unit >= BANKS:
                        pe.wait_ge(max_taken, UNITS * b.n + unit - BANKS + 1)
                    elif not early(b, 1):
                        pe.wait_ge(max_cast, b.n)
                    nc.tensor.matmul(m_ps[unit % BANKS][:, :], st[0:STACK, h, P * qt:P * qt + P],
                                     st[0:STACK, X_HEADS + h, :], start=True, stop=True).then_inc(max_done, 1)

                def transpose_max(b):
                    pe.wait_ge(max_taken, UNITS * (b.n + 1))
                    nc.tensor.transpose(m_ps[0][0:X_HEADS * KT, 0:P], row_max[:, :], ident[:, :]).then_inc(max_t, 1)

                def scores(b, h, kt):
                    st, unit = stack[b.par], KT * h + kt
                    if unit == 0:
                        pe.wait_ge(max_placed[b.par], 16 * (b.half + 1))
                    if unit >= BANKS:
                        pe.wait_ge(prob_ready, UNITS * b.n + unit - BANKS + 1)
                    elif not early(b, 1):
                        pe.wait_ge(prob_ready, UNITS * b.n + LAST_USE[unit] + 1)
                    nc.tensor.matmul(s_ps[unit % BANKS][:, :], st[0:MAX_ROW + 1, X_HEADS + h, P * kt:P * kt + P],
                                     st[0:MAX_ROW + 1, h, :], start=True, stop=True).then_inc(score_done, 1)

                def weighted_values(b, t, kt, summed):
                    n = TT * b.n + t
                    if kt == 0 and not summed:
                        pe.wait_ge(prob_ready, UNITS * b.n + KT * HPT * (t + 1))
                        pe.wait_ge(vt_ready, 2 * (b.n + 1))
                        if not (early(b, 1) and t == 0):
                            pe.wait_ge(o_taken, n)
                    if kt == 0 and summed and not (early(b, 1) and t == 0):
                        pe.wait_ge(n_chain, N_LINKS * (n - 1) + 1)
                    for j in range(HPT):
                        row = X_D * (HPT * t + j)
                        lhs = ones[:, 0:X_D] if summed else v_t[b.par][:, kt, row:row + X_D]
                        last = nc.tensor.matmul((r_ps if summed else o_ps)[X_D * j:X_D * j + X_D, :], lhs,
                                                prob[t][j][:, kt, :], start=kt == 0, stop=kt == KT - 1)
                    if kt == KT - 1 and summed:
                        last.then_inc(pv_done, 1)

                pe.wait_ge(ident_ready, 1)
                transpose_context(At(0, 0), 1)
                transpose_context(At(0, 0), 0)
                for unit in range(UNITS):
                    max_scores(At(0, 0), unit)
                transpose_max(At(0, 0))
                pe.wait_ge(fixed_ready, len(MOMENT_CONSTANTS) + 2)

                def body(b):
                    for h in range(X_HEADS):
                        step = lambda slot: max_scores(b.plus(1), max_unit(h, slot))
                        owner, t = (b.plus(-1), 1) if h < HPT else (b, 0)
                        weighted = not early(owner, 0)
                        scores(b, h, 0)
                        if h == LAST and within(b.plus(1)):
                            transpose_max(b.plus(1))
                        step(0)
                        scores(b, h, 1)
                        step(1)
                        if h == 0 and not early(b, 1):
                            transpose_context(b, 0)
                        if weighted:
                            weighted_values(owner, t, h % HPT, False)
                        scores(b, h, 2)
                        step(2)
                        if h == LAST and within(b.plus(1)):
                            transpose_context(b.plus(1), 1)
                        scores(b, h, 3)
                        step(3)
                        if weighted:
                            weighted_values(owner, t, h % HPT, True)
                        step(4)
                        step(5)
                        step(6)

                batches(pe, body)
                for kt in range(KT):
                    for summed in (False, True):
                        weighted_values(At(BATCH // 2 - 1, 1), 1, kt, summed)
def decoder_block(nc, x, context, wq, bq, wk, bk, wv, bv, wo, bo, gamma, gate_w, up_w, down_w, out):
    scratch = lambda name, shape, dt=F32: nc.dram_tensor(name, shape, dt, kind="Internal").ap()
    x1, x2 = scratch("x1", (BATCH, SEQ, E)), scratch("x2", (BATCH, SEQ, E))
    qk = scratch("qk_halves", (BATCH, 2, E + KV_HEADS * D, SEQ), F16)
    xc = scratch("xc_halves", (BATCH, 2, 2, SEQ, E), F16)
    weights = scratch("weights", (3 * FF // P, P, E))
    gate_up = 2 * FF // P
    self_attention(nc, x, wq, bq, wk, bk, wv, bv, wo, bo, qk, x1, gate_w, up_w, weights[0:gate_up])
    cross_attention(nc, x1, context, gamma, xc, x2, down_w, weights[gate_up:])
    rows = lambda t: t.rearrange("b s e -> (b s) e")
    feed_forward(nc, rows(x2), weights, rows(out))


_INS = ["x", "ctx_2048", "L0_attn_Wq", "L0_attn_bq", "L0_attn_Wk", "L0_attn_bk", "L0_attn_Wv", "L0_attn_bv",
        "L0_attn_Wo", "L0_attn_bo", "L0_xattn_gamma", "L0_ffn_gate_w", "L0_ffn_up_w", "L0_ffn_down_w"]


def kernel(**inputs):
    import numpy as _np
    import concourse.bacc as _bacc
    from concourse.bass_utils import run_bass_kernel_spmd as _run

    nc = _bacc.Bacc("TRN2", target_bir_lowering=False, num_devices=1)
    arrays, args = {}, []
    for name in _INS:
        a = _np.ascontiguousarray(inputs[name])
        if a.ndim == 0:
            a = a.reshape(1)
        arrays[f"in_{name}_dram"] = a
        args.append(nc.dram_tensor(f"in_{name}_dram", a.shape, mybir.dt.from_np(a.dtype), kind="ExternalInput").ap())
    args.append(nc.dram_tensor("out_0_dram", (BATCH, SEQ, E), F32, kind="ExternalOutput").ap())
    decoder_block(nc, *args)
    r = _run(nc, [arrays], core_ids=[0])
    return r.results[0]["out_0_dram"]
```
